# Optimizing a Trainium2 kernel written in Bass

```python
import numpy as np
import jax
import jax.numpy as jnp

def _softmax(x, axis=-1):
    return jax.nn.softmax(x, axis=axis)

def _gelu(x):
    return jax.nn.gelu(x, approximate=True)

def _silu(x):
    return jax.nn.silu(x)

def _sigmoid(x):
    return jax.nn.sigmoid(x)

def _layernorm(x, axis=-1, eps=1e-05):
    m = jnp.mean(x, axis=axis, keepdims=True)
    v = jnp.var(x, axis=axis, keepdims=True)
    return (x - m) / jnp.sqrt(v + eps)

def _scatter_add(tgt, idx, src, axis=0):
    return tgt.at[idx].add(src)

def _segment_sum(src, seg, n):
    return jax.ops.segment_sum(src, seg, n)
kernel_name = 'mk_gnn_ffn_d1_gnn_r8_eab8f3'

def setup_inputs(seed: int=0):
    np.random.seed(seed)
    _w = jnp.asarray

    def _rec_inputs():
        import jax
        import jax.numpy as jnp
        _gk = jax.random.key(seed)
        x = -0.0003713 + 1 * jax.random.normal(jax.random.fold_in(_gk, 1), (12500, 256), jnp.float32)
        _s = jax.random.randint(jax.random.fold_in(_gk, 2), (100000,), 0, 12500, jnp.int32)
        _d = jax.random.randint(jax.random.fold_in(_gk, 3), (100000,), 0, 12500, jnp.int32)
        _loop = jnp.arange(12500, dtype=jnp.int32)
        src = jnp.concatenate([_s, _d, _loop])
        dst = jnp.concatenate([_d, _s, _loop])
        _o = jnp.argsort(dst, stable=True)
        src = src[_o]
        dst = dst[_o]
        return (x, src, dst)
    x, src, dst = _rec_inputs()

    def _L0_gnn_setup():
        import jax, jax.numpy as jnp
        import numpy as np
        N, E = (6250, 100000)
        H, C_IN, C_HID, C_OUT = (4, 256, 64, 64)
        NEG_SLOPE = 0.2

        def leaky_relu(x, s=NEG_SLOPE):
            return jnp.where(x >= 0, x, s * x)

        def gat_conv(x, src, dst, W, att_src, att_dst, bias, n_nodes):
            Hh, Cc = (att_src.shape[1], att_src.shape[2])
            h = (x @ W).reshape(n_nodes, Hh, Cc)
            a_src = (h * att_src).sum(-1)
            a_dst = (h * att_dst).sum(-1)
            alpha = leaky_relu(a_src[src] + a_dst[dst])
            m = jax.ops.segment_max(alpha, dst, num_segments=n_nodes)
            e = jnp.exp(alpha - m[dst])
            denom = jax.ops.segment_sum(e, dst, num_segments=n_nodes)
            w = e / jnp.clip(denom, 1e-16)[dst]
            out = jax.ops.segment_sum(w[:, :, None] * h[src], dst, num_segments=n_nodes)
            return out.reshape(n_nodes, Hh * Cc) + bias
        key = jax.random.key(seed)
        ks = jax.random.split(key, 10)
        glorot = lambda k, shp: jax.random.normal(k, shp, jnp.float32) * np.sqrt(2.0 / (shp[0] + shp[-1]))
        return {'x': jax.random.normal(ks[0], (N, C_IN), jnp.float32), 'edge_index': jax.random.randint(ks[1], (2, E), 0, N, jnp.int32), 'W1': glorot(ks[2], (C_IN, H * C_HID)), 'att_src1': glorot(ks[3], (1, H, C_HID)), 'att_dst1': glorot(ks[4], (1, H, C_HID)), 'b1': jnp.zeros((H * C_HID,), jnp.float32), 'W2': glorot(ks[5], (H * C_HID, H * C_OUT)), 'att_src2': glorot(ks[6], (1, H, C_OUT)), 'att_dst2': glorot(ks[7], (1, H, C_OUT)), 'b2': jnp.zeros((H * C_OUT,), jnp.float32)}
    _L0_gnn_all = _L0_gnn_setup()
    _L0_gnn_in = {k: v for k, v in _L0_gnn_all.items() if k in ('W1', 'att_src1', 'att_dst1', 'b1', 'W2', 'att_src2', 'att_dst2', 'b2')}
    del _L0_gnn_all

    def _L0_ffn_setup():
        import math
        import jax, jax.numpy as jnp
        import numpy as np
        CAPACITY_FACTOR = 1.25
        TOP_K = 2
        LN_EPS = 1e-05

        def _layer_norm(x, gamma, beta):
            mu = jnp.mean(x, axis=-1, keepdims=True)
            var = jnp.var(x, axis=-1, keepdims=True)
            return (x - mu) * jax.lax.rsqrt(var + LN_EPS) * gamma + beta
        key = jax.random.key(seed)
        ks = jax.random.split(key, 4)
        B, S, D, F, E = (8, 512, 256, 512, 8)
        x = jax.random.normal(ks[0], (B, S, D), dtype=jnp.float32)
        Wr = jax.random.normal(ks[1], (D, E), dtype=jnp.float32) / np.sqrt(D)
        br = jnp.zeros((E,), jnp.float32)
        W1 = jax.random.normal(ks[2], (E, D, F), dtype=jnp.float32) / np.sqrt(D)
        b1 = jnp.zeros((E, F), jnp.float32)
        W2 = jax.random.normal(ks[3], (E, F, D), dtype=jnp.float32) / np.sqrt(F)
        b2 = jnp.zeros((E, D), jnp.float32)
        gamma = jnp.ones((D,), jnp.float32)
        beta = jnp.zeros((D,), jnp.float32)
        return {'x': x, 'Wr': Wr, 'br': br, 'W1': W1, 'b1': b1, 'W2': W2, 'b2': b2, 'gamma': gamma, 'beta': beta}
    _L0_ffn_all = _L0_ffn_setup()
    _L0_ffn_in = {k: v for k, v in _L0_ffn_all.items() if k in ('Wr', 'br', 'W1', 'b1', 'W2', 'b2', 'gamma', 'beta')}
    del _L0_ffn_all
    return {'x': x, 'src': src, 'dst': dst, 'L0_gnn_W1': _L0_gnn_in['W1'], 'L0_gnn_att_src1': _L0_gnn_in['att_src1'], 'L0_gnn_att_dst1': _L0_gnn_in['att_dst1'], 'L0_gnn_b1': _L0_gnn_in['b1'], 'L0_gnn_W2': _L0_gnn_in['W2'], 'L0_gnn_att_src2': _L0_gnn_in['att_src2'], 'L0_gnn_att_dst2': _L0_gnn_in['att_dst2'], 'L0_gnn_b2': _L0_gnn_in['b2'], 'L0_ffn_Wr': _L0_ffn_in['Wr'], 'L0_ffn_br': _L0_ffn_in['br'], 'L0_ffn_W1': _L0_ffn_in['W1'], 'L0_ffn_b1': _L0_ffn_in['b1'], 'L0_ffn_W2': _L0_ffn_in['W2'], 'L0_ffn_b2': _L0_ffn_in['b2'], 'L0_ffn_gamma': _L0_ffn_in['gamma'], 'L0_ffn_beta': _L0_ffn_in['beta']}

def reference(x, src, dst, L0_gnn_W1, L0_gnn_att_src1, L0_gnn_att_dst1, L0_gnn_b1, L0_gnn_W2, L0_gnn_att_src2, L0_gnn_att_dst2, L0_gnn_b2, L0_ffn_Wr, L0_ffn_br, L0_ffn_W1, L0_ffn_b1, L0_ffn_W2, L0_ffn_b2, L0_ffn_gamma, L0_ffn_beta):
    import jax
    import jax.numpy as jnp

    def _L0_gnn_ref(x, edge_index, W1, att_src1, att_dst1, b1, W2, att_src2, att_dst2, b2):
        import jax, jax.numpy as jnp
        import numpy as np
        N, E = (6250, 100000)
        H, C_IN, C_HID, C_OUT = (4, 256, 64, 64)
        NEG_SLOPE = 0.2

        def leaky_relu(x, s=NEG_SLOPE):
            return jnp.where(x >= 0, x, s * x)

        def gat_conv(x, src, dst, W, att_src, att_dst, bias, n_nodes):
            Hh, Cc = (att_src.shape[1], att_src.shape[2])
            h = (x @ W).reshape(n_nodes, Hh, Cc)
            a_src = (h * att_src).sum(-1)
            a_dst = (h * att_dst).sum(-1)
            alpha = leaky_relu(a_src[src] + a_dst[dst])
            m = jax.ops.segment_max(alpha, dst, num_segments=n_nodes)
            e = jnp.exp(alpha - m[dst])
            denom = jax.ops.segment_sum(e, dst, num_segments=n_nodes)
            w = e / jnp.clip(denom, 1e-16)[dst]
            out = jax.ops.segment_sum(w[:, :, None] * h[src], dst, num_segments=n_nodes)
            return out.reshape(n_nodes, Hh * Cc) + bias
        n = x.shape[0]
        loops = jnp.arange(n, dtype=edge_index.dtype)
        src = jnp.concatenate([edge_index[0], loops])
        dst = jnp.concatenate([edge_index[1], loops])
        h1 = gat_conv(x, src, dst, W1, att_src1, att_dst1, b1, n)
        h1 = jax.nn.relu(h1)
        out = gat_conv(h1, src, dst, W2, att_src2, att_dst2, b2, n)
        return out

    def _L0_ffn_ref(x, Wr, br, W1, b1, W2, b2, gamma, beta):
        import math
        import jax, jax.numpy as jnp
        import numpy as np
        CAPACITY_FACTOR = 1.25
        TOP_K = 2
        LN_EPS = 1e-05

        def _layer_norm(x, gamma, beta):
            mu = jnp.mean(x, axis=-1, keepdims=True)
            var = jnp.var(x, axis=-1, keepdims=True)
            return (x - mu) * jax.lax.rsqrt(var + LN_EPS) * gamma + beta
        B, S, D = x.shape
        E = Wr.shape[1]
        N = B * S
        K = TOP_K
        logits = jnp.mean(x, axis=1) @ Wr + br
        routing_weights = jax.nn.softmax(logits, axis=-1)
        capacity = float(math.ceil(N * CAPACITY_FACTOR / E))
        expected_loads = routing_weights.sum(axis=0) * (N / B)
        scale = jnp.where(expected_loads > capacity, capacity / expected_loads, 1.0)
        routing_weights = jax.nn.softmax(routing_weights * scale, axis=-1)
        rw_tok = jnp.broadcast_to(routing_weights[:, None, :], (B, S, E)).reshape(N, E)
        top_w, top_i = jax.lax.top_k(rw_tok, K)
        top_w = jax.nn.softmax(top_w, axis=-1)
        xf = x.reshape(N, D)
        h = jax.nn.gelu(jnp.einsum('nd,edf->enf', xf, W1) + b1[:, None, :], approximate=False)
        y = jnp.einsum('enf,efd->end', h, W2) + b2[:, None, :]
        w_dense = jnp.zeros((N, E), x.dtype).at[jnp.arange(N)[:, None], top_i].add(top_w)
        out = jnp.einsum('ne,end->nd', w_dense, y).reshape(B, S, D)
        out = _layer_norm(out + x, gamma, beta)
        return out
    edge_index = jnp.stack([src, dst])
    x = x + _L0_gnn_ref(_layernorm(x, axis=-1), edge_index, L0_gnn_W1, L0_gnn_att_src1, L0_gnn_att_dst1, L0_gnn_b1, L0_gnn_W2, L0_gnn_att_src2, L0_gnn_att_dst2, L0_gnn_b2)
    x = x + _L0_ffn_ref(_layernorm(x, axis=-1)[None], L0_ffn_Wr, L0_ffn_br, L0_ffn_W1, L0_ffn_b1, L0_ffn_W2, L0_ffn_b2, L0_ffn_gamma, L0_ffn_beta)[0]
    return x

_drawn_inputs = setup_inputs


def setup_inputs(seed=0):
    import zlib

    import numpy as np

    out = dict(_drawn_inputs(seed))
    spreads = {'L0_gnn_b1': (0.0, 0.1),
     'L0_gnn_b2': (0.0, 0.1),
     'L0_ffn_br': (0.0, 0.1),
     'L0_ffn_b1': (0.0, 0.362),
     'L0_ffn_b2': (0.0, 0.1),
     'L0_ffn_gamma': (1.0, 0.2),
     'L0_ffn_beta': (0.0, 0.1)}
    factors = {'L0_gnn_att_dst1': 3.561, 'L0_gnn_att_src2': 3.858, 'L0_gnn_att_dst2': 8.0}
    for name, (base, spread) in spreads.items():
        noise = np.random.default_rng([zlib.crc32(name.encode()), seed]).standard_normal(out[name].shape)
        drawn = base * np.exp(spread * noise) if base else spread * noise
        out[name] = jnp.asarray(drawn.astype(out[name].dtype))
    for name, factor in factors.items():
        out[name] = (out[name] * factor).astype(out[name].dtype)
    return out
```

```python
from contextlib import ExitStack

import concourse.bass as bass
from concourse import mybir

ALU = mybir.AluOpType
ACT = mybir.ActivationFunctionType
AX = mybir.AxisListType
F32 = mybir.dt.float32
BF16 = mybir.dt.bfloat16
I32 = mybir.dt.int32

P = 128
NBLK = 125
T = 18
CAP = P * T
HEADS = 4
STG = 4
GRP = 4
BIG = 1.0e30
SLOPE = 0.2
LN_EPS = 1e-5
RSQRT_MAGIC = float(0x5F3759DF)
TOP_K = 2


class Chain:

    def __init__(self, eng, sem):
        self.eng, self.sem = eng, sem
        self.base, self.n, self.per = 0, 0, {}

    def link(self, ins):
        self.n += 1
        ins.then_inc(self.sem, 1)
        self.eng.wait_ge(self.sem, self.base + self.n)

    def steps(self, total, first, last, body):
        pairs = (total - first - last) // 2
        assert first % 2 == 0 and first >= 2 and pairs * 2 == total - first - last
        for b in range(first):
            before = self.n
            body(b, b // 2, b % 2)
            per = self.n - before
        start = self.n
        if pairs:
            with self.eng.Fori(0, pairs) as i:
                for u in range(2):
                    self.base, self.n = i * (2 * per) + (start + u * per), 0
                    body(i * 2 + (first + u), i + first // 2, u)
                    assert self.n == per, (self.n, per)
        self.base, self.n = 0, start + per * 2 * pairs
        for b in range(total - last, total):
            body(b, b // 2, b % 2)


def build(nc, x, src, dst, W1, as1, ad1, b1, W2, as2, ad2, b2, Wr, br, fW1, fb1, fW2, fb2, gamma, beta, out):
    N, D = x.shape
    E, = src.shape
    C = D // HEADS
    KT = D // P
    NX, F = Wr.shape[1], fW1.shape[2]
    FT = F // P
    NB = N // NBLK
    NG = NB // GRP
    HW = D + HEADS
    HWX = D + 2 * HEADS
    GW = D + 2 * HEADS + 1
    ER = 125
    EC = E // ER
    SAMP = 68 if EC % 68 == 0 else EC
    NS = EC // SAMP
    CHUNK = GRP * NBLK
    NGROUPS_ST = (T + STG - 1) // STG
    capacity = float(-(-int(N * 1.25) // NX)) if (N * 1.25) == int(N * 1.25) else float(int(N * 1.25 / NX) + 1)
    import math
    capacity = float(math.ceil(N * 1.25 / NX))
    assert KT == 2 and NB * NBLK == N and NG * GRP == NB and EC * ER == E and E >= CAP

    def dram(name, shape, dt=F32):
        return nc.dram_tensor(name, shape, dt).ap()

    dpad = dram("dpad", (E + 2,))
    samples_d = dram("samples_d", (ER * NS,))
    tables = [dram("table1", (N, HW)), dram("table2", (N, HW))]
    x1_d = dram("x1_d", (N, D))
    xn_d = dram("xn_d", (N, D))
    xT_d = dram("xT_d", (KT, P, N))

    with ExitStack() as ctx:
        def sb(name, shape, dt=F32):
            return ctx.enter_context(nc.sbuf_tensor(name, shape, dt))

        def sem(name):
            return ctx.enter_context(nc.semaphore(name))

        bank = {n: ctx.enter_context(nc.psum_tensor(n, [P, 512], F32)) for n in
                ("p_acc", "p_st0", "p_st1", "p_expand", "p_rows", "p_xt", "p_h", "p_small")}
        p_acc, p_expand, p_rows, p_xt, p_h, p_small = (bank[n] for n in ("p_acc", "p_expand", "p_rows", "p_xt", "p_h", "p_small"))
        p_st = [bank["p_st0"], bank["p_st1"]]

        ident = sb("ident", [P, P])
        zeros = sb("zeros", [P, P])
        ones = sb("ones", [1, P])
        node_iota = sb("node_iota", [P, NBLK])
        block_base = sb("block_base", [P, NB])
        bias = [sb("bias1", [NBLK, D]), sb("bias2", [NBLK, D])]
        gamma_b, beta_b = sb("gamma_b", [NBLK, D]), sb("beta_b", [NBLK, D])

        wext = [sb("wext1", [P, KT, HWX]), sb("wext2", [P, KT, HWX])]
        wT = sb("wT", [P, KT, D])
        att = sb("att", [P, 4, KT])
        attm = sb("attm", [P, 2, KT, 2 * HEADS])

        hid = [sb(f"hid{q}", [P, TOP_K * FT, CHUNK]) for q in range(2)]
        G = [sb(f"G{q}", [P, T, GW]) for q in range(2)]
        dst_i = hid[0][:].rearrange("p n c -> p (n c)")[0:ER, 0:EC].bitcast(I32)
        dst_f = hid[1][:].rearrange("p n c -> p (n c)")[0:ER, 0:EC]
        samp = sb("samp", [ER, NS])
        sentinel = sb("sentinel", [1, 2])
        samp_b = G[0][:].rearrange("p t n -> p (t n)")[0:NB, 0:ER * NS]
        samp_lt = G[1][:].rearrange("p t n -> p (t n)")[0:NB, 0:ER * NS]
        first_node = sb("first_node", [NB, 1])
        st_f = sb("st_f", [NB, 8])
        st_i = sb("st_i", [NB, 1], I32)
        swin = sb("swin", [NB, SAMP], I32)
        swin_lt = sb("swin_lt", [NB, SAMP])
        starts_i = sb("starts_i", [1, NB], I32)

        xg = [sb(f"xg{q}", [NBLK, GRP, D]) for q in range(2)]
        xng = [sb(f"xng{q}", [NBLK, GRP, D]) for q in range(2)]
        stats = sb("stats", [NBLK, GRP, 6])
        mv = sb("mv", [NBLK, GRP, 2])
        rs = sb("rs", [NBLK, 6, GRP])
        rs_i = sb("rs_i", [NBLK, 2, GRP], I32)
        xT = [sb(f"xT{q}", [P, KT, NBLK]) for q in range(2)]
        hout = [sb(f"hout{q}", [NBLK, GRP, HWX]) for q in range(2)]
        node = [sb("node1", [NBLK, NB, 2 * HEADS]), sb("node2", [NBLK, NB, 2 * HEADS])]
        node_parts = sb("node_parts", [NBLK, NB, 3, 2 * HEADS], BF16)
        node_rest = sb("node_rest", [NBLK, NB, 2 * HEADS])

        src_w = [sb(f"src_w{q}", [P, T], I32) for q in range(2)]
        dst_w = [sb(f"dst_w{q}", [P, T + 2]) for q in range(2)]
        hself = [sb(f"hself{q}", [NBLK, HW]) for q in range(2)]
        xres = [sb(f"xres{q}", [NBLK, D]) for q in range(2)]
        onehot = [sb(f"onehot{q}", [P, T, NBLK]) for q in range(2)]
        onehotT = sb("onehotT", [NBLK, T, P], BF16)
        node_q = [sb(f"node_q{q}", [NBLK, 2 * HEADS]) for q in range(2)]
        parts_q = [sb(f"parts_q{q}", [NBLK, 3 * 2 * HEADS], BF16) for q in range(2)]
        dloc = sb("dloc", [P, T])
        link_w = sb("link_w", [P, T + 1])
        pen = sb("pen", [P, T + 1])
        run_end = [sb(f"run_end{q}", [P, T]) for q in range(2)]
        penF = [sb(f"penF{q}", [P, HEADS, T + 1]) for q in range(2)]
        penB = [sb(f"penB{q}", [P, HEADS, T + 1]) for q in range(2)]
        whole = [sb(f"whole{q}", [P, 2, HEADS]) for q in range(2)]
        vF = sb("vF", [P, HEADS, T + 1])
        vB = sb("vB", [P, HEADS, T + 1])
        rF = sb("rF", [P, HEADS, T + 1])
        rB = sb("rB", [P, HEADS, T + 1])
        row_pen = sb("row_pen", [HEADS, 2, P])
        carF = sb("carF", [HEADS, P + 1])
        carB = sb("carB", [HEADS, P + 1])
        expn = [sb(f"expn{q}", [P, T, 2 * HEADS]) for q in range(2)]
        runmax = sb("runmax", [P, T, HEADS])
        alpha = sb("alpha", [P, T, HEADS])
        logit = sb("logit", [P, T, HEADS])
        self_s = sb("self_s", [NBLK, 8, HEADS])
        hs = sb("hs", [NBLK, D])
        num = sb("num", [NBLK, D])
        h1 = sb("h1", [NBLK, D])
        hT = [sb(f"hT{q}", [P, KT, NBLK]) for q in range(2)]
        x1 = [sb(f"x1{q}", [NBLK, D]) for q in range(2)]
        xn2 = [sb(f"xn2{q}", [NBLK, D]) for q in range(2)]
        colsum = sb("colsum", [P, KT, NB])

        mean = sb("mean", [P, KT])
        wr_sb = sb("wr_sb", [P, KT, NX])
        rt = sb("rt", [1, 16, NX])
        sel_i = sb("sel_i", [1, TOP_K], I32)
        wsel = sb("wsel", [1, TOP_K])
        wsel_b = sb("wsel_b", [P, TOP_K])
        eW1 = sb("eW1", [P, TOP_K, KT, F])
        eb1 = sb("eb1", [P, TOP_K, FT])
        eW2 = sb("eW2", [P, TOP_K, FT, D])
        eb2 = sb("eb2", [1, TOP_K, D])
        eb2s = sb("eb2s", [1, D])
        fxT = [sb(f"fxT{q}", [P, KT, CHUNK]) for q in range(2)]
        fx1 = [sb(f"fx1{q}", [NBLK, GRP, D]) for q in range(2)]

        wait_here = sem("wait_here")
        dve_s, act_s = sem("dve_chain"), sem("act_chain")
        s_const, s_in, s_in2, s_wT, s_wTc, s_att, s_watt, s_wext = (sem(n) for n in (
            "s_const", "s_in", "s_in2", "s_wT", "s_wTc", "s_att", "s_watt", "s_wext"))
        s_dst, s_dstf, s_pad, s_sampd, s_sampb, s_idx, s_swin, s_st, s_stT, s_starts = (sem(n) for n in (
            "s_dst", "s_dstf", "s_pad", "s_sampd", "s_sampb", "s_idx", "s_swin", "s_st", "s_stT", "s_starts"))
        x_ok = [sem(f"x_ok{q}") for q in range(2)]
        x_norm, xt_done, xt_copied, h_done, h_copied = (sem(n) for n in ("x_norm", "xt_done", "xt_copied", "h_done", "h_copied"))
        tab_st = [sem(f"tab_st{q}") for q in range(2)]
        L = []
        for l in range(2):
            d = {n: sem(f"{n}_l{l}") for n in (
                "parts", "onehot_ok", "st_done", "st_copied", "expand_done", "expand_read", "whole_ok", "ends_ok", "rows_done",
                "carry_ok", "back_done", "logit_ok", "exp_ok", "prod_ok", "main_done", "acc_read", "sarg_ok", "sexp_ok",
                "feat_ok", "ft_done", "ft_copied", "hh_done", "hh_copied", "epi_done")}
            for n in ("src_ok", "dst_ok", "self_ok", "xres_ok", "gathered", "stored", "stored2"):
                d[n] = [sem(f"{n}_l{l}_{q}") for q in range(2)]
            L.append(d)
        r_mean, r_logit, r_exp, r_sel, r_w, r_wb, r_load, r_ready, r_in, r_exp2, r_exp3, r_arg, r_arg2, r_arg3 = (sem(n) for n in (
            "r_mean", "r_logit", "r_exp", "r_sel", "r_w", "r_wb", "r_load", "r_ready", "r_in", "r_exp2", "r_exp3", "r_arg", "r_arg2", "r_arg3"))
        f_ok = [sem(f"f_ok{q}") for q in range(2)]
        f_st = [sem(f"f_st{q}") for q in range(2)]
        f_hid, f_gelu, f_out, f_read, f_done = (sem(n) for n in ("f_hid", "f_gelu", "f_out", "f_read", "f_done"))

        xrows = x.rearrange("(b p) d -> p b d", p=NBLK)
        outrows = out.rearrange("(b p) d -> p b d", p=NBLK)
        x1rows = x1_d.rearrange("(b p) d -> p b d", p=NBLK)
        xnrows = xn_d.rearrange("(b p) d -> p b d", p=NBLK)
        tabrows = [t.rearrange("(b p) d -> p b d", p=NBLK) for t in tables]
        SETUP_LOADS = 16 * (2 + 4 + 4 + 2)

        def rsqrt(ch, eps_var, n, r, ri):
            v, y, t = r[:, 1, 0:n], r[:, 0, 0:n], r[:, 2, 0:n]
            vec = nc.vector
            ch.link(vec.tensor_scalar(v, eps_var, LN_EPS, None, ALU.add))
            ch.link(vec.tensor_scalar(ri[:, 0, 0:n], v.bitcast(I32), 1, None, ALU.logical_shift_right))
            ch.link(vec.tensor_scalar(y.bitcast(I32), ri[:, 0, 0:n], -1.0, RSQRT_MAGIC, ALU.mult, ALU.add))
            for _ in range(3):
                ch.link(vec.tensor_tensor(t, y, y, ALU.mult))
                ch.link(vec.tensor_tensor(t, t, v, ALU.mult))
                ch.link(vec.tensor_scalar(t, t, -0.5, 1.5, ALU.mult, ALU.add))
                ch.link(vec.tensor_tensor(y, y, t, ALU.mult))

        block = ctx.enter_context(nc.Block())

        @block.sync
        def _(sp):
            ch = Chain(sp, None)
            with nc.allow_non_contiguous_dma(reason="attention vectors and samples, one element a row"):
                sp.dma_start(dst_i, dst.rearrange("(p k) -> p k", p=ER)).then_inc(s_dst, 16)
                sp.dma_start(wext[0][:, :, 0:D], W1.rearrange("(t p) n -> p t n", p=P)).then_inc(s_in, 16)
                sp.dma_start(wext[1][:, :, 0:D], W2.rearrange("(t p) n -> p t n", p=P)).then_inc(s_in, 16)
                for i, a in enumerate((as1, ad1, as2, ad2)):
                    sp.dma_start(att[:, i, :], a.rearrange("o (t h) c -> (o h c) t", t=KT)).then_inc(s_in, 16)
                for dst_t, v in ((bias[0], b1), (bias[1], b2), (gamma_b, gamma), (beta_b, beta)):
                    sp.dma_start(dst_t[:], v.partition_broadcast(NBLK)).then_inc(s_in, 16)
                sp.dma_start(wr_sb[:], Wr.rearrange("(t p) n -> p t n", p=P)).then_inc(s_in, 16)
                sp.dma_start(rt[:, 0, :], br.rearrange("(a n) -> a n", a=1)).then_inc(s_in, 16)
                for g in range(2):
                    sp.dma_start(xg[g][:], xrows[:, g * GRP:(g + 1) * GRP, :]).then_inc(x_ok[g], 16)
                sp.wait_ge(s_dstf, 1)
                sp.dma_start(dpad[bass.ds(1, E)].rearrange("(p k) -> p k", p=ER), dst_f).then_inc(s_pad, 16)
                sp.dma_start(dpad[0:1].rearrange("(a n) -> a n", a=1), sentinel[:, 0:1]).then_inc(s_pad, 16)
                sp.dma_start(dpad[bass.ds(E + 1, 1)].rearrange("(a n) -> a n", a=1), sentinel[:, 1:2]).then_inc(s_pad, 16)
                sp.dma_start(samples_d.rearrange("(p k) -> p k", p=ER), samp[:]).then_inc(s_sampd, 16)
                sp.wait_ge(s_sampd, 16)
                sp.dma_start(samp_b, samples_d.partition_broadcast(NB)).then_inc(s_sampb, 16)

            def table_group(g, half, q):
                sp.wait_ge(h_copied, g * GRP + GRP)
                sp.dma_start(tabrows[0][:, bass.ds(g * GRP, GRP), :], hout[q][:, :, 0:HW]).then_inc(tab_st[q], 16)
                if not isinstance(g, int) or g < NG - 2:
                    sp.wait_ge(x_norm, g + 1)
                    sp.dma_start(xg[q][:], xrows[:, bass.ds(g * GRP + 2 * GRP, GRP), :]).then_inc(x_ok[q], 16)
            ch.steps(NG, 2, 3, table_group)
            sp.wait_ge(tab_st[0], 16 * ((NG + 1) // 2))
            sp.wait_ge(tab_st[1], 16 * (NG // 2))
            sp.wait_ge(s_starts, 1)
            sp.wait_ge(s_pad, 48)

            for l in range(2):
                s = L[l]

                def load_edges(b, q, s=s):
                    at = sp.value_load(starts_i[0:1, bass.ds(b, 1)], min_val=0, max_val=E - CAP)
                    sp.dma_start(src_w[q][:], src[bass.ds(at, CAP)].rearrange("(p k) -> p k", p=P)).then_inc(s["src_ok"][q], 16)
                    window = dpad[bass.ds(at, CAP)]
                    sp.dma_start(dst_w[q][:], bass.AP(window.tensor, window.offset, [[T, P], [1, T + 2]])).then_inc(s["dst_ok"][q], 16)

                def load_nodes(b, q, s=s, l=l):
                    sp.dma_start(hself[q][:], tabrows[l][:, bass.ds(b, 1), :].rearrange("p b d -> p (b d)")).then_inc(s["self_ok"][q], 16)
                    if l == 1:
                        sp.dma_start(xres[q][:], xrows[:, bass.ds(b, 1), :].rearrange("p b d -> p (b d)")).then_inc(s["xres_ok"][q], 16)

                for b in range(2):
                    load_edges(b, b)
                    load_nodes(b, b)

                def agg_block(b, half, q, s=s, l=l):
                    last = isinstance(b, int) and b >= NB - 2
                    if not last:
                        sp.wait_ge(s["gathered"][q], (half + 1) * (16 * T))
                        sp.wait_ge(s["onehot_ok"], b + 1)
                        load_edges(b + 2, q)
                    if l == 0:
                        sp.wait_ge(s["hh_copied"], b + 1)
                        sp.dma_start(tabrows[1][:, bass.ds(b, 1), :].rearrange("p b d -> p (b d)"),
                                     hout[q][:, 0, 0:HW]).then_inc(s["stored"][q], 16)
                    else:
                        sp.wait_ge(s["feat_ok"], b + 1)
                        sp.dma_start(x1rows[:, bass.ds(b, 1), :].rearrange("p b d -> p (b d)"), x1[q][:]).then_inc(s["stored"][q], 16)
                        sp.dma_start(xnrows[:, bass.ds(b, 1), :].rearrange("p b d -> p (b d)"), xn2[q][:]).then_inc(s["stored"][q], 16)
                        sp.wait_ge(s["ft_copied"], b + 1)
                        sp.dma_start(xT_d.rearrange("t p n -> p t n")[:, :, bass.ds(b * NBLK, NBLK)], hT[q][:]).then_inc(s["stored2"][q], 16)
                    if not last:
                        sp.wait_ge(s["epi_done"], b + 1)
                        load_nodes(b + 2, q)
                ch.steps(NB, 2, 2, agg_block)
                for q in range(2):
                    sp.wait_ge(s["stored"][q], 16 * (l + 1) * (NB // 2))
                    if l == 1:
                        sp.wait_ge(s["stored2"][q], 16 * (NB // 2))
                if l == 0:
                    sp.sem_inc(s["parts"], 1)

            sp.wait_ge(r_sel, 1)
            for k in range(TOP_K):
                e = sp.value_load(sel_i[0:1, k:k + 1], min_val=0, max_val=NX - 1)
                sp.dma_start(eW1[:, k, :, :], fW1[bass.ds(e, 1), :, :].rearrange("e (t p) f -> p (e t) f", p=P)).then_inc(r_load, 16)
                sp.dma_start(eW2[:, k, :, :], fW2[bass.ds(e, 1), :, :].rearrange("e (t p) n -> p (e t) n", p=P)).then_inc(r_load, 16)
                with nc.allow_non_contiguous_dma(reason="a bias by partition"):
                    sp.dma_start(eb1[:, k, :], fb1[bass.ds(e, 1), :].rearrange("e (t p) -> p (e t)", p=P)).then_inc(r_load, 16)
                sp.dma_start(eb2[:, k, :], fb2[bass.ds(e, 1), :]).then_inc(r_load, 16)

            def load_chunk(g, q):
                sp.dma_start(fxT[q][:], xT_d.rearrange("t p n -> p t n")[:, :, bass.ds(g * CHUNK, CHUNK)]).then_inc(f_ok[q], 16)
                sp.dma_start(xng[q][:], xnrows[:, bass.ds(g * GRP, GRP), :]).then_inc(f_ok[q], 16)
                sp.dma_start(fx1[q][:], x1rows[:, bass.ds(g * GRP, GRP), :]).then_inc(f_ok[q], 16)
            for g in range(2):
                load_chunk(g, g)

            def ffn_chunk(g, half, q):
                sp.wait_ge(f_done, g + 1)
                sp.dma_start(outrows[:, bass.ds(g * GRP, GRP), :], xg[q][:]).then_inc(f_st[q], 16)
                if not isinstance(g, int) or g < NG - 2:
                    sp.wait_ge(f_hid, g * (TOP_K * FT) + TOP_K * FT)
                    load_chunk(g + 2, q)
            ch.steps(NG, 2, 3, ffn_chunk)
            sp.wait_ge(f_st[0], 16 * ((NG + 1) // 2))
            sp.wait_ge(f_st[1], 16 * (NG // 2))

        @block.gpsimd
        def _(pool):
            ch = Chain(pool, None)
            nc.gpsimd.memset(ident[:], 0.0).then_inc(s_const, 1)
            nc.gpsimd.iota(node_iota[:], [[1, NBLK]], base=0, channel_multiplier=0, allow_small_or_imprecise_dtypes=True).then_inc(s_const, 1)
            nc.gpsimd.iota(block_base[:], [[NBLK, NB]], base=0, channel_multiplier=0, allow_small_or_imprecise_dtypes=True).then_inc(s_const, 1)
            nc.gpsimd.iota(first_node[:], [[0, 1]], base=0, channel_multiplier=NBLK, allow_small_or_imprecise_dtypes=True).then_inc(s_const, 1)
            nc.gpsimd.iota(rt[:, 1, :], [[1, NX]], base=0, channel_multiplier=0, allow_small_or_imprecise_dtypes=True).then_inc(s_const, 1)
            pool.wait_ge(s_const, 5)
            nc.gpsimd.affine_select(out=ident[:], in_=ident[:], compare_op=ALU.not_equal, fill=1.0, base=0,
                                    pattern=[[-1, P]], channel_multiplier=1).then_inc(s_const, 1)
            pool.wait_ge(s_idx, 1)
            pool.indirect_dma_start(out=swin[:], out_offset=None, in_=dst.rearrange("(n k) -> n k", k=SAMP),
                                    in_offset=bass.IndirectOffsetOnAxis(ap=st_i[:], axis=0),
                                    bounds_check=E // SAMP - 1, oob_is_err=False).then_inc(s_swin, 16)

            for l in range(2):
                s = L[l]
                if l == 0:
                    pool.wait_ge(tab_st[0], 16 * ((NG + 1) // 2))
                    pool.wait_ge(tab_st[1], 16 * (NG // 2))
                else:
                    for q in range(2):
                        pool.wait_ge(L[0]["stored"][q], 16 * (NB // 2))

                def gather(b, half, q, s=s, l=l):
                    pool.wait_ge(s["src_ok"][q], half * 16 + 16)
                    if not isinstance(b, int) or b >= 2:
                        pool.wait_ge(s["main_done"], b - 1)
                    elif l == 1:
                        pool.wait_ge(L[0]["main_done"], NB)
                    pool.sem_inc(wait_here, 1)
                    for t in range(T):
                        pool.indirect_dma_start(out=G[q][:, t, 0:HW], out_offset=None, in_=tables[l],
                                                in_offset=bass.IndirectOffsetOnAxis(ap=src_w[q][:, t:t + 1], axis=0),
                                                bounds_check=N - 1, oob_is_err=False).then_inc(s["gathered"][q], 16)
                ch.steps(NB, 2, 2, gather)

        @block.tensor
        def _(pe):
            ch = Chain(pe, None)
            pe.wait_ge(s_const, 6)
            pe.wait_ge(s_in, SETUP_LOADS)
            for l in range(2):
                if l == 1:
                    pe.wait_ge(s_wTc, 1)
                for i in range(KT):
                    for j in range(KT):
                        m = pe.transpose(p_xt[:, (j * KT + i) * P:(j * KT + i + 1) * P], wext[l][:, i, j * P:(j + 1) * P], ident[:])
                m.then_inc(s_wT, 1)
                pe.wait_ge(s_wTc, l + 1)
                pe.wait_ge(s_att, 1)
                for i in range(KT):
                    for j in range(KT):
                        m = pe.matmul(p_small[:, (l * KT + i) * 16:(l * KT + i) * 16 + 2 * HEADS], wT[:, j, i * P:(i + 1) * P], attm[:, l, j, :],
                                      start=(j == 0), stop=(j == KT - 1))
                m.then_inc(s_watt, 1)
            pe.wait_ge(s_wext, 2)
            xtb, hb = [p_xt, p_rows], [p_h, p_expand]

            def table_group(g, half, q):
                pe.wait_ge(x_norm, g + 1)
                for j in range(GRP):
                    c, k = g * GRP + j, j % 2
                    early = isinstance(c, int) and c < 2
                    if not early:
                        pe.wait_ge(xt_copied, c - 1)
                    for t in range(KT):
                        m = pe.transpose(xtb[k][:, t * P:t * P + NBLK], xng[q][:, j, t * P:(t + 1) * P], ident[0:NBLK, 0:NBLK])
                    m.then_inc(xt_done, 1)
                    pe.wait_ge(xt_copied, c + 1)
                    if not early:
                        pe.wait_ge(h_copied, c - 1)
                    for t in range(KT):
                        m = pe.matmul(hb[k][0:NBLK, 0:HWX], xT[k][:, t, :], wext[0][:, t, :], start=(t == 0), stop=(t == KT - 1))
                    m.then_inc(h_done, 1)
            ch.steps(NG, 2, 3, table_group)
            pe.wait_ge(s_st, 1)
            pe.transpose(p_small[0:1, 128:128 + NB], st_f[:, 4:5], ident[0:NB, 0:NB]).then_inc(s_stT, 1)

            for l in range(2):
                s = L[l]
                pe.wait_ge(h_copied, NB)
                if l == 1:
                    pe.wait_ge(L[0]["hh_copied"], NB)
                    pe.wait_ge(L[0]["epi_done"], NB)
                pe.wait_ge(s_starts, 1)

                def pre(b, q, s=s):
                    pe.wait_ge(s["onehot_ok"], b + 1)
                    for gi in range(NGROUPS_ST):
                        n = b * NGROUPS_ST + gi
                        if not (isinstance(n, int) and n < 2):
                            pe.wait_ge(s["st_copied"], n - 1)
                        lo, hi = gi * STG, min(T, gi * STG + STG)
                        bankt = p_st[(gi + q * (NGROUPS_ST % 2)) % 2]
                        for t in range(lo, hi):
                            m = pe.transpose(bankt[0:NBLK, (t - lo) * P:(t - lo + 1) * P], onehot[q][:, t, :], ident[:])
                        m.then_inc(s["st_done"], 1)
                    if not (isinstance(b, int) and b == 0):
                        pe.wait_ge(s["expand_read"], b)
                    for gi in range(NGROUPS_ST):
                        pe.wait_ge(s["st_copied"], b * NGROUPS_ST + gi + 1)
                        for t in range(gi * STG, min(T, gi * STG + STG)):
                            m = pe.matmul(p_expand[:, t * 24:t * 24 + 24], onehotT[:, t, :], parts_q[q][:, :], start=True, stop=True)
                    m.then_inc(s["expand_done"], 1)

                def agg_block(b, half, q, s=s, l=l):
                    pe.wait_ge(s["ends_ok"], b + 1)
                    for i, a in enumerate((rF[:, :, T], whole[q][:, 0, :], rB[:, :, 0], whole[q][:, 1, :])):
                        m = pe.transpose(p_rows[0:HEADS, i * P:(i + 1) * P], a, ident[:])
                    m.then_inc(s["rows_done"], 1)
                    pe.wait_ge(s["carry_ok"], b + 1)
                    pe.sem_inc(wait_here, 1)
                    pe.transpose(p_small[:, 0:HEADS], carF[:, 0:P], ident[0:HEADS, 0:HEADS])
                    pe.transpose(p_small[:, HEADS:2 * HEADS], carB[:, 1:P + 1], ident[0:HEADS, 0:HEADS]).then_inc(s["back_done"], 1)
                    if not (isinstance(b, int) and b == 0):
                        pe.wait_ge(s["acc_read"], b)
                    for t in range(T):
                        if t % 6 == 0:
                            pe.wait_ge(s["prod_ok"], b * 3 + (t // 6 + 1))
                        m = pe.matmul(p_acc[0:NBLK, 0:GW], onehot[q][:, t, :], G[q][:, t, :], start=(t == 0), stop=(t == T - 1))
                    m.then_inc(s["main_done"], 1)
                    if not (isinstance(b, int) and b == NB - 1):
                        pre(b + 1, 1 - q)
                    pe.wait_ge(s["feat_ok"], b + 1)
                    f = h1 if l == 0 else xn2[q]
                    if not (isinstance(b, int) and b == 0):
                        pe.wait_ge(s["ft_copied"], b)
                    for t in range(KT):
                        m = pe.transpose(p_xt[:, t * P:t * P + NBLK], f[:, t * P:(t + 1) * P], ident[0:NBLK, 0:NBLK])
                    m.then_inc(s["ft_done"], 1)
                    if l == 0:
                        pe.wait_ge(s["ft_copied"], b + 1)
                        if not (isinstance(b, int) and b == 0):
                            pe.wait_ge(s["hh_copied"], b)
                        for t in range(KT):
                            m = pe.matmul(p_h[0:NBLK, 0:HWX], hT[q][:, t, :], wext[1][:, t, :], start=(t == 0), stop=(t == KT - 1))
                        m.then_inc(s["hh_done"], 1)
                pre(0, 0)
                ch.steps(NB, 2, 2, agg_block)

            pe.wait_ge(r_mean, 1)
            for t in range(KT):
                m = pe.matmul(p_small[0:1, 0:NX], mean[:, t:t + 1], wr_sb[:, t, :], start=(t == 0), stop=(t == KT - 1))
            m.then_inc(r_logit, 1)
            pe.wait_ge(r_w, 1)
            pe.matmul(p_small[:, 16:16 + TOP_K], ones[:, :], wsel[:, :], start=True, stop=True).then_inc(r_wb, 1)

            pe.wait_ge(r_ready, 1)
            hbank = [p_st[0], p_st[1], p_expand, p_rows]
            obank = [p_acc, p_xt, p_h, p_small]

            def ffn_chunk(g, half, q):
                pe.wait_ge(f_ok[q], half * 48 + 48)
                for n in range(TOP_K * FT):
                    c = g * (TOP_K * FT) + n
                    if not (isinstance(c, int) and c < 4):
                        pe.wait_ge(f_gelu, c - 3)
                    for t in range(KT):
                        m = pe.matmul(hbank[n % 4][:, 0:CHUNK], eW1[:, n // FT, t, (n % FT) * P:(n % FT + 1) * P], fxT[q][:, t, :],
                                      start=(t == 0), stop=(t == KT - 1))
                    m.then_inc(f_hid, 1)
                pe.wait_ge(f_gelu, g * (TOP_K * FT) + TOP_K * FT)
                for j in range(GRP):
                    if not (isinstance(g, int) and g == 0):
                        pe.wait_ge(f_read, g * GRP + (j + 1 - GRP))
                    pe.matmul(obank[j][0:NBLK, 0:D], ones[:, 0:NBLK], eb2s[:, :], start=True, stop=False)
                    for n in range(TOP_K * FT):
                        m = pe.matmul(obank[j][0:NBLK, 0:D], hid[q][:, n, j * NBLK:(j + 1) * NBLK], eW2[:, n // FT, n % FT, :],
                                      start=False, stop=(n == TOP_K * FT - 1))
                    m.then_inc(f_out, 1)
            ch.steps(NG, 2, 3, ffn_chunk)

        @block.scalar
        def _(act):
            ch = Chain(act, act_s)
            for l in range(2):
                act.wait_ge(s_wT, l + 1)
                if l == 1:
                    act.wait_ge(s_watt, 1)
                nc.scalar.copy(wT[:].rearrange("p t n -> p (t n)"), p_xt[:, 0:KT * D]).then_inc(s_wTc, 1)
                act.wait_ge(s_watt, l + 1)
                for i in range(KT):
                    m = nc.scalar.copy(wext[l][:, i, D:HWX], p_small[:, (l * KT + i) * 16:(l * KT + i) * 16 + 2 * HEADS])
                    if i == KT - 1:
                        m.then_inc(s_wext, 1)
            act.wait_ge(s_wext, 2)
            xtb, hb = [p_xt, p_rows], [p_h, p_expand]

            def table_group(g, half, q):
                for j in range(GRP):
                    c, k = g * GRP + j, j % 2
                    early = isinstance(c, int) and c < 2
                    act.wait_ge(xt_done, c + 1)
                    if not early:
                        act.wait_ge(h_done, c - 1)
                    nc.scalar.copy(xT[k][:], xtb[k][:, 0:KT * P].rearrange("p (t n) -> p t n", t=KT)[:, :, 0:NBLK]).then_inc(xt_copied, 1)
                    act.wait_ge(h_done, c + 1)
                    if j == 0 and not (isinstance(g, int) and g < 2):
                        act.wait_ge(tab_st[q], half * 16)
                    nc.scalar.copy(node[0][:, bass.ds(c, 1), :].rearrange("p b n -> p (b n)"), hb[k][0:NBLK, D:HWX])
                    nc.scalar.copy(hout[q][:, j, :], hb[k][0:NBLK, 0:HWX]).then_inc(h_copied, 1)
            ch.steps(NG, 2, 3, table_group)

            for l in range(2):
                s = L[l]

                def pre(b, q, s=s):
                    for gi in range(NGROUPS_ST):
                        act.wait_ge(s["st_done"], b * NGROUPS_ST + gi + 1)
                        if gi == 0 and not (isinstance(b, int) and b == 0):
                            act.wait_ge(s["expand_done"], b)
                        lo, hi = gi * STG, min(T, gi * STG + STG)
                        nc.scalar.copy(onehotT[:, lo:hi, :], p_st[(gi + q * (NGROUPS_ST % 2)) % 2][0:NBLK, 0:(hi - lo) * P].rearrange("p (t n) -> p t n", n=P)).then_inc(s["st_copied"], 1)

                def agg_block(b, half, q, s=s, l=l):
                    act.wait_ge(s["logit_ok"], b + 1)
                    nc.scalar.activation(G[q][:, :, D:HW], logit[:], ACT.Exp).then_inc(s["exp_ok"], 1)
                    if not (isinstance(b, int) and b == NB - 1):
                        pre(b + 1, 1 - q)
                    act.wait_ge(s["sarg_ok"], b + 1)
                    nc.scalar.activation(self_s[:, 3, :], self_s[:, 2, :], ACT.Exp).then_inc(s["sexp_ok"], 1)
                    act.wait_ge(s["ft_done"], b + 1)
                    if not (isinstance(b, int) and b < 2):
                        if l == 0:
                            act.wait_ge(s["hh_done"], b - 1)
                        else:
                            act.wait_ge(s["stored2"][q], half * 16)
                    elif l == 1:
                        act.wait_ge(L[0]["hh_done"], NB)
                    if l == 0:
                        nc.scalar.copy(hT[q][:], p_xt[:, 0:KT * P].rearrange("p (t n) -> p t n", t=KT)[:, :, 0:NBLK]).then_inc(s["ft_copied"], 1)
                        act.wait_ge(s["hh_done"], b + 1)
                        if not (isinstance(b, int) and b < 2):
                            act.wait_ge(s["stored"][q], half * 16)
                        elif b == 0:
                            act.wait_ge(tab_st[0], 16 * ((NG + 1) // 2))
                            act.wait_ge(tab_st[1], 16 * (NG // 2))
                        nc.scalar.copy(node[1][:, bass.ds(b, 1), :].rearrange("p b n -> p (b n)"), p_h[0:NBLK, D:HWX])
                        nc.scalar.copy(hout[q][:, 0, :], p_h[0:NBLK, 0:HWX]).then_inc(s["hh_copied"], 1)
                    else:
                        for t in range(KT):
                            m = nc.scalar.activation(hT[q][:, t, :], p_xt[:, t * P:t * P + NBLK], ACT.Copy,
                                                     accum_out=colsum[:, t, bass.ds(b, 1)])
                        m.then_inc(s["ft_copied"], 1)
                pre(0, 0)
                ch.steps(NB, 2, 2, agg_block)

            for arg, done in ((r_arg, r_exp), (r_arg2, r_exp2), (r_arg3, r_exp3)):
                act.wait_ge(arg, 1)
                nc.scalar.activation(rt[:, 4, :], rt[:, 3, :], ACT.Exp).then_inc(done, 1)
            act.wait_ge(r_ready, 1)
            hbank = [p_st[0], p_st[1], p_expand, p_rows]

            def ffn_chunk(g, half, q):
                for n in range(TOP_K * FT):
                    c = g * (TOP_K * FT) + n
                    act.wait_ge(f_hid, c + 1)
                    if n == 0 and not (isinstance(g, int) and g < 2):
                        act.wait_ge(f_out, g * GRP - GRP)
                    nc.scalar.activation(hid[q][:, n, :], hbank[n % 4][:, 0:CHUNK], ACT.Gelu,
                                         bias=eb1[:, n // FT, n % FT:n % FT + 1]).then_inc(f_gelu, 1)
            ch.steps(NG, 2, 3, ffn_chunk)

        @block.vector
        def _(dve):
            vec = nc.vector
            ch = Chain(dve, dve_s)
            link = ch.link
            link(vec.memset(sentinel[:, 0:1], -1.0))
            link(vec.memset(sentinel[:, 1:2], -2.0))
            dve.wait_ge(s_dst, 16)
            link(vec.tensor_copy(dst_f, dst_i))
            vec.tensor_copy(samp[:], dst_f.rearrange("p (n k) -> p n k", k=SAMP)[:, :, 0]).then_inc(s_dstf, 1)
            link(vec.memset(ones[:], 1.0))
            link(vec.memset(attm[:].rearrange("p l t h -> p (l t h)"), 0.0))
            dve.wait_ge(s_in, SETUP_LOADS)
            for i in range(4):
                for h in range(HEADS):
                    p0, t = (h % 2) * C, h // 2
                    m = vec.tensor_copy(attm[p0:p0 + C, i // 2, t, (i % 2) * HEADS + h:(i % 2) * HEADS + h + 1], att[p0:p0 + C, i, t:t + 1])
            m.then_inc(s_att, 1)
            dve.wait_ge(s_const, 6)
            dve.wait_ge(s_sampb, 16)
            link(vec.tensor_scalar(samp_lt, samp_b, first_node[:, 0:1], None, ALU.is_lt))
            link(vec.tensor_reduce(st_f[:, 0:1], samp_lt, AX.X, ALU.add))
            link(vec.tensor_scalar(st_f[:, 1:2], st_f[:, 0:1], -1.0, 0.0, ALU.add, ALU.max))
            vec.tensor_copy(st_i[:], st_f[:, 1:2]).then_inc(s_idx, 1)
            dve.wait_ge(s_swin, 16)
            link(vec.tensor_scalar(swin_lt[:], swin[:], first_node[:, 0:1], None, ALU.is_lt))
            link(vec.tensor_reduce(st_f[:, 2:3], swin_lt[:], AX.X, ALU.add))
            link(vec.tensor_scalar(st_f[:, 3:4], st_f[:, 1:2], float(SAMP), st_f[:, 2:3], ALU.mult, ALU.add))
            vec.tensor_scalar(st_f[:, 4:5], st_f[:, 3:4], float(E - CAP), None, ALU.min).then_inc(s_st, 1)

            def table_group(g, half, q):
                dve.wait_ge(x_ok[q], half * 16 + 16)
                for j in range(GRP):
                    link(vec.bn_stats(stats[:, j, :], xg[q][:, j, :]))
                    dve.sem_inc(wait_here, 1)
                    link(vec.bn_aggr(mv[:, j, :], stats[:, j, :]))
                rsqrt(ch, mv[:, :, 1], GRP, rs, rs_i)
                if not (isinstance(g, int) and g < 2):
                    dve.wait_ge(xt_done, g * GRP - GRP)
                for j in range(GRP):
                    m = vec.tensor_scalar(xng[q][:, j, :], xg[q][:, j, :], mv[:, j, 0:1], rs[:, 0, j:j + 1], ALU.subtract, ALU.mult)
                m.then_inc(x_norm, 1)
            ch.steps(NG, 2, 3, table_group)
            dve.wait_ge(s_stT, 1)
            vec.tensor_copy(starts_i[:], p_small[0:1, 128:128 + NB]).then_inc(s_starts, 1)

            for t_, col in ((vF, 0), (vB, T)):
                link(vec.memset(t_[:, :, col], -BIG))
            for q in range(2):
                link(vec.memset(penF[q][:, :, 0], -BIG))
                link(vec.memset(penB[q][:, :, T], -BIG))
            link(vec.memset(carF[:, 0:1], -BIG))
            link(vec.memset(carB[:, P:P + 1], -BIG))
            link(vec.memset(zeros[:], 0.0))

            for l in range(2):
                s = L[l]
                if l == 0:
                    dve.wait_ge(h_copied, NB)
                else:
                    dve.wait_ge(L[0]["hh_copied"], NB)
                    dve.wait_ge(L[0]["expand_done"], NB)
                link(vec.tensor_copy(node_parts[:, :, 0, :], node[l][:]))
                link(vec.tensor_tensor(node_rest[:], node[l][:], node_parts[:, :, 0, :], ALU.subtract))
                link(vec.tensor_copy(node_parts[:, :, 1, :], node_rest[:]))
                link(vec.tensor_tensor(node_rest[:], node_rest[:], node_parts[:, :, 1, :], ALU.subtract))
                link(vec.tensor_copy(node_parts[:, :, 2, :], node_rest[:]))

                def pre(b, q, s=s, l=l):
                    dve.wait_ge(s["dst_ok"][q], (b.half if False else 0) + pre_half(b, q) * 16 + 16)
                    if not (isinstance(b, int) and b < 2):
                        dve.wait_ge(s["main_done"], b - 1)
                    elif l == 1:
                        dve.wait_ge(L[0]["main_done"], NB)
                    d = dst_w[q]
                    link(vec.tensor_copy(node_q[q][:], node[l][:, bass.ds(b, 1), :].rearrange("p b n -> p (b n)")))
                    link(vec.tensor_copy(parts_q[q][:], node_parts[:, bass.ds(b, 1), :, :].rearrange("p b k n -> p (b k n)")))
                    link(vec.tensor_scalar(dloc[:], d[:, 1:T + 1], block_base[:, bass.ds(b, 1)], None, ALU.subtract))
                    link(vec.tensor_tensor(link_w[:], d[:, 0:T + 1], d[:, 1:T + 2], ALU.is_equal))
                    link(vec.tensor_scalar(pen[:], link_w[:], -1.0, BIG, ALU.add, ALU.mult))
                    link(vec.tensor_scalar(run_end[q][:], link_w[:, 1:T + 1], -1.0, 1.0, ALU.mult, ALU.add))
                    link(vec.tensor_copy(penF[q][:, :, 1:T + 1], pen[:, 0:T].unsqueeze(1).to_broadcast([P, HEADS, T])))
                    link(vec.tensor_copy(penB[q][:, :, 0:T], pen[:, 1:T + 1].unsqueeze(1).to_broadcast([P, HEADS, T])))
                    link(vec.tensor_tensor(whole[q][:, 0, :], d[:, 0:1].to_broadcast([P, HEADS]), d[:, T:T + 1].to_broadcast([P, HEADS]), ALU.is_equal))
                    link(vec.tensor_tensor(whole[q][:, 1, :], d[:, 1:2].to_broadcast([P, HEADS]), d[:, T + 1:T + 2].to_broadcast([P, HEADS]), ALU.is_equal))
                    link(vec.tensor_scalar(whole[q][:], whole[q][:], -1.0, BIG, ALU.add, ALU.mult))
                    link(vec.tensor_tensor(onehot[q][:], node_iota[:, :].unsqueeze(1).to_broadcast([P, T, NBLK]),
                                           dloc[:].unsqueeze(2).to_broadcast([P, T, NBLK]), ALU.is_equal))
                    dve.sem_inc(s["onehot_ok"], 1)
                    dve.wait_ge(s["expand_done"], b + 1)
                    vec.tensor_reduce(expn[q][:], p_expand[:, 0:T * 24].rearrange("p (t k n) -> p t n k", k=3, n=2 * HEADS),
                                      AX.X, ALU.add).then_inc(s["expand_read"], 1)
                    dve.wait_ge(s["expand_read"], b + 1)

                def pre_half(b, q):
                    return half_of[0]

                half_of = [0]

                def agg_block(b, half, q, s=s, l=l):
                    g = G[q]
                    dve.wait_ge(s["gathered"][q], (half + 1) * (16 * T))
                    a_src = g[:, :, D:HW].rearrange("p t h -> p h t")
                    link(vec.tensor_copy(vF[:, :, 1:T + 1], a_src))
                    link(vec.tensor_copy(vB[:, :, 0:T], a_src))

                    def flat(a):
                        return a[:].rearrange("p h t -> p (h t)")

                    def scans():
                        link(vec.tensor_tensor_scan(flat(rF), flat(penF[q]), flat(vF), -BIG, ALU.add, ALU.max))
                        link(vec.tensor_tensor_scan(flat(rB)[:, ::-1], flat(penB[q])[:, ::-1], flat(vB)[:, ::-1], -BIG, ALU.add, ALU.max))
                    scans()
                    dve.sem_inc(s["ends_ok"], 1)
                    dve.wait_ge(s["rows_done"], b + 1)
                    rows = p_rows[0:HEADS, :].rearrange("h (i p) -> h i p", p=P)
                    link(vec.tensor_copy(row_pen[:, 0, :], rows[:, 1, :]))
                    link(vec.tensor_copy(row_pen[:, 1, :], rows[:, 3, :]))
                    link(vec.tensor_tensor_scan(carF[:, 1:P + 1], row_pen[:, 0, :], rows[:, 0, :], -BIG, ALU.add, ALU.max))
                    link(vec.tensor_tensor_scan(carB[:, 0:P][:, ::-1], row_pen[:, 1, :][:, ::-1], rows[:, 2, :][:, ::-1], -BIG, ALU.add, ALU.max))
                    dve.sem_inc(s["carry_ok"], 1)
                    dve.wait_ge(s["back_done"], b + 1)
                    link(vec.tensor_copy(vF[:, :, 0], p_small[:, 0:HEADS]))
                    link(vec.tensor_copy(vB[:, :, T], p_small[:, HEADS:2 * HEADS]))
                    scans()
                    link(vec.memset(vF[:, :, 0], -BIG))
                    link(vec.memset(vB[:, :, T], -BIG))
                    a_self, a_dst = expn[q][:, :, 0:HEADS], expn[q][:, :, HEADS:2 * HEADS]
                    link(vec.tensor_tensor(runmax[:], rF[:, :, 1:T + 1].rearrange("p h t -> p t h"), rB[:, :, 0:T].rearrange("p h t -> p t h"), ALU.max))
                    link(vec.tensor_tensor(runmax[:], runmax[:], a_self, ALU.max))
                    link(vec.tensor_tensor(runmax[:], runmax[:], a_dst, ALU.add))
                    link(vec.scalar_tensor_tensor(runmax[:], runmax[:], SLOPE, runmax[:], ALU.mult, ALU.max))
                    link(vec.tensor_tensor(alpha[:], g[:, :, D:HW], a_dst, ALU.add))
                    link(vec.scalar_tensor_tensor(alpha[:], alpha[:], SLOPE, alpha[:], ALU.mult, ALU.max))
                    link(vec.tensor_tensor(alpha[:], alpha[:], runmax[:], ALU.subtract))
                    link(vec.tensor_scalar(logit[:], alpha[:], 0.0, None, ALU.min))
                    dve.sem_inc(s["logit_ok"], 1)
                    link(vec.tensor_tensor(g[:, :, HW:HW + HEADS], runmax[:], run_end[q][:].unsqueeze(2).to_broadcast([P, T, HEADS]), ALU.mult))
                    link(vec.tensor_copy(g[:, :, HW + HEADS], run_end[q][:]))
                    dve.wait_ge(s["exp_ok"], b + 1)
                    for i in range(3):
                        t0, t1 = i * 6, i * 6 + 6
                        hv = g[:, t0:t1, 0:D].rearrange("p t (h c) -> p t h c", h=HEADS)
                        vec.tensor_tensor(hv, hv, g[:, t0:t1, D:HW].unsqueeze(3).to_broadcast([P, 6, HEADS, C]), ALU.mult).then_inc(s["prod_ok"], 1)

                    if not (isinstance(b, int) and b == NB - 1):
                        half_of[0] = half + q
                        pre(b + 1, 1 - q)

                    dve.wait_ge(s["main_done"], b + 1)
                    nq = node_q[q]
                    acc = p_acc[0:NBLK, :]
                    own, top, arg, es, den = (self_s[:, i, :] for i in (0, 1, 2, 3, 4))
                    link(vec.tensor_tensor(own, nq[:, 0:HEADS], nq[:, HEADS:2 * HEADS], ALU.add))
                    link(vec.scalar_tensor_tensor(own, own, SLOPE, own, ALU.mult, ALU.max))
                    link(vec.tensor_scalar(self_s[:, 5, 0:1], acc[:, GW - 1:GW], -1.0, BIG, ALU.add, ALU.mult))
                    link(vec.tensor_scalar(top, acc[:, HW:HW + HEADS], self_s[:, 5, 0:1], None, ALU.add))
                    link(vec.tensor_tensor(top, top, own, ALU.max))
                    link(vec.tensor_tensor(arg, own, top, ALU.subtract))
                    dve.sem_inc(s["sarg_ok"], 1)
                    dve.wait_ge(s["self_ok"][q], half * 16 + 16)
                    dve.wait_ge(s["sexp_ok"], b + 1)
                    link(vec.tensor_tensor(den, acc[:, D:HW], es, ALU.add))
                    link(vec.tensor_scalar(den, den, 1e-16, None, ALU.max))
                    link(vec.reciprocal(den, den))

                    def by_head(a):
                        return a.rearrange("p (h c) -> p h c", h=HEADS)
                    link(vec.tensor_tensor(by_head(hs[:]), by_head(hself[q][:, 0:D]), es.unsqueeze(2).to_broadcast([NBLK, HEADS, C]), ALU.mult))
                    link(vec.tensor_tensor(num[:], hs[:], acc[:, 0:D], ALU.add))
                    dve.sem_inc(s["acc_read"], 1)
                    link(vec.tensor_tensor(by_head(num[:]), by_head(num[:]), den.unsqueeze(2).to_broadcast([NBLK, HEADS, C]), ALU.mult))
                    if l == 0:
                        link(vec.tensor_tensor(num[:], num[:], bias[0][:], ALU.add))
                        dve.sem_inc(s["epi_done"], 1)
                        if not (isinstance(b, int) and b == 0):
                            dve.wait_ge(s["ft_done"], b)
                        vec.tensor_scalar(h1[:], num[:], 0.0, None, ALU.max).then_inc(s["feat_ok"], 1)
                    else:
                        link(vec.tensor_tensor(num[:], num[:], bias[1][:], ALU.add))
                        dve.wait_ge(s["xres_ok"][q], half * 16 + 16)
                        if not (isinstance(b, int) and b < 2):
                            dve.wait_ge(s["stored"][q], half * 32)
                            dve.wait_ge(s["ft_done"], b - 1)
                        link(vec.tensor_tensor(x1[q][:], num[:], xres[q][:], ALU.add))
                        dve.sem_inc(s["epi_done"], 1)
                        link(vec.bn_stats(stats[:, 0, :], x1[q][:]))
                        dve.sem_inc(wait_here, 1)
                        link(vec.bn_aggr(mv[:, 0, :], stats[:, 0, :]))
                        rsqrt(ch, mv[:, 0, 1:2], 1, rs, rs_i)
                        vec.tensor_scalar(xn2[q][:], x1[q][:], mv[:, 0, 0:1], rs[:, 0, 0:1], ALU.subtract, ALU.mult).then_inc(s["feat_ok"], 1)

                half_of[0] = 0
                pre(0, 0)
                ch.steps(NB, 2, 2, agg_block)

            dve.wait_ge(L[1]["ft_copied"], NB)
            link(vec.tensor_reduce(mean[:], colsum[:], AX.X, ALU.add))
            vec.tensor_scalar(mean[:], mean[:], 1.0 / N, None, ALU.mult).then_inc(r_mean, 1)
            dve.wait_ge(r_logit, 1)
            R = lambda i: rt[:, i, :]
            S = lambda i, k: rt[:, i, k:k + 1]
            link(vec.tensor_tensor(R(2), p_small[0:1, 0:NX], R(0), ALU.add))

            def softmax(dst_i_, src_i_, arg, done):
                link(vec.tensor_reduce(S(5, 0), R(src_i_), AX.X, ALU.max))
                vec.tensor_scalar(R(3), R(src_i_), S(5, 0), None, ALU.subtract).then_inc(arg, 1)
                dve.wait_ge(done, 1)
                link(vec.tensor_reduce(S(5, 1), R(4), AX.X, ALU.add))
                link(vec.reciprocal(S(5, 2), S(5, 1)))
                link(vec.tensor_scalar(R(dst_i_), R(4), S(5, 2), None, ALU.mult))
            softmax(6, 2, r_arg, r_exp)
            link(vec.tensor_scalar(R(7), R(6), float(N), None, ALU.mult))
            link(vec.tensor_scalar(R(8), R(7), capacity, None, ALU.is_gt))
            link(vec.tensor_scalar(R(9), R(7), capacity, None, ALU.max))
            link(vec.reciprocal(R(9), R(9)))
            link(vec.tensor_scalar(R(9), R(9), capacity, -1.0, ALU.mult, ALU.add))
            link(vec.tensor_tensor(R(9), R(9), R(8), ALU.mult))
            link(vec.tensor_scalar(R(9), R(9), 1.0, None, ALU.add))
            link(vec.tensor_tensor(R(10), R(6), R(9), ALU.mult))
            softmax(6, 10, r_arg2, r_exp2)
            link(vec.memset(R(15), -BIG))
            for k in range(TOP_K):
                link(vec.tensor_reduce(S(15, k), R(6), AX.X, ALU.max))
                link(vec.tensor_scalar(R(11), R(6), S(15, k), None, ALU.not_equal))
                link(vec.scalar_tensor_tensor(R(12), R(11), 1024.0, R(1), ALU.mult, ALU.add))
                link(vec.tensor_reduce(S(13, k), R(12), AX.X, ALU.min))
                link(vec.tensor_scalar(R(14), R(1), S(13, k), None, ALU.is_equal))
                link(vec.scalar_tensor_tensor(R(6), R(14), -1024.0, R(6), ALU.mult, ALU.add))
            vec.tensor_copy(sel_i[:], rt[:, 13, 0:TOP_K]).then_inc(r_sel, 1)
            softmax(6, 15, r_arg3, r_exp3)
            vec.tensor_copy(wsel[:], rt[:, 6, 0:TOP_K]).then_inc(r_w, 1)
            dve.wait_ge(r_wb, 1)
            link(vec.tensor_copy(wsel_b[:], p_small[:, 16:16 + TOP_K]))
            dve.wait_ge(r_load, 16 * 4 * TOP_K)
            for k in range(TOP_K):
                w = eW2[:, k, :, :].rearrange("p t n -> p (t n)")
                link(vec.tensor_scalar(w, w, wsel_b[:, k:k + 1], None, ALU.mult))
            link(vec.tensor_scalar(eb2s[:], eb2[:, 0, :], wsel[:, 0:1], None, ALU.mult))
            vec.scalar_tensor_tensor(eb2s[:], eb2[:, 1, :], wsel[:, 1:2], eb2s[:], ALU.mult, ALU.add).then_inc(r_ready, 1)
            obank = [p_acc, p_xt, p_h, p_small]

            def ffn_chunk(g, half, q):
                dve.wait_ge(f_ok[q], half * 48 + 48)
                if not (isinstance(g, int) and g < 2):
                    dve.wait_ge(f_st[q], half * 16)
                y = xg[q]
                for j in range(GRP):
                    dve.wait_ge(f_out, g * GRP + (j + 1))
                    link(vec.tensor_tensor(y[:, j, :], obank[j][0:NBLK, 0:D], xng[q][:, j, :], ALU.add))
                    dve.sem_inc(f_read, 1)
                    link(vec.bn_stats(stats[:, j, :], y[:, j, :]))
                    dve.sem_inc(wait_here, 1)
                    link(vec.bn_aggr(mv[:, j, :], stats[:, j, :]))
                rsqrt(ch, mv[:, :, 1], GRP, rs, rs_i)
                for j in range(GRP):
                    link(vec.tensor_scalar(y[:, j, :], y[:, j, :], mv[:, j, 0:1], rs[:, 0, j:j + 1], ALU.subtract, ALU.mult))
                wide = [NBLK, GRP, D]
                link(vec.tensor_tensor(y[:], y[:], gamma_b[:].unsqueeze(1).to_broadcast(wide), ALU.mult))
                link(vec.tensor_tensor(y[:], y[:], beta_b[:].unsqueeze(1).to_broadcast(wide), ALU.add))
                vec.tensor_tensor(y[:], y[:], fx1[q][:], ALU.add).then_inc(f_done, 1)
            ch.steps(NG, 2, 3, ffn_chunk)


_INS = ["x", "src", "dst", "L0_gnn_W1", "L0_gnn_att_src1", "L0_gnn_att_dst1", "L0_gnn_b1", "L0_gnn_W2", "L0_gnn_att_src2",
        "L0_gnn_att_dst2", "L0_gnn_b2", "L0_ffn_Wr", "L0_ffn_br", "L0_ffn_W1", "L0_ffn_b1", "L0_ffn_W2", "L0_ffn_b2",
        "L0_ffn_gamma", "L0_ffn_beta"]


def kernel(**inputs):
    import numpy as np
    import concourse.bacc as bacc
    from concourse.bass_utils import run_bass_kernel_spmd

    nc = bacc.Bacc("TRN2", target_bir_lowering=False, num_devices=1)
    arrays, args = {}, []
    for name in _INS:
        a = np.ascontiguousarray(inputs[name])
        arrays[f"in_{name}"] = a
        args.append(nc.dram_tensor(f"in_{name}", a.shape, mybir.dt.from_np(a.dtype), kind="ExternalInput").ap())
    args.append(nc.dram_tensor("out_x", arrays["in_x"].shape, F32, kind="ExternalOutput").ap())
    build(nc, *args)
    r = run_bass_kernel_spmd(nc, [arrays], core_ids=[0])
    return r.results[0]["out_x"]
```

```python
import math
from contextlib import ExitStack

import concourse.bass as bass
from concourse import mybir

ALU = mybir.AluOpType
ACT = mybir.ActivationFunctionType
AX = mybir.AxisListType
F32 = mybir.dt.float32
BF16 = mybir.dt.bfloat16
I32 = mybir.dt.int32

P = 128
NBLK = 125
T = 18
CAP = P * T
HEADS = 4
STG = 8
GRP = 4
BIG = 1.0e30
SLOPE = 0.2
LN_EPS = 1e-5
RSQRT_MAGIC = float(0x5F3759DF)
TOP_K = 2


class Chain:

    def __init__(self, eng, sem):
        self.eng, self.sem = eng, sem
        self.base, self.n, self.per = 0, 0, {}

    def do(self, ins):
        self.n += 1
        ins.then_inc(self.sem, 1)
        return self.n

    def after(self, count):
        self.eng.wait_ge(self.sem, self.base + count)

    def link(self, ins):
        self.after(self.do(ins))

    def steps(self, total, first, last, body, unroll=2):
        rounds = (total - first - last) // unroll
        assert rounds * unroll == total - first - last

        def at(b, i, u):
            parts = (i * (unroll // 2) + (first + u) // 2, (first + u) % 2)
            if unroll == 6:
                parts += (i * 2 + (first + u) // 3, (first + u) % 3)
            body(b, *parts)
        for b in range(first):
            before = self.n
            at(b, 0, b - first)
            per = self.n - before
        start = self.n
        if rounds:
            with self.eng.Fori(0, rounds) as i:
                for u in range(unroll):
                    self.base, self.n = i * (unroll * per) + (start + u * per), 0
                    at(i * unroll + (first + u), i, u)
                    assert self.n == per, (self.n, per)
        self.base, self.n = 0, start + per * unroll * rounds
        for b in range(total - last, total):
            at(b, 0, b - first)


def build(nc, x, src, dst, W1, as1, ad1, b1, W2, as2, ad2, b2, Wr, br, fW1, fb1, fW2, fb2, gamma, beta, out):
    N, D = x.shape
    E, = src.shape
    C = D // HEADS
    KT = D // P
    NX, F = Wr.shape[1], fW1.shape[2]
    FT = F // P
    NB = N // NBLK
    NG = NB // GRP
    HW = D + HEADS
    HWX = D + 2 * HEADS
    GW = D + 2 * HEADS + 1
    ER = 125
    EC = E // ER
    SAMP = 68 if EC % 68 == 0 else EC
    NS = EC // SAMP
    CHUNK = GRP * NBLK
    NGROUPS_ST = (T + STG - 1) // STG
    capacity = float(math.ceil(N * 1.25 / NX))
    TG = max(t for t in range(1, T + 1) if EC % t == 0)
    NW = EC // TG
    TURN = 4
    NTURN = (TG + TURN - 1) // TURN
    assert KT == 2 and NB * NBLK == N and NG * GRP == NB and EC * ER == E and E >= CAP

    def dram(name, shape, dt=F32):
        return nc.dram_tensor(name, shape, dt).ap()

    dpad = dram("dpad", (E + 2,))
    samples_d = dram("samples_d", (ER * NS,))
    tables = [dram("table1", (N, HW)), dram("table2", (N, HW))]
    x1_d = dram("x1_d", (N, D))
    xn_d = dram("xn_d", (N, D))
    xT_d = dram("xT_d", (KT, P, N))

    with ExitStack() as ctx:
        def sb(name, shape, dt=F32):
            return ctx.enter_context(nc.sbuf_tensor(name, shape, dt))

        def sem(name):
            return ctx.enter_context(nc.semaphore(name))

        bank = {n: ctx.enter_context(nc.psum_tensor(n, [P, 512], F32)) for n in
                ("p_acc0", "p_acc1", "p_st0", "p_st1", "p_expand", "p_rows", "p_xt", "p_h")}
        p_expand, p_rows, p_xt, p_h = (bank[n] for n in ("p_expand", "p_rows", "p_xt", "p_h"))
        p_acc = [bank["p_acc0"], bank["p_acc1"]]
        p_st = [bank["p_st0"], bank["p_st1"]]
        p_stb = [b[:, :].bitcast(BF16) for b in p_st]
        p_small = bank["p_acc1"]
        p_back = p_rows[:, 0:2 * HEADS]

        ident = sb("ident", [P, P])
        ident_b = sb("ident_b", [P, P], BF16)
        ones = sb("ones", [1, P])
        node_iota = sb("node_iota", [P, NBLK])
        block_base = sb("block_base", [P, NB])
        bias = [sb("bias1", [NBLK, D]), sb("bias2", [NBLK, D])]
        gamma_b, beta_b = sb("gamma_b", [NBLK, D]), sb("beta_b", [NBLK, D])

        wext = [sb("wext1", [P, KT, HWX]), sb("wext2", [P, KT, HWX])]
        wT = sb("wT", [P, KT, D])
        att = sb("att", [P, 4, KT])
        attm = sb("attm", [P, 2, KT, 2 * HEADS])

        hid = [sb(f"hid{q}", [P, TOP_K * FT, CHUNK]) for q in range(2)]
        G = [sb(f"G{r}", [P, T, GW]) for r in range(3)]
        dst_i = hid[0][:].rearrange("p n c -> p (n c)")[0:ER, 0:EC].bitcast(I32)
        dst_f = hid[1][:].rearrange("p n c -> p (n c)")[0:ER, 0:EC]
        samp = sb("samp", [ER, NS])
        sentinel = sb("sentinel", [1, 2])
        samp_b = G[0][:].rearrange("p t n -> p (t n)")[0:NB, 0:ER * NS]
        samp_lt = G[1][:].rearrange("p t n -> p (t n)")[0:NB, 0:ER * NS]
        first_node = sb("first_node", [NB, 1])
        st_f = sb("st_f", [NB, 8])
        st_i = sb("st_i", [NB, 1], I32)
        swin = sb("swin", [NB, SAMP], I32)
        swin_lt = sb("swin_lt", [NB, SAMP])
        starts_i = sb("starts_i", [1, NB], I32)
        starts_row = sb("starts_row", [1, NB + 1])
        fits = sb("fits", [1, 4])
        fits_i = sb("fits_i", [1, 1], I32)
        next_f = G[2][:].rearrange("p t n -> p (t n)")[0:ER, 0:EC]
        falls = G[0][:].rearrange("p t n -> p (t n)")[0:ER, 0:EC]
        n_falls = sb("n_falls", [ER, 1])

        xg = [sb(f"xg{q}", [NBLK, GRP, D]) for q in range(2)]
        xng = [sb(f"xng{q}", [NBLK, GRP, D]) for q in range(2)]
        stats = sb("stats", [NBLK, GRP, 6])
        mv = sb("mv", [NBLK, GRP, 2])
        rs = sb("rs", [NBLK, 6, GRP])
        rs_i = sb("rs_i", [NBLK, 2, GRP], I32)
        xT = [sb(f"xT{q}", [P, KT, NBLK]) for q in range(2)]
        hout = [sb(f"hout{q}", [NBLK, GRP, HWX]) for q in range(2)]
        node = [sb("node1", [NBLK, NB, 2 * HEADS]), sb("node2", [NBLK, NB, 2 * HEADS])]

        node_parts = sb("node_parts", [NBLK, NB, 3, 2 * HEADS], BF16)
        node_rest = sb("node_rest", [NBLK, NB, 2 * HEADS])

        src_w = [sb(f"src_w{q}", [P, T], I32) for q in range(2)]
        dst_w = [sb(f"dst_w{q}", [P, T + 2]) for q in range(2)]
        hself = [sb(f"hself{q}", [NBLK, HW]) for q in range(2)]
        xres = [sb(f"xres{q}", [NBLK, D]) for q in range(2)]
        onehot = [sb(f"onehot{q}", [P, T, NBLK]) for q in range(2)]
        onehot_b = sb("onehot_b", [P, T, NBLK], BF16)
        onehotT = sb("onehotT", [NBLK, T, P], BF16)
        node_q = [sb(f"node_q{q}", [NBLK, 2 * HEADS]) for q in range(2)]
        parts_q = [sb(f"parts_q{q}", [NBLK, 3, 2 * HEADS], BF16) for q in range(2)]
        node_iota_b = sb("node_iota_b", [P, NBLK], BF16)
        dloc = sb("dloc", [P, T])
        link_w = sb("link_w", [P, T + 1])
        pen = sb("pen", [P, T + 1])
        run_end = [sb(f"run_end{q}", [P, T]) for q in range(2)]
        penF = [sb(f"penF{q}", [P, HEADS, T + 1]) for q in range(2)]
        penB = [sb(f"penB{q}", [P, HEADS, T + 1]) for q in range(2)]
        whole = [sb(f"whole{q}", [P, 2, HEADS]) for q in range(2)]
        vF = sb("vF", [P, HEADS, T + 1])
        vB = sb("vB", [P, HEADS, T + 1])
        rF = sb("rF", [P, HEADS, T + 1])
        rB = sb("rB", [P, HEADS, T + 1])
        row_pen = sb("row_pen", [HEADS, 2, P])
        carF = sb("carF", [HEADS, P + 1])
        carB = sb("carB", [HEADS, P + 1])
        runmax = sb("runmax", [P, T, HEADS])
        alpha = sb("alpha", [P, T, HEADS])
        logit = sb("logit", [P, T, HEADS])
        self_s = sb("self_s", [NBLK, 8, HEADS])
        hs = sb("hs", [NBLK, D])
        num = sb("num", [NBLK, D])
        h1 = sb("h1", [NBLK, D])
        hT = [sb(f"hT{q}", [P, KT, NBLK]) for q in range(2)]
        x1 = [sb(f"x1{q}", [NBLK, D]) for q in range(2)]
        xn2 = [sb(f"xn2{q}", [NBLK, D]) for q in range(2)]
        colsum = sb("colsum", [P, KT, NB])

        g_rows = G[0][0:ER, 0:TG, :]
        g_src, g_dst, g_dloc = src_w[0][0:ER, 0:TG], dst_w[0][0:ER, 0:TG], dloc[0:ER, 0:TG]
        g_onehot = onehot[0][0:ER, 0:TG, :]
        g_onehotT = onehot[1][:].rearrange("p t n -> p (t n)")[0:NBLK, 0:TG * ER].rearrange("p (t n) -> p t n", n=ER)
        g_other = G[2][:].rearrange("p t n -> p (t n)")[0:ER, 0:TG * NBLK].rearrange("p (t n) -> p t n", n=NBLK)
        g_best = G[1][:].rearrange("p t n -> p (t n)")[0:ER, 0:HEADS * NBLK].rearrange("p (h n) -> p h n", n=NBLK)
        g_alpha, g_logit_t = alpha[0:ER, 0:TG, :], logit[0:ER, 0:TG, :]
        g_sum, g_node = num, node_q[0]
        g_state = sb("g_state", [NBLK, 6, HEADS])

        mean = sb("mean", [P, KT])
        wr_sb = sb("wr_sb", [P, KT, NX])
        rt = sb("rt", [1, 16, NX])
        sel_i = sb("sel_i", [1, TOP_K], I32)
        wsel = sb("wsel", [1, TOP_K])
        wsel_b = sb("wsel_b", [P, TOP_K])
        def over(r, lo, parts, shape):
            size = 1
            for n in shape:
                size *= n
            flat = G[r][:].rearrange("p t n -> p (t n)")[0:parts, lo:lo + size]
            names = " ".join("abc"[:len(shape)])
            return flat.rearrange(f"p ({names}) -> p {names}", **dict(zip("abc", shape)))
        eW1 = over(1, 0, P, [TOP_K, KT, F])
        eb1 = sb("eb1", [P, TOP_K, FT])
        eW2 = over(1, TOP_K * KT * F, P, [TOP_K, FT, D])
        eb2 = sb("eb2", [1, TOP_K, D])
        eb2s = sb("eb2s", [1, D])
        fxT = [over(0, q * KT * CHUNK, P, [KT, CHUNK]) for q in range(2)]
        fx1 = [over(0, 2 * KT * CHUNK + q * GRP * D, NBLK, [GRP, D]) for q in range(2)]

        wait_here = sem("wait_here")
        dve_s, act_s = sem("dve_chain"), sem("act_chain")
        dve_agg_s, dve_general_s, dve_ffn_s, s_next, s_falls = (sem(n) for n in (
            "dve_agg_chain", "dve_general_chain", "dve_ffn_chain", "s_next", "s_falls"))
        s_const, s_in, s_in2, s_wT, s_wTc, s_att, s_watt, s_wext = (sem(n) for n in (
            "s_const", "s_in", "s_in2", "s_wT", "s_wTc", "s_att", "s_watt", "s_wext"))
        s_dst, s_dstf, s_pad, s_sampd, s_sampb, s_idx, s_swin, s_st, s_stT, s_starts = (sem(n) for n in (
            "s_dst", "s_dstf", "s_pad", "s_sampd", "s_sampb", "s_idx", "s_swin", "s_st", "s_stT", "s_starts"))
        x_ok = [sem(f"x_ok{q}") for q in range(2)]
        x_norm, xt_done, xt_copied, h_done, h_copied = (sem(n) for n in ("x_norm", "xt_done", "xt_copied", "h_done", "h_copied"))
        tab_st = [sem(f"tab_st{q}") for q in range(2)]
        L = []
        for l in range(2):
            d = {n: sem(f"{n}_l{l}") for n in (
                "onehot_done", "wide_ok", "hs_ok", "sum_ok", "onehot_ok", "st_done", "st_copied", "expand_done", "ends_ok", "rows_done",
                "carry_ok", "back_done", "logit_ok", "exp_ok", "prod_ok", "main_done", "acc_read", "sarg_ok", "sexp_ok",
                "feat_ok", "ft_done", "ft_copied", "hh_done", "hh_copied", "epi_done")}
            for n in ("src_ok", "dst_ok", "self_ok", "xres_ok", "stored", "stored2"):
                d[n] = [sem(f"{n}_l{l}_{q}") for q in range(2)]
            d["gathered"] = [sem(f"gathered_l{l}_{r}") for r in range(3)]
            L.append(d)
        (g_own0, g_own1, g_edges, g_gathered, g_onehot_ok, g_turned, g_turned_sb, g_best_ok, g_best_turned, g_arg, g_scale,
         g_spread, g_logit, g_exp, g_prod, g_acc, g_window, g_feat, g_ft, g_ft_sb, g_hh, g_out, g_stored, g_table) = (
            [L[0][n][0] for n in ("self_ok", "dst_ok", "src_ok", "gathered")]
            + [L[0][n] for n in ("onehot_done", "st_done", "st_copied", "ends_ok", "rows_done", "sarg_ok", "sexp_ok", "expand_done",
                                 "logit_ok", "exp_ok", "prod_ok", "main_done", "acc_read", "feat_ok", "ft_done", "ft_copied",
                                 "hh_done", "hh_copied")]
            + [L[0]["stored"][0], L[0]["stored"][1]])
        r_mean, r_logit, r_exp, r_sel, r_w, r_wb, r_load, r_ready, r_in, r_exp2, r_exp3, r_arg, r_arg2, r_arg3 = (sem(n) for n in (
            "r_mean", "r_logit", "r_exp", "r_sel", "r_w", "r_wb", "r_load", "r_ready", "r_in", "r_exp2", "r_exp3", "r_arg", "r_arg2", "r_arg3"))
        f_ok = [sem(f"f_ok{q}") for q in range(2)]
        f_st = [sem(f"f_st{q}") for q in range(2)]
        f_hid, f_gelu, f_out, f_read, f_done = (sem(n) for n in ("f_hid", "f_gelu", "f_out", "f_read", "f_done"))

        xrows = x.rearrange("(b p) d -> p b d", p=NBLK)
        outrows = out.rearrange("(b p) d -> p b d", p=NBLK)
        x1rows = x1_d.rearrange("(b p) d -> p b d", p=NBLK)
        xnrows = xn_d.rearrange("(b p) d -> p b d", p=NBLK)
        tabrows = [t.rearrange("(b p) d -> p b d", p=NBLK) for t in tables]
        SETUP_LOADS = 16 * (2 + 4 + 4 + 2)

        def rsqrt(ch, eps_var, n, r, ri):
            v, y, t = r[:, 1, 0:n], r[:, 0, 0:n], r[:, 2, 0:n]
            vec = nc.vector
            ch.link(vec.tensor_scalar(v, eps_var, LN_EPS, None, ALU.add))
            ch.link(vec.tensor_scalar(ri[:, 0, 0:n], v.bitcast(I32), 1, None, ALU.logical_shift_right))
            ch.link(vec.tensor_scalar(y.bitcast(I32), ri[:, 0, 0:n], -1.0, RSQRT_MAGIC, ALU.mult, ALU.add))
            for _ in range(3):
                ch.link(vec.tensor_tensor(t, y, y, ALU.mult))
                ch.link(vec.tensor_tensor(t, t, v, ALU.mult))
                ch.link(vec.tensor_scalar(t, t, -0.5, 1.5, ALU.mult, ALU.add))
                ch.link(vec.tensor_tensor(y, y, t, ALU.mult))

        block = ctx.enter_context(nc.Block())

        @block.sync
        def _(sp):
            ch = Chain(sp, None)
            with nc.allow_non_contiguous_dma(reason="attention vectors and samples, one element a row"):
                sp.dma_start(dst_i, dst.rearrange("(p k) -> p k", p=ER)).then_inc(s_dst, 16)
                sp.dma_start(wext[0][:, :, 0:D], W1.rearrange("(t p) n -> p t n", p=P)).then_inc(s_in, 16)
                sp.dma_start(wext[1][:, :, 0:D], W2.rearrange("(t p) n -> p t n", p=P)).then_inc(s_in, 16)
                for i, a in enumerate((as1, ad1, as2, ad2)):
                    sp.dma_start(att[:, i, :], a.rearrange("o (t h) c -> (o h c) t", t=KT)).then_inc(s_in, 16)
                for dst_t, v in ((bias[0], b1), (bias[1], b2), (gamma_b, gamma), (beta_b, beta)):
                    sp.dma_start(dst_t[:], v.partition_broadcast(NBLK)).then_inc(s_in, 16)
                sp.dma_start(wr_sb[:], Wr.rearrange("(t p) n -> p t n", p=P)).then_inc(s_in, 16)
                sp.dma_start(rt[:, 0, :], br.rearrange("(a n) -> a n", a=1)).then_inc(s_in, 16)
                for g in range(2):
                    sp.dma_start(xg[g][:], xrows[:, g * GRP:(g + 1) * GRP, :]).then_inc(x_ok[g], 16)
                sp.wait_ge(s_dstf, 1)
                sp.dma_start(dpad[bass.ds(1, E)].rearrange("(p k) -> p k", p=ER), dst_f).then_inc(s_pad, 16)
                sp.dma_start(dpad[0:1].rearrange("(a n) -> a n", a=1), sentinel[:, 0:1]).then_inc(s_pad, 16)
                sp.dma_start(dpad[bass.ds(E + 1, 1)].rearrange("(a n) -> a n", a=1), sentinel[:, 1:2]).then_inc(s_pad, 16)
                sp.dma_start(samples_d.rearrange("(p k) -> p k", p=ER), samp[:]).then_inc(s_sampd, 16)
                sp.wait_ge(s_sampd, 16)
                sp.dma_start(samp_b, samples_d.partition_broadcast(NB)).then_inc(s_sampb, 16)
                sp.wait_ge(s_pad, 48)
                sp.dma_start(next_f, dpad[bass.ds(2, E)].rearrange("(p k) -> p k", p=ER)).then_inc(s_next, 16)

            def table_group(g, half, q):
                sp.wait_ge(h_copied, g * GRP + GRP)
                sp.dma_start(tabrows[0][:, bass.ds(g * GRP, GRP), :], hout[q][:, :, 0:HW]).then_inc(tab_st[q], 16)
                if not isinstance(g, int) or g < NG - 2:
                    sp.wait_ge(x_norm, g + 1)
                    sp.dma_start(xg[q][:], xrows[:, bass.ds(g * GRP + 2 * GRP, GRP), :]).then_inc(x_ok[q], 16)
            ch.steps(NG, 2, 3, table_group)
            sp.wait_ge(tab_st[0], 16 * ((NG + 1) // 2))
            sp.wait_ge(tab_st[1], 16 * (NG // 2))
            sp.wait_ge(s_starts, 1)
            fit = sp.value_load(fits_i[0:1, 0:1], min_val=0, max_val=1)

            with sp.If(fit > 0):
                for l in range(2):
                    s = L[l]

                    def load_edges(b, q, s=s):
                        at = sp.value_load(starts_i[0:1, bass.ds(b, 1)], min_val=0, max_val=E - CAP)
                        sp.dma_start(src_w[q][:], src[bass.ds(at, CAP)].rearrange("(p k) -> p k", p=P)).then_inc(s["src_ok"][q], 16)
                        window = dpad[bass.ds(at, CAP)]
                        sp.dma_start(dst_w[q][:], bass.AP(window.tensor, window.offset, [[T, P], [1, T + 2]])).then_inc(s["dst_ok"][q], 16)

                    def load_nodes(b, q, s=s, l=l):
                        sp.dma_start(hself[q][:], tabrows[l][:, bass.ds(b, 1), :].rearrange("p b d -> p (b d)")).then_inc(s["self_ok"][q], 16)
                        if l == 1:
                            sp.dma_start(xres[q][:], xrows[:, bass.ds(b, 1), :].rearrange("p b d -> p (b d)")).then_inc(s["xres_ok"][q], 16)

                    for b in range(2):
                        load_edges(b, b)
                    for b in range(2):
                        load_nodes(b, b)

                    def store_block(b, q, s=s, l=l):
                        if l == 0:
                            sp.wait_ge(s["hh_copied"], b + 1)
                            sp.dma_start(tabrows[1][:, bass.ds(b, 1), :].rearrange("p b d -> p (b d)"),
                                         hout[q][:, 0, 0:HW]).then_inc(s["stored"][q], 16)
                        else:
                            sp.wait_ge(s["feat_ok"], b + 1)
                            sp.dma_start(x1rows[:, bass.ds(b, 1), :].rearrange("p b d -> p (b d)"), x1[q][:]).then_inc(s["stored"][q], 16)
                            sp.dma_start(xnrows[:, bass.ds(b, 1), :].rearrange("p b d -> p (b d)"), xn2[q][:]).then_inc(s["stored"][q], 16)
                            sp.wait_ge(s["ft_copied"], b + 1)
                            sp.dma_start(xT_d.rearrange("t p n -> p t n")[:, :, bass.ds(b * NBLK, NBLK)], hT[q][:]).then_inc(s["stored2"][q], 16)

                    def agg_block(b, half, q, third, r, s=s, l=l):
                        if not (isinstance(b, int) and b >= NB - 2):
                            sp.wait_ge(s["gathered"][r], (third + 1) * (16 * T))
                            sp.wait_ge(s["onehot_ok"], b + 1)
                            load_edges(b + 2, q)
                        if not (isinstance(b, int) and b == 0):
                            if not (isinstance(b, int) and b == NB - 1):
                                sp.wait_ge(s["epi_done"], b)
                                load_nodes(b + 1, 1 - q)
                            store_block(b - 1, 1 - q)
                    ch.steps(NB, 2, 2, agg_block, unroll=6)
                    store_block(NB - 1, (NB - 1) % 2)
                    for q in range(2):
                        sp.wait_ge(s["stored"][q], 16 * (l + 1) * (NB // 2))
                        if l == 1:
                            sp.wait_ge(s["stored2"][q], 16 * (NB // 2))
            with sp.Else():
                rows_w = src.rearrange("(p k) -> p k", p=ER)
                rows_d = dpad[bass.ds(1, E)].rearrange("(p k) -> p k", p=ER)
                for l in range(2):
                    with sp.Fori(0, NB) as b:
                        own = g_own0 if l == 0 else g_own1
                        sp.dma_start(hself[0][:], tabrows[l][:, bass.ds(b, 1), :].rearrange("p b d -> p (b d)")).then_inc(own, 16)
                        if l == 1:
                            sp.dma_start(xres[0][:], xrows[:, bass.ds(b, 1), :].rearrange("p b d -> p (b d)")).then_inc(own, 16)
                        with sp.Fori(0, NW) as w:
                            sp.wait_ge(g_window, b * NW + w + (l * NB * NW + 1))
                            with nc.allow_non_contiguous_dma(reason="a part of each row of the edge list"):
                                sp.dma_start(g_src, rows_w[:, bass.ds(w * TG, TG)]).then_inc(g_edges, 16)
                                sp.dma_start(g_dst, rows_d[:, bass.ds(w * TG, TG)]).then_inc(g_edges, 16)
                        sp.wait_ge(g_out, b + (l * NB + 1))
                        if l == 0:
                            sp.dma_start(tabrows[1][:, bass.ds(b, 1), :].rearrange("p b d -> p (b d)"), hout[0][:, 0, 0:HW]).then_inc(g_table, 16)
                            sp.wait_ge(g_table, b * 16 + 16)
                            sp.sem_inc(wait_here, 1)
                        else:
                            sp.dma_start(x1rows[:, bass.ds(b, 1), :].rearrange("p b d -> p (b d)"), x1[0][:]).then_inc(g_stored, 16)
                            sp.dma_start(xnrows[:, bass.ds(b, 1), :].rearrange("p b d -> p (b d)"), xn2[0][:]).then_inc(g_stored, 16)
                            sp.dma_start(xT_d.rearrange("t p n -> p t n")[:, :, bass.ds(b * NBLK, NBLK)], hT[0][:]).then_inc(g_stored, 16)
                            sp.wait_ge(g_stored, b * 48 + 48)
                            sp.sem_inc(wait_here, 1)

            sp.wait_ge(r_sel, 1)
            for k in range(TOP_K):
                e = sp.value_load(sel_i[0:1, k:k + 1], min_val=0, max_val=NX - 1)
                sp.dma_start(eW1[:, k, :, :], fW1[bass.ds(e, 1), :, :].rearrange("e (t p) f -> p (e t) f", p=P)).then_inc(r_load, 16)
                sp.dma_start(eW2[:, k, :, :], fW2[bass.ds(e, 1), :, :].rearrange("e (t p) n -> p (e t) n", p=P)).then_inc(r_load, 16)
                with nc.allow_non_contiguous_dma(reason="a bias by partition"):
                    sp.dma_start(eb1[:, k, :], fb1[bass.ds(e, 1), :].rearrange("e (t p) -> p (e t)", p=P)).then_inc(r_load, 16)
                sp.dma_start(eb2[:, k, :], fb2[bass.ds(e, 1), :]).then_inc(r_load, 16)

            def load_chunk(g, q):
                sp.dma_start(fxT[q][:], xT_d.rearrange("t p n -> p t n")[:, :, bass.ds(g * CHUNK, CHUNK)]).then_inc(f_ok[q], 16)
                sp.dma_start(xng[q][:], xnrows[:, bass.ds(g * GRP, GRP), :]).then_inc(f_ok[q], 16)
                sp.dma_start(fx1[q][:], x1rows[:, bass.ds(g * GRP, GRP), :]).then_inc(f_ok[q], 16)
            for g in range(2):
                load_chunk(g, g)

            def ffn_chunk(g, half, q):
                sp.wait_ge(f_done, g + 1)
                sp.dma_start(outrows[:, bass.ds(g * GRP, GRP), :], xg[q][:]).then_inc(f_st[q], 16)
                if not isinstance(g, int) or g < NG - 2:
                    sp.wait_ge(f_hid, g * (TOP_K * FT) + TOP_K * FT)
                    load_chunk(g + 2, q)
            ch.steps(NG, 2, 3, ffn_chunk)
            sp.wait_ge(f_st[0], 16 * ((NG + 1) // 2))
            sp.wait_ge(f_st[1], 16 * (NG // 2))

        @block.gpsimd
        def _(pool):
            ch = Chain(pool, None)
            nc.gpsimd.memset(ident[:], 0.0).then_inc(s_const, 1)
            nc.gpsimd.iota(node_iota[:], [[1, NBLK]], base=0, channel_multiplier=0, allow_small_or_imprecise_dtypes=True).then_inc(s_const, 1)
            nc.gpsimd.iota(block_base[:], [[NBLK, NB]], base=0, channel_multiplier=0, allow_small_or_imprecise_dtypes=True).then_inc(s_const, 1)
            nc.gpsimd.iota(first_node[:], [[0, 1]], base=0, channel_multiplier=NBLK, allow_small_or_imprecise_dtypes=True).then_inc(s_const, 1)
            nc.gpsimd.iota(rt[:, 1, :], [[1, NX]], base=0, channel_multiplier=0, allow_small_or_imprecise_dtypes=True).then_inc(s_const, 1)
            pool.wait_ge(s_const, 5)
            nc.gpsimd.affine_select(out=ident[:], in_=ident[:], compare_op=ALU.not_equal, fill=1.0, base=0,
                                    pattern=[[-1, P]], channel_multiplier=1).then_inc(s_const, 1)
            pool.wait_ge(s_idx, 1)
            pool.indirect_dma_start(out=swin[:], out_offset=None, in_=dst.rearrange("(n k) -> n k", k=SAMP),
                                    in_offset=bass.IndirectOffsetOnAxis(ap=st_i[:], axis=0),
                                    bounds_check=E // SAMP - 1, oob_is_err=False).then_inc(s_swin, 16)

            pool.wait_ge(s_starts, 1)
            fit = pool.value_load(fits_i[0:1, 0:1], min_val=0, max_val=1)
            with pool.If(fit > 0):
                for l in range(2):
                    s = L[l]
                    if l == 0:
                        pool.wait_ge(tab_st[0], 16 * ((NG + 1) // 2))
                        pool.wait_ge(tab_st[1], 16 * (NG // 2))
                    else:
                        for q in range(2):
                            pool.wait_ge(L[0]["stored"][q], 16 * (NB // 2))

                    def gather(b, half, q, third, r, s=s, l=l):
                        pool.wait_ge(s["src_ok"][q], half * 16 + 16)
                        if not isinstance(b, int) or b >= 3:
                            pool.wait_ge(s["main_done"], b - 2)
                        elif l == 1:
                            pool.wait_ge(L[0]["main_done"], NB)
                        pool.sem_inc(wait_here, 1)
                        for t in range(T):
                            pool.indirect_dma_start(out=G[r][:, t, 0:HW], out_offset=None, in_=tables[l],
                                                    in_offset=bass.IndirectOffsetOnAxis(ap=src_w[q][:, t:t + 1], axis=0),
                                                    bounds_check=N - 1, oob_is_err=False).then_inc(s["gathered"][r], 16)
                    ch.steps(NB, 3, 1, gather, unroll=6)
            with pool.Else():
                for l in range(2):
                    with pool.Fori(0, NB) as b:
                        with pool.Fori(0, NW) as w:
                            pool.wait_ge(g_edges, (b * NW + w) * 32 + (l * NB * NW * 32 + 32))
                            pool.sem_inc(wait_here, 1)
                            for t in range(TG):
                                pool.indirect_dma_start(out=G[0][0:ER, t, 0:HW], out_offset=None, in_=tables[l],
                                                        in_offset=bass.IndirectOffsetOnAxis(ap=src_w[0][0:ER, t:t + 1], axis=0),
                                                        bounds_check=N - 1, oob_is_err=False).then_inc(g_gathered, 16)

        @block.tensor
        def _(pe):
            ch = Chain(pe, None)
            pe.wait_ge(s_const, 6)
            pe.wait_ge(s_in, SETUP_LOADS)
            for l in range(2):
                if l == 1:
                    pe.wait_ge(s_wTc, 1)
                for i in range(KT):
                    for j in range(KT):
                        m = pe.transpose(p_xt[:, (j * KT + i) * P:(j * KT + i + 1) * P], wext[l][:, i, j * P:(j + 1) * P], ident[:])
                m.then_inc(s_wT, 1)
                pe.wait_ge(s_wTc, l + 1)
                pe.wait_ge(s_att, 1)
                for i in range(KT):
                    for j in range(KT):
                        m = pe.matmul(p_small[:, (l * KT + i) * 16:(l * KT + i) * 16 + 2 * HEADS], wT[:, j, i * P:(i + 1) * P], attm[:, l, j, :],
                                      start=(j == 0), stop=(j == KT - 1))
                m.then_inc(s_watt, 1)
            pe.wait_ge(s_wext, 2)
            xtb, hb = [p_xt, p_rows], [p_h, p_expand]

            def turn_x(g, j, q):
                c, k = g * GRP + j, j % 2
                if j == 0:
                    pe.wait_ge(x_norm, g + 1)
                if not (isinstance(c, int) and c < 2):
                    pe.wait_ge(xt_copied, c - 1)
                for t in range(KT):
                    m = pe.transpose(xtb[k][:, t * P:t * P + NBLK], xng[q][:, j, t * P:(t + 1) * P], ident[0:NBLK, 0:NBLK])
                m.then_inc(xt_done, 1)

            def table_group(g, half, q):
                for j in range(GRP):
                    c, k = g * GRP + j, j % 2
                    if j < GRP - 1:
                        turn_x(g, j + 1, q)
                    elif not (isinstance(g, int) and g == NG - 1):
                        turn_x(g + 1, 0, 1 - q)
                    pe.wait_ge(xt_copied, c + 1)
                    if not (isinstance(c, int) and c < 2):
                        pe.wait_ge(h_copied, c - 1)
                    for t in range(KT):
                        m = pe.matmul(hb[k][0:NBLK, 0:HWX], xT[k][:, t, :], wext[0][:, t, :], start=(t == 0), stop=(t == KT - 1))
                    m.then_inc(h_done, 1)
            turn_x(0, 0, 0)
            ch.steps(NG, 2, 3, table_group)
            pe.wait_ge(s_st, 1)
            pe.transpose(p_small[0:1, 128:128 + NB], st_f[:, 4:5], ident[0:NB, 0:NB])
            pe.transpose(p_small[0:1, 256:256 + NB], st_f[:, 3:4], ident[0:NB, 0:NB])
            pe.wait_ge(s_falls, 1)
            pe.transpose(p_small[0:1, 384:384 + ER], n_falls[:], ident[0:ER, 0:ER]).then_inc(s_stT, 1)
            pe.wait_ge(s_starts, 1)
            fit = pe.value_load(fits_i[0:1, 0:1], min_val=0, max_val=1)

            with pe.If(fit > 0):
                for l in range(2):
                    s = L[l]
                    pe.wait_ge(h_copied, NB)
                    if l == 1:
                        pe.wait_ge(L[0]["hh_copied"], NB)
                        pe.wait_ge(L[0]["epi_done"], NB)

                    def pre(b, q, s=s):
                        pe.wait_ge(s["onehot_done"], b + 1)
                        for gi in range(NGROUPS_ST):
                            n = b * NGROUPS_ST + gi
                            if not (isinstance(n, int) and n < 2):
                                pe.wait_ge(s["st_copied"], n - 1)
                            lo, hi = gi * STG, min(T, gi * STG + STG)
                            bankt = p_stb[(gi + q * (NGROUPS_ST % 2)) % 2]
                            for t in range(lo, hi):
                                m = pe.transpose(bankt[0:NBLK, (t - lo) * P:(t - lo + 1) * P], onehot_b[:, t, :], ident_b[:])
                            m.then_inc(s["st_done"], 1)
                        if not (isinstance(b, int) and b == 0):
                            pe.wait_ge(s["logit_ok"], b)
                        for gi in range(NGROUPS_ST):
                            pe.wait_ge(s["st_copied"], b * NGROUPS_ST + gi + 1)
                            for t in range(gi * STG, min(T, gi * STG + STG)):
                                for k in range(3):
                                    m = pe.matmul(p_expand[:, t * 8:t * 8 + 8], onehotT[:, t, :], parts_q[q][:, k, :], start=(k == 0), stop=(k == 2))
                        m.then_inc(s["expand_done"], 1)

                    def turn(b, q, s=s, l=l):
                        pe.wait_ge(s["feat_ok"], b + 1)
                        f = h1 if l == 0 else xn2[q]
                        if not (isinstance(b, int) and b == 0):
                            pe.wait_ge(s["ft_copied"], b)
                        for t in range(KT):
                            m = pe.transpose(p_xt[:, t * P:t * P + NBLK], f[:, t * P:(t + 1) * P], ident[0:NBLK, 0:NBLK])
                        m.then_inc(s["ft_done"], 1)

                    def project(b, q, s=s):
                        pe.wait_ge(s["ft_copied"], b + 1)
                        if not (isinstance(b, int) and b == 0):
                            pe.wait_ge(s["hh_copied"], b)
                        for t in range(KT):
                            m = pe.matmul(p_h[0:NBLK, 0:HWX], hT[q][:, t, :], wext[1][:, t, :], start=(t == 0), stop=(t == KT - 1))
                        m.then_inc(s["hh_done"], 1)

                    def agg_block(b, half, q, third, r, s=s, l=l):
                        pe.wait_ge(s["ends_ok"], b + 1)
                        for i, a in enumerate((rF[:, :, T], whole[q][:, 0, :], rB[:, :, 0], whole[q][:, 1, :])):
                            m = pe.transpose(p_rows[0:HEADS, i * P:(i + 1) * P], a, ident[:])
                        m.then_inc(s["rows_done"], 1)
                        pe.wait_ge(s["carry_ok"], b + 1)
                        pe.sem_inc(wait_here, 1)
                        pe.transpose(p_back[:, 0:HEADS], carF[:, 0:P], ident[0:HEADS, 0:HEADS])
                        pe.transpose(p_back[:, HEADS:2 * HEADS], carB[:, 1:P + 1], ident[0:HEADS, 0:HEADS]).then_inc(s["back_done"], 1)
                        if l == 0 and not (isinstance(b, int) and b == 0):
                            turn(b - 1, 1 - q)
                        if not (isinstance(b, int) and b < 2):
                            pe.wait_ge(s["acc_read"], b - 1)
                        pe.wait_ge(s["wide_ok"], b + 1)
                        for t in range(T):
                            if t % 2 == 0:
                                pe.wait_ge(s["prod_ok"], b * 9 + (t // 2 + 1))
                            m = pe.matmul(p_acc[q][0:NBLK, 0:GW], onehot[q][:, t, :], G[r][:, t, :], start=(t == 0), stop=(t == T - 1))
                        m.then_inc(s["main_done"], 1)
                        if l == 0 and not (isinstance(b, int) and b == 0):
                            project(b - 1, 1 - q)
                        if not (isinstance(b, int) and b == NB - 1):
                            pre(b + 1, 1 - q)
                        if l == 1 and not (isinstance(b, int) and b == 0):
                            turn(b - 1, 1 - q)
                    pre(0, 0)
                    ch.steps(NB, 3, 1, agg_block, unroll=6)
                    turn(NB - 1, (NB - 1) % 2)
                    if l == 0:
                        project(NB - 1, (NB - 1) % 2)
            with pe.Else():
                for l in range(2):
                    with pe.Fori(0, NB) as b:
                        with pe.Fori(0, NW) as w:
                            n = b * NW + w
                            pe.wait_ge(g_onehot_ok, n + (l * NB * NW + 1))
                            for i in range(NTURN):
                                if i >= 2:
                                    pe.wait_ge(g_turned_sb, n * NTURN + (l * NB * NW * NTURN + i - 1))
                                for t in range(i * TURN, min(TG, (i + 1) * TURN)):
                                    m = pe.transpose(p_st[i % 2][0:NBLK, (t % TURN) * P:(t % TURN) * P + ER], g_onehot[:, t, :], ident[0:ER, 0:ER])
                                m.then_inc(g_turned, 1)
                            pe.wait_ge(g_best_ok, n + (l * NB * NW + 1))
                            for h in range(HEADS):
                                m = pe.transpose(p_rows[0:NBLK, h * P:h * P + ER], g_best[:, h, :], ident[0:ER, 0:ER])
                            m.then_inc(g_best_turned, 1)
                            pe.wait_ge(g_arg, n + (l * NB * NW + 1))
                            pe.wait_ge(g_turned_sb, n * NTURN + (l * NB * NW + 1) * NTURN)
                            for t in range(TG):
                                m = pe.matmul(p_expand[0:ER, t * 8:t * 8 + 8], g_onehotT[:, t, :], g_node[:], start=True, stop=True)
                            m.then_inc(g_spread, 1)
                            pe.wait_ge(g_prod, n + (l * NB * NW + 1))
                            for t in range(TG):
                                m = pe.matmul(p_acc[0][0:NBLK, 0:HW], g_onehot[:, t, :], g_rows[:, t, 0:HW], start=(t == 0), stop=(t == TG - 1))
                            m.then_inc(g_acc, 1)
                        pe.wait_ge(g_feat, b + (l * NB + 1))
                        f = h1 if l == 0 else xn2[0]
                        for t in range(KT):
                            m = pe.transpose(p_xt[:, t * P:t * P + NBLK], f[:, t * P:(t + 1) * P], ident[0:NBLK, 0:NBLK])
                        m.then_inc(g_ft, 1)
                        if l == 0:
                            pe.wait_ge(g_ft_sb, b + 1)
                            for t in range(KT):
                                m = pe.matmul(p_h[0:NBLK, 0:HWX], hT[0][:, t, :], wext[1][:, t, :], start=(t == 0), stop=(t == KT - 1))
                            m.then_inc(g_hh, 1)

            pe.wait_ge(r_mean, 1)
            for t in range(KT):
                m = pe.matmul(p_small[0:1, 0:NX], mean[:, t:t + 1], wr_sb[:, t, :], start=(t == 0), stop=(t == KT - 1))
            m.then_inc(r_logit, 1)
            pe.wait_ge(r_w, 1)
            pe.matmul(p_small[:, 16:16 + TOP_K], ones[:, :], wsel[:, :], start=True, stop=True).then_inc(r_wb, 1)

            pe.wait_ge(r_ready, 1)
            hbank = [p_st[0], p_st[1], p_expand, p_rows]
            obank = [p_acc[0], p_xt, p_h, p_acc[1]]

            def ffn_chunk(g, half, q):
                pe.wait_ge(f_ok[q], half * 48 + 48)
                for n in range(TOP_K * FT):
                    c = g * (TOP_K * FT) + n
                    if not (isinstance(c, int) and c < 4):
                        pe.wait_ge(f_gelu, c - 3)
                    for t in range(KT):
                        m = pe.matmul(hbank[n % 4][:, 0:CHUNK], eW1[:, n // FT, t, (n % FT) * P:(n % FT + 1) * P], fxT[q][:, t, :],
                                      start=(t == 0), stop=(t == KT - 1))
                    m.then_inc(f_hid, 1)
                pe.wait_ge(f_gelu, g * (TOP_K * FT) + TOP_K * FT)
                for j in range(GRP):
                    if not (isinstance(g, int) and g == 0):
                        pe.wait_ge(f_read, g * GRP + (j + 1 - GRP))
                    pe.matmul(obank[j][0:NBLK, 0:D], ones[:, 0:NBLK], eb2s[:, :], start=True, stop=False)
                    for n in range(TOP_K * FT):
                        m = pe.matmul(obank[j][0:NBLK, 0:D], hid[q][:, n, j * NBLK:(j + 1) * NBLK], eW2[:, n // FT, n % FT, :],
                                      start=False, stop=(n == TOP_K * FT - 1))
                    m.then_inc(f_out, 1)
            ch.steps(NG, 2, 3, ffn_chunk)

        @block.scalar
        def _(act):
            ch = Chain(act, act_s)
            for l in range(2):
                act.wait_ge(s_wT, l + 1)
                if l == 1:
                    act.wait_ge(s_watt, 1)
                nc.scalar.copy(wT[:].rearrange("p t n -> p (t n)"), p_xt[:, 0:KT * D]).then_inc(s_wTc, 1)
                act.wait_ge(s_watt, l + 1)
                for i in range(KT):
                    m = nc.scalar.copy(wext[l][:, i, D:HWX], p_small[:, (l * KT + i) * 16:(l * KT + i) * 16 + 2 * HEADS])
                    if i == KT - 1:
                        m.then_inc(s_wext, 1)
            act.wait_ge(s_wext, 2)
            xtb, hb = [p_xt, p_rows], [p_h, p_expand]

            def copy_x(c, k):
                act.wait_ge(xt_done, c + 1)
                if not (isinstance(c, int) and c < 2):
                    act.wait_ge(h_done, c - 1)
                nc.scalar.copy(xT[k][:], xtb[k][:, 0:KT * P].rearrange("p (t n) -> p t n", t=KT)[:, :, 0:NBLK]).then_inc(xt_copied, 1)

            def table_group(g, half, q):
                for j in range(GRP):
                    c, k = g * GRP + j, j % 2
                    if not (isinstance(c, int) and c == NB - 1):
                        copy_x(c + 1, 1 - k)
                    act.wait_ge(h_done, c + 1)
                    if j == 0 and not (isinstance(g, int) and g < 2):
                        act.wait_ge(tab_st[q], half * 16)
                    nc.scalar.copy(node[0][:, bass.ds(c, 1), :].rearrange("p b n -> p (b n)"), hb[k][0:NBLK, D:HWX])
                    nc.scalar.copy(hout[q][:, j, :], hb[k][0:NBLK, 0:HWX]).then_inc(h_copied, 1)
            copy_x(0, 0)
            ch.steps(NG, 2, 3, table_group)

            act.wait_ge(s_starts, 1)
            fit = act.value_load(fits_i[0:1, 0:1], min_val=0, max_val=1)
            with act.If(fit > 0):
                for l in range(2):
                    s = L[l]

                    def pre(b, q, s=s, l=l):
                        act.wait_ge(s["onehot_done"], b + 1)
                        if not (isinstance(b, int) and b < 2):
                            act.wait_ge(s["main_done"], b - 1)
                        elif l == 1:
                            act.wait_ge(L[0]["main_done"], NB)
                        for gi in range(NGROUPS_ST):
                            act.wait_ge(s["st_done"], b * NGROUPS_ST + gi + 1)
                            if gi == 0 and not (isinstance(b, int) and b == 0):
                                act.wait_ge(s["expand_done"], b)
                            lo, hi = gi * STG, min(T, gi * STG + STG)
                            nc.scalar.copy(onehotT[:, lo:hi, :], p_stb[(gi + q * (NGROUPS_ST % 2)) % 2][0:NBLK, 0:(hi - lo) * P].rearrange("p (t n) -> p t n", n=P)).then_inc(s["st_copied"], 1)

                    def widen(b, q, s=s):
                        nc.scalar.copy(onehot[q][:], onehot_b[:]).then_inc(s["wide_ok"], 1)

                    def relu(b, s=s):
                        act.wait_ge(s["sum_ok"], b + 1)
                        if not (isinstance(b, int) and b == 0):
                            act.wait_ge(s["ft_done"], b)
                        nc.scalar.activation(h1[:], num[:], ACT.Relu).then_inc(s["feat_ok"], 1)

                    def features(b, half, q, s=s, l=l):
                        act.wait_ge(s["ft_done"], b + 1)
                        if not (isinstance(b, int) and b < 2):
                            if l == 0:
                                act.wait_ge(s["hh_done"], b - 1)
                            else:
                                act.wait_ge(s["stored2"][q], half * 16)
                        elif l == 1:
                            act.wait_ge(L[0]["hh_done"], NB)
                        if l == 0:
                            nc.scalar.copy(hT[q][:], p_xt[:, 0:KT * P].rearrange("p (t n) -> p t n", t=KT)[:, :, 0:NBLK]).then_inc(s["ft_copied"], 1)
                        else:
                            for t in range(KT):
                                m = nc.scalar.activation(hT[q][:, t, :], p_xt[:, t * P:t * P + NBLK], ACT.Copy,
                                                         accum_out=colsum[:, t, bass.ds(b, 1)])
                            m.then_inc(s["ft_copied"], 1)

                    def projected(b, half, q, s=s):
                        act.wait_ge(s["hh_done"], b + 1)
                        if not (isinstance(b, int) and b < 2):
                            act.wait_ge(s["stored"][q], half * 16)
                        elif isinstance(b, int) and b == 0:
                            act.wait_ge(tab_st[0], 16 * ((NG + 1) // 2))
                            act.wait_ge(tab_st[1], 16 * (NG // 2))
                        nc.scalar.copy(node[1][:, bass.ds(b, 1), :].rearrange("p b n -> p (b n)"), p_h[0:NBLK, D:HWX])
                        nc.scalar.copy(hout[q][:, 0, :], p_h[0:NBLK, 0:HWX]).then_inc(s["hh_copied"], 1)

                    def own_exp(b, half, q, s=s):
                        act.wait_ge(s["sarg_ok"], b + 1)
                        ch.link(nc.scalar.activation(self_s[:, 3, :], self_s[:, 2, :], ACT.Exp))
                        act.sem_inc(s["sexp_ok"], 1)
                        act.wait_ge(s["self_ok"][q], half * 16 + 16)
                        for h in range(HEADS):
                            m = nc.scalar.activation(hs[:, h * C:(h + 1) * C], hself[q][:, h * C:(h + 1) * C], ACT.Copy, scale=self_s[:, 3, h:h + 1])
                        m.then_inc(s["hs_ok"], 1)

                    def agg_block(b, half, q, third, r, s=s, l=l):
                        later = not (isinstance(b, int) and b == 0)
                        before = (half - 1 + q, 1 - q)
                        if later:
                            own_exp(b - 1, *before)
                        act.wait_ge(s["logit_ok"], b + 1)
                        nc.scalar.activation(G[r][:, :, D:HW], logit[:], ACT.Exp).then_inc(s["exp_ok"], 1)
                        if l == 0 and later:
                            relu(b - 1)
                            features(b - 1, *before)
                            projected(b - 1, *before)
                        if not (isinstance(b, int) and b == NB - 1):
                            pre(b + 1, 1 - q)
                        if l == 1 and later:
                            features(b - 1, *before)
                        if not (isinstance(b, int) and b == NB - 1):
                            widen(b + 1, 1 - q)
                    pre(0, 0)
                    widen(0, 0)
                    ch.steps(NB, 3, 1, agg_block, unroll=6)
                    final = (NB - 1, (NB - 1) // 2, (NB - 1) % 2)
                    own_exp(*final)
                    if l == 0:
                        relu(NB - 1)
                    features(*final)
                    if l == 0:
                        projected(*final)
            with act.Else():
                for l in range(2):
                    with act.Fori(0, NB) as b:
                        with act.Fori(0, NW) as w:
                            n = b * NW + w
                            for i in range(NTURN):
                                act.wait_ge(g_turned, n * NTURN + (l * NB * NW * NTURN + i + 1))
                                t0, t1 = i * TURN, min(TG, (i + 1) * TURN)
                                nc.scalar.copy(g_onehotT[:, t0:t1, :], p_st[i % 2][0:NBLK, 0:(t1 - t0) * P].rearrange("p (t n) -> p t n", n=P)[:, :, 0:ER]).then_inc(g_turned_sb, 1)
                            act.wait_ge(g_arg, n + (l * NB * NW + 1))
                            nc.scalar.activation(g_state[:, 4, :], g_state[:, 3, :], ACT.Exp).then_inc(g_scale, 1)
                            act.wait_ge(g_logit, n + (l * NB * NW + 1))
                            nc.scalar.activation(g_rows[:, :, D:HW], g_logit_t, ACT.Exp).then_inc(g_exp, 1)
                        act.wait_ge(g_ft, b + (l * NB + 1))
                        if l == 0:
                            nc.scalar.copy(hT[0][:], p_xt[:, 0:KT * P].rearrange("p (t n) -> p t n", t=KT)[:, :, 0:NBLK]).then_inc(g_ft_sb, 1)
                            act.wait_ge(g_hh, b + 1)
                            nc.scalar.copy(node[1][:, bass.ds(b, 1), :].rearrange("p b n -> p (b n)"), p_h[0:NBLK, D:HWX])
                            nc.scalar.copy(hout[0][:, 0, :], p_h[0:NBLK, 0:HWX]).then_inc(g_out, 1)
                        else:
                            for t in range(KT):
                                m = nc.scalar.activation(hT[0][:, t, :], p_xt[:, t * P:t * P + NBLK], ACT.Copy, accum_out=colsum[:, t, bass.ds(b, 1)])
                            m.then_inc(g_out, 1)

            for arg, done in ((r_arg, r_exp), (r_arg2, r_exp2), (r_arg3, r_exp3)):
                act.wait_ge(arg, 1)
                nc.scalar.activation(rt[:, 4, :], rt[:, 3, :], ACT.Exp).then_inc(done, 1)
            act.wait_ge(r_ready, 1)
            hbank = [p_st[0], p_st[1], p_expand, p_rows]

            def ffn_chunk(g, half, q):
                for n in range(TOP_K * FT):
                    c = g * (TOP_K * FT) + n
                    act.wait_ge(f_hid, c + 1)
                    if n == 0 and not (isinstance(g, int) and g < 2):
                        act.wait_ge(f_out, g * GRP - GRP)
                    nc.scalar.activation(hid[q][:, n, :], hbank[n % 4][:, 0:CHUNK], ACT.Gelu,
                                         bias=eb1[:, n // FT, n % FT:n % FT + 1]).then_inc(f_gelu, 1)
            ch.steps(NG, 2, 3, ffn_chunk)

        @block.vector
        def _(dve):
            vec = nc.vector
            ch = Chain(dve, dve_s)
            link = ch.link
            link(vec.memset(sentinel[:, 0:1], -1.0))
            link(vec.memset(sentinel[:, 1:2], -2.0))
            dve.wait_ge(s_dst, 16)
            link(vec.tensor_copy(dst_f, dst_i))
            vec.tensor_copy(samp[:], dst_f.rearrange("p (n k) -> p n k", k=SAMP)[:, :, 0]).then_inc(s_dstf, 1)
            link(vec.memset(ones[:], 1.0))
            link(vec.memset(attm[:].rearrange("p l t h -> p (l t h)"), 0.0))
            dve.wait_ge(s_in, SETUP_LOADS)
            for i in range(4):
                for h in range(HEADS):
                    p0, t = (h % 2) * C, h // 2
                    m = vec.tensor_copy(attm[p0:p0 + C, i // 2, t, (i % 2) * HEADS + h:(i % 2) * HEADS + h + 1], att[p0:p0 + C, i, t:t + 1])
            m.then_inc(s_att, 1)
            dve.wait_ge(s_const, 6)
            link(vec.tensor_copy(ident_b[:], ident[:]))
            dve.wait_ge(s_sampb, 16)
            link(vec.tensor_scalar(samp_lt, samp_b, first_node[:, 0:1], None, ALU.is_lt))
            link(vec.tensor_reduce(st_f[:, 0:1], samp_lt, AX.X, ALU.add))
            link(vec.tensor_scalar(st_f[:, 1:2], st_f[:, 0:1], -1.0, 0.0, ALU.add, ALU.max))
            vec.tensor_copy(st_i[:], st_f[:, 1:2]).then_inc(s_idx, 1)
            dve.wait_ge(s_swin, 16)
            link(vec.tensor_scalar(swin_lt[:], swin[:], first_node[:, 0:1], None, ALU.is_lt))
            link(vec.tensor_reduce(st_f[:, 2:3], swin_lt[:], AX.X, ALU.add))
            link(vec.tensor_scalar(st_f[:, 3:4], st_f[:, 1:2], float(SAMP), st_f[:, 2:3], ALU.mult, ALU.add))
            vec.tensor_scalar(st_f[:, 4:5], st_f[:, 3:4], float(E - CAP), None, ALU.min).then_inc(s_st, 1)
            dve.wait_ge(s_next, 16)
            link(vec.tensor_tensor(falls, dst_f, next_f, ALU.is_gt))
            vec.tensor_reduce(n_falls[:], falls, AX.X, ALU.add).then_inc(s_falls, 1)

            def table_group(g, half, q):
                dve.wait_ge(x_ok[q], half * 16 + 16)
                for j in range(GRP):
                    link(vec.bn_stats(stats[:, j, :], xg[q][:, j, :]))
                    dve.sem_inc(wait_here, 1)
                    link(vec.bn_aggr(mv[:, j, :], stats[:, j, :]))
                rsqrt(ch, mv[:, :, 1], GRP, rs, rs_i)
                if not (isinstance(g, int) and g < 2):
                    dve.wait_ge(xt_done, g * GRP - GRP)
                for j in range(GRP):
                    m = vec.tensor_scalar(xng[q][:, j, :], xg[q][:, j, :], mv[:, j, 0:1], rs[:, 0, j:j + 1], ALU.subtract, ALU.mult)
                m.then_inc(x_norm, 1)
            ch.steps(NG, 2, 3, table_group)
            dve.wait_ge(s_stT, 1)
            link(vec.tensor_copy(starts_i[:], p_small[0:1, 128:128 + NB]))
            vec.memset(starts_row[:, NB:NB + 1], float(E))
            vec.tensor_reduce(fits[:, 0:1], p_small[0:1, 384:384 + ER], AX.X, ALU.add)
            link(vec.tensor_copy(starts_row[:, 0:NB], p_small[0:1, 256:256 + NB]))
            link(vec.tensor_tensor(starts_row[:, 0:NB], starts_row[:, 1:NB + 1], starts_row[:, 0:NB], ALU.subtract))
            link(vec.tensor_reduce(fits[:, 1:2], starts_row[:, 0:NB], AX.X, ALU.max))
            link(vec.tensor_scalar(fits[:, 2:3], fits[:, 0:1], 1.0, None, ALU.is_equal))
            link(vec.tensor_scalar(fits[:, 3:4], fits[:, 1:2], float(CAP), None, ALU.is_le))
            vec.tensor_tensor(fits_i[:], fits[:, 2:3], fits[:, 3:4], ALU.mult).then_inc(s_starts, 1)

            for t_, col in ((vF, 0), (vB, T)):
                link(vec.memset(t_[:, :, col], -BIG))
            for q in range(2):
                link(vec.memset(penF[q][:, :, 0], -BIG))
                link(vec.memset(penB[q][:, :, T], -BIG))
            link(vec.memset(carF[:, 0:1], -BIG))
            link(vec.memset(carB[:, P:P + 1], -BIG))
            link(vec.tensor_copy(node_iota_b[:], node_iota[:]))
            dve.wait_ge(s_starts, 1)
            fit = dve.value_load(fits_i[0:1, 0:1], min_val=0, max_val=1)

            def by_head(h):
                return slice(h * C, (h + 1) * C)

            def norm_step(i, q):
                v, y, t = rs[:, 1, 0:1], rs[:, 0, 0:1], rs[:, 2, 0:1]
                if i == 0:
                    link(vec.bn_stats(stats[:, 0, :], x1[q][:]))
                    dve.sem_inc(wait_here, 1)
                    return ch.do(vec.bn_aggr(mv[:, 0, :], stats[:, 0, :]))
                if i == 1:
                    return ch.do(vec.tensor_scalar(v, mv[:, 0, 1:2], LN_EPS, None, ALU.add))
                if i == 2:
                    link(vec.tensor_scalar(rs_i[:, 0, 0:1], v.bitcast(I32), 1, None, ALU.logical_shift_right))
                    return ch.do(vec.tensor_scalar(y.bitcast(I32), rs_i[:, 0, 0:1], -1.0, RSQRT_MAGIC, ALU.mult, ALU.add))
                if i in (3, 5, 7):
                    return ch.do(vec.tensor_scalar(t, y, y, v, ALU.mult, ALU.mult))
                link(vec.tensor_scalar(t, t, -0.5, 1.5, ALU.mult, ALU.add))
                return ch.do(vec.tensor_scalar(y, y, t, None, ALU.mult))

            with dve.If(fit > 0):
                ch = Chain(dve, dve_agg_s)
                link = ch.link
                for l in range(2):
                    s = L[l]
                    if l == 0:
                        dve.wait_ge(h_copied, NB)
                    else:
                        dve.wait_ge(L[0]["hh_copied"], NB)
                        dve.wait_ge(L[0]["expand_done"], NB)

                    link(vec.tensor_copy(node_parts[:, :, 0, :], node[l][:]))
                    link(vec.tensor_tensor(node_rest[:], node[l][:], node_parts[:, :, 0, :], ALU.subtract))
                    link(vec.tensor_copy(node_parts[:, :, 1, :], node_rest[:]))
                    link(vec.tensor_tensor(node_rest[:], node_rest[:], node_parts[:, :, 1, :], ALU.subtract))
                    link(vec.tensor_copy(node_parts[:, :, 2, :], node_rest[:]))

                    def pre(b, half, q, s=s, l=l):
                        dve.wait_ge(s["dst_ok"][q], half * 16 + 16)
                        d = dst_w[q]
                        c = ch.do(vec.tensor_scalar(dloc[:], d[:, 1:T + 1], block_base[:, bass.ds(b, 1)], None, ALU.subtract))
                        c1 = ch.do(vec.tensor_tensor(link_w[:], d[:, 0:T + 1], d[:, 1:T + 2], ALU.is_equal))
                        vec.tensor_copy(node_q[q][:], node[l][:, bass.ds(b, 1), :].rearrange("p b n -> p (b n)"))
                        vec.tensor_copy(parts_q[q][:], node_parts[:, bass.ds(b, 1), :, :].rearrange("p b k n -> p (b k) n"))
                        if not (isinstance(b, int) and b == 0):
                            dve.wait_ge(s["wide_ok"], b)
                            dve.wait_ge(s["st_done"], b * NGROUPS_ST)
                        ch.after(c)
                        for t in range(T):
                            m = vec.tensor_scalar(onehot_b[:, t, :], node_iota_b[:, :], dloc[:, t:t + 1], None, ALU.is_equal)
                        m.then_inc(s["onehot_done"], 1)
                        vec.tensor_tensor(whole[q][:, 0, :], d[:, 0:1].to_broadcast([P, HEADS]), d[:, T:T + 1].to_broadcast([P, HEADS]), ALU.is_equal)
                        c2 = ch.do(vec.tensor_tensor(whole[q][:, 1, :], d[:, 1:2].to_broadcast([P, HEADS]), d[:, T + 1:T + 2].to_broadcast([P, HEADS]), ALU.is_equal))
                        ch.after(c1)
                        c3 = ch.do(vec.tensor_scalar(pen[:], link_w[:], -1.0, BIG, ALU.add, ALU.mult))
                        vec.tensor_scalar(run_end[q][:], link_w[:, 1:T + 1], -1.0, 1.0, ALU.mult, ALU.add)
                        ch.after(c2)
                        vec.tensor_scalar(whole[q][:], whole[q][:], -1.0, BIG, ALU.add, ALU.mult)
                        ch.after(c3)
                        vec.tensor_copy(penF[q][:, :, 1:T + 1], pen[:, 0:T].unsqueeze(1).to_broadcast([P, HEADS, T]))
                        link(vec.tensor_copy(penB[q][:, :, 0:T], pen[:, 1:T + 1].unsqueeze(1).to_broadcast([P, HEADS, T])))
                        dve.sem_inc(s["onehot_ok"], 1)

                    def own_loop(b, q, s=s):
                        dve.wait_ge(s["main_done"], b + 1)
                        nq = node_q[q]
                        acc = p_acc[q][0:NBLK, :]
                        own, top, arg = (self_s[:, i, :] for i in (0, 1, 2))
                        link(vec.tensor_tensor(own, nq[:, 0:HEADS], nq[:, HEADS:2 * HEADS], ALU.add))
                        link(vec.tensor_scalar(self_s[:, 5, 0:1], acc[:, GW - 1:GW], -1.0, BIG, ALU.add, ALU.mult))
                        link(vec.scalar_tensor_tensor(own, own, SLOPE, own, ALU.mult, ALU.max))
                        link(vec.tensor_scalar(top, acc[:, HW:HW + HEADS], self_s[:, 5, 0:1], None, ALU.add))
                        link(vec.tensor_tensor(top, top, own, ALU.max))
                        link(vec.tensor_tensor(arg, own, top, ALU.subtract))
                        dve.sem_inc(s["sarg_ok"], 1)

                    def quotient(b, half, q, s=s, l=l):
                        acc = p_acc[q][0:NBLK, :]
                        es, den = self_s[:, 3, :], self_s[:, 4, :]
                        dve.wait_ge(s["sexp_ok"], b + 1)
                        c = ch.do(vec.tensor_tensor(den, acc[:, D:HW], es, ALU.add))
                        if l == 0 and not (isinstance(b, int) and b == 0):
                            dve.wait_ge(s["feat_ok"], b)
                        ch.after(c)
                        c = ch.do(vec.tensor_scalar(den, den, 1e-16, None, ALU.max))
                        dve.wait_ge(s["hs_ok"], b + 1)
                        c1 = ch.do(vec.tensor_tensor(num[:], hs[:], acc[:, 0:D], ALU.add))
                        ch.after(c)
                        c = ch.do(vec.reciprocal(den, den))
                        if l == 1:
                            dve.wait_ge(s["xres_ok"][q], half * 16 + 16)
                            c2 = ch.do(vec.tensor_tensor(xres[q][:], xres[q][:], bias[1][:], ALU.add))
                            if not (isinstance(b, int) and b < 2):
                                dve.wait_ge(s["stored"][q], half * 32)
                                dve.wait_ge(s["ft_done"], b - 1)
                            ch.after(c2)
                        ch.after(c1)
                        dve.sem_inc(s["acc_read"], 1)
                        ch.after(c)
                        more, res = (bias[0], num) if l == 0 else (xres[q], x1[q])
                        for h in range(HEADS):
                            hc = slice(h * C, (h + 1) * C)
                            m = vec.scalar_tensor_tensor(res[:, hc], num[:, hc], self_s[:, 4, h:h + 1], more[:, hc], ALU.mult, ALU.add)
                        if l == 0:
                            m.then_inc(s["sum_ok"], 1)
                        else:
                            link(m)
                        dve.sem_inc(s["epi_done"], 1)

                    def norm_apply(b, q, s=s):
                        vec.tensor_scalar(xn2[q][:], x1[q][:], mv[:, 0, 0:1], rs[:, 0, 0:1], ALU.subtract, ALU.mult).then_inc(s["feat_ok"], 1)

                    def agg_block(b, half, q, third, r, s=s, l=l):
                        g = G[r]
                        later = not (isinstance(b, int) and b == 0)
                        dve.wait_ge(s["gathered"][r], (third + 1) * (16 * T))
                        a_src = g[:, :, D:HW].rearrange("p t h -> p h t")
                        vec.tensor_copy(vF[:, :, 1:T + 1], a_src)
                        link(vec.tensor_copy(vB[:, :, 0:T], a_src))

                        def flat(a):
                            return a[:].rearrange("p h t -> p (h t)")

                        def scans():
                            vec.tensor_tensor_scan(flat(rF), flat(penF[q]), flat(vF), -BIG, ALU.add, ALU.max)
                            return ch.do(vec.tensor_tensor_scan(flat(rB)[:, ::-1], flat(penB[q])[:, ::-1], flat(vB)[:, ::-1], -BIG, ALU.add, ALU.max))
                        ch.after(scans())
                        dve.sem_inc(s["ends_ok"], 1)
                        if later:
                            own_loop(b - 1, 1 - q)
                        dve.wait_ge(s["rows_done"], b + 1)
                        rows = p_rows[0:HEADS, :].rearrange("h (i p) -> h i p", p=P)
                        vec.tensor_copy(row_pen[:, 0, :], rows[:, 1, :])
                        link(vec.tensor_copy(row_pen[:, 1, :], rows[:, 3, :]))
                        vec.tensor_tensor_scan(carF[:, 1:P + 1], row_pen[:, 0, :], rows[:, 0, :], -BIG, ALU.add, ALU.max)
                        link(vec.tensor_tensor_scan(carB[:, 0:P][:, ::-1], row_pen[:, 1, :][:, ::-1], rows[:, 2, :][:, ::-1], -BIG, ALU.add, ALU.max))
                        dve.sem_inc(s["carry_ok"], 1)
                        dve.wait_ge(s["expand_done"], b + 1)
                        spread = p_expand[:, 0:T * 8].rearrange("p (t n) -> p t n", n=8)
                        a_self, a_dst = spread[:, :, 0:HEADS], spread[:, :, HEADS:2 * HEADS]
                        link(vec.tensor_tensor(alpha[:], g[:, :, D:HW], a_dst, ALU.add))
                        ca = ch.do(vec.scalar_tensor_tensor(alpha[:], alpha[:], SLOPE, alpha[:], ALU.mult, ALU.max))
                        dve.wait_ge(s["back_done"], b + 1)
                        vec.tensor_copy(vF[:, :, 0], p_back[:, 0:HEADS])
                        link(vec.tensor_copy(vB[:, :, T], p_back[:, HEADS:2 * HEADS]))
                        ch.after(scans())
                        vec.memset(vF[:, :, 0], -BIG)
                        vec.memset(vB[:, :, T], -BIG)
                        link(vec.tensor_tensor(runmax[:], rF[:, :, 1:T + 1].rearrange("p h t -> p t h"), rB[:, :, 0:T].rearrange("p h t -> p t h"), ALU.max))
                        link(vec.tensor_tensor(runmax[:], runmax[:], a_self, ALU.max))
                        link(vec.tensor_tensor(runmax[:], runmax[:], a_dst, ALU.add))
                        ch.after(ca)
                        link(vec.scalar_tensor_tensor(runmax[:], runmax[:], SLOPE, runmax[:], ALU.mult, ALU.max))
                        link(vec.tensor_tensor(alpha[:], alpha[:], runmax[:], ALU.subtract))
                        link(vec.tensor_scalar(logit[:], alpha[:], 0.0, None, ALU.min))
                        dve.sem_inc(s["logit_ok"], 1)
                        vec.tensor_tensor(g[:, :, HW:HW + HEADS], runmax[:], run_end[q][:].unsqueeze(2).to_broadcast([P, T, HEADS]), ALU.mult)
                        vec.tensor_copy(g[:, :, HW + HEADS], run_end[q][:])
                        if later:
                            quotient(b - 1, half - 1 + q, 1 - q)
                        dve.wait_ge(s["exp_ok"], b + 1)
                        count = 0
                        for i in range(9):
                            t0, t1 = i * 2, i * 2 + 2
                            hv = g[:, t0:t1, 0:D].rearrange("p t (h c) -> p t h c", h=HEADS)
                            vec.tensor_tensor(hv, hv, g[:, t0:t1, D:HW].unsqueeze(3).to_broadcast([P, 2, HEADS, C]), ALU.mult).then_inc(s["prod_ok"], 1)
                            if l == 1 and later:
                                if count:
                                    ch.after(count)
                                count = norm_step(i, 1 - q)
                        if not (isinstance(b, int) and b == NB - 1):
                            pre(b + 1, half + q, 1 - q)
                        if l == 1 and later:
                            ch.after(count)
                            norm_apply(b - 1, 1 - q)

                    pre(0, 0, 0)
                    ch.steps(NB, 3, 1, agg_block, unroll=6)
                    own_loop(NB - 1, (NB - 1) % 2)
                    quotient(NB - 1, (NB - 1) // 2, (NB - 1) % 2)
                    if l == 1:
                        for i in range(9):
                            ch.after(norm_step(i, (NB - 1) % 2))
                        norm_apply(NB - 1, (NB - 1) % 2)
                dve.wait_ge(L[1]["ft_copied"], NB)
            with dve.Else():
                ch = Chain(dve, dve_general_s)
                link = ch.link
                top, new, a_dst_n, arg, shrink, den = (g_state[:, i, :] for i in range(6))
                BEFORE, WINDOW, AFTER = 8, TG + 15, (4, 18)
                dve.sem_inc(g_window, 1)
                for l in range(2):
                    block_links = BEFORE + NW * WINDOW + AFTER[l]
                    start = l * NB * (BEFORE + NW * WINDOW + AFTER[0])
                    with dve.Fori(0, NB) as b:
                        ch.base, ch.n = b * block_links + start, 0
                        dve.wait_ge(g_own0 if l == 0 else g_own1, b * (16 * (l + 1)) + 16 * (l + 1))
                        nb = node[l][:, bass.ds(b, 1), :].rearrange("p b n -> p (b n)")
                        c_top = ch.do(vec.tensor_copy(top, nb[:, 0:HEADS]))
                        c = ch.do(vec.tensor_copy(g_node[:, 0:HEADS], nb[:, HEADS:2 * HEADS]))
                        link(vec.tensor_copy(a_dst_n, nb[:, HEADS:2 * HEADS]))
                        link(vec.memset(den, 1.0))
                        link(vec.tensor_copy(g_sum[:], hself[0][:, 0:D]))
                        link(vec.tensor_tensor(new, top, a_dst_n, ALU.add))
                        link(vec.scalar_tensor_tensor(new, new, SLOPE, new, ALU.mult, ALU.max))
                        link(vec.tensor_copy(g_node[:, HEADS:2 * HEADS], new))
                        assert ch.n == BEFORE, ch.n
                        dve.sem_inc(wait_here, 1)
                        with dve.Fori(0, NW) as w:
                            n = b * NW + w
                            ch.base, ch.n = b * block_links + w * WINDOW + (start + BEFORE), 0
                            dve.wait_ge(g_edges, n * 32 + (l * NB * NW * 32 + 32))
                            link(vec.tensor_scalar(g_dloc, g_dst, block_base[0:ER, bass.ds(b, 1)], None, ALU.subtract))
                            for t in range(TG):
                                m = vec.tensor_scalar(g_onehot[:, t, :], node_iota[0:ER, :], g_dloc[:, t:t + 1], None, ALU.is_equal)
                            link(m)
                            dve.sem_inc(g_onehot_ok, 1)
                            link(vec.tensor_scalar(g_other, g_onehot, -1.0, BIG, ALU.add, ALU.mult))
                            dve.wait_ge(g_gathered, n * (16 * TG) + (l * NB * NW + 1) * (16 * TG))
                            for t in range(TG):
                                for h in range(HEADS):
                                    a = g_rows[:, t, D + h:D + h + 1]
                                    if t == 0:
                                        m = vec.tensor_scalar(g_best[:, h, :], g_other[:, t, :], a, None, ALU.add)
                                    else:
                                        m = vec.scalar_tensor_tensor(g_best[:, h, :], g_other[:, t, :], a, g_best[:, h, :], ALU.add, ALU.max)
                                link(m)
                            dve.sem_inc(g_best_ok, 1)
                            dve.wait_ge(g_best_turned, n + (l * NB * NW + 1))
                            turned = p_rows[0:NBLK, :].rearrange("p (h n) -> p h n", n=P)[:, :, 0:ER]
                            link(vec.tensor_reduce(new, turned, AX.X, ALU.max))
                            link(vec.tensor_tensor(top, top, new, ALU.max))
                            link(vec.tensor_tensor(new, top, a_dst_n, ALU.add))
                            link(vec.scalar_tensor_tensor(new, new, SLOPE, new, ALU.mult, ALU.max))
                            link(vec.tensor_tensor(arg, g_node[:, HEADS:2 * HEADS], new, ALU.subtract))
                            link(vec.tensor_copy(g_node[:, HEADS:2 * HEADS], new))
                            dve.sem_inc(g_arg, 1)
                            dve.wait_ge(g_spread, n + (l * NB * NW + 1))
                            spread = p_expand[0:ER, 0:TG * 8].rearrange("p (t n) -> p t n", n=8)
                            link(vec.tensor_tensor(g_alpha, g_rows[:, :, D:HW], spread[:, :, 0:HEADS], ALU.add))
                            link(vec.scalar_tensor_tensor(g_alpha, g_alpha, SLOPE, g_alpha, ALU.mult, ALU.max))
                            link(vec.tensor_tensor(g_alpha, g_alpha, spread[:, :, HEADS:2 * HEADS], ALU.subtract))
                            vec.tensor_scalar(g_logit_t, g_alpha, 0.0, None, ALU.min).then_inc(g_logit, 1)
                            dve.wait_ge(g_exp, n + (l * NB * NW + 1))
                            hv = g_rows[:, :, 0:D].rearrange("p t (h c) -> p t h c", h=HEADS)
                            for t in range(TG):
                                m = vec.tensor_tensor(hv[:, t], hv[:, t], g_rows[:, t, D:HW].unsqueeze(2).to_broadcast([ER, HEADS, C]), ALU.mult)
                            m.then_inc(g_prod, 1)
                            dve.wait_ge(g_scale, n + (l * NB * NW + 1))
                            dve.wait_ge(g_acc, n + (l * NB * NW + 1))
                            acc = p_acc[0][0:NBLK, :]
                            link(vec.tensor_tensor(den, den, shrink, ALU.mult))
                            link(vec.tensor_tensor(den, den, acc[:, D:HW], ALU.add))
                            for h in range(HEADS):
                                m = vec.scalar_tensor_tensor(g_sum[:, by_head(h)], g_sum[:, by_head(h)], shrink[:, h:h + 1], acc[:, by_head(h)], ALU.mult, ALU.add)
                            link(m)
                            assert ch.n == WINDOW, (ch.n, WINDOW)
                            dve.sem_inc(g_window, 1)
                        ch.base, ch.n = b * block_links + (start + BEFORE + NW * WINDOW), 0
                        link(vec.tensor_scalar(den, den, 1e-16, None, ALU.max))
                        link(vec.reciprocal(den, den))
                        if l == 0:
                            for h in range(HEADS):
                                m = vec.scalar_tensor_tensor(g_sum[:, by_head(h)], g_sum[:, by_head(h)], den[:, h:h + 1], bias[0][:, by_head(h)], ALU.mult, ALU.add)
                            link(m)
                            link(vec.tensor_scalar(h1[:], g_sum[:], 0.0, None, ALU.max))
                            dve.sem_inc(g_feat, 1)
                        else:
                            link(vec.tensor_tensor(xres[0][:], xres[0][:], bias[1][:], ALU.add))
                            for h in range(HEADS):
                                m = vec.scalar_tensor_tensor(x1[0][:, by_head(h)], g_sum[:, by_head(h)], den[:, h:h + 1], xres[0][:, by_head(h)], ALU.mult, ALU.add)
                            link(m)
                            for i in range(9):
                                ch.after(norm_step(i, 0))
                            vec.tensor_scalar(xn2[0][:], x1[0][:], mv[:, 0, 0:1], rs[:, 0, 0:1], ALU.subtract, ALU.mult).then_inc(g_feat, 1)
                        assert ch.n == AFTER[l], (l, ch.n)
                dve.wait_ge(g_out, 2 * NB)


            ch = Chain(dve, dve_ffn_s)
            link = ch.link
            link(vec.tensor_reduce(mean[:], colsum[:], AX.X, ALU.add))
            vec.tensor_scalar(mean[:], mean[:], 1.0 / N, None, ALU.mult).then_inc(r_mean, 1)
            dve.wait_ge(r_logit, 1)
            R = lambda i: rt[:, i, :]
            S = lambda i, k: rt[:, i, k:k + 1]
            link(vec.tensor_tensor(R(2), p_small[0:1, 0:NX], R(0), ALU.add))

            def softmax(dst_i_, src_i_, arg, done):
                link(vec.tensor_reduce(S(5, 0), R(src_i_), AX.X, ALU.max))
                vec.tensor_scalar(R(3), R(src_i_), S(5, 0), None, ALU.subtract).then_inc(arg, 1)
                dve.wait_ge(done, 1)
                link(vec.tensor_reduce(S(5, 1), R(4), AX.X, ALU.add))
                link(vec.reciprocal(S(5, 2), S(5, 1)))
                link(vec.tensor_scalar(R(dst_i_), R(4), S(5, 2), None, ALU.mult))
            softmax(6, 2, r_arg, r_exp)
            link(vec.tensor_scalar(R(7), R(6), float(N), None, ALU.mult))
            link(vec.tensor_scalar(R(8), R(7), capacity, None, ALU.is_gt))
            link(vec.tensor_scalar(R(9), R(7), capacity, None, ALU.max))
            link(vec.reciprocal(R(9), R(9)))
            link(vec.tensor_scalar(R(9), R(9), capacity, -1.0, ALU.mult, ALU.add))
            link(vec.tensor_tensor(R(9), R(9), R(8), ALU.mult))
            link(vec.tensor_scalar(R(9), R(9), 1.0, None, ALU.add))
            link(vec.tensor_tensor(R(10), R(6), R(9), ALU.mult))
            softmax(6, 10, r_arg2, r_exp2)
            link(vec.memset(R(15), -BIG))
            for k in range(TOP_K):
                link(vec.tensor_reduce(S(15, k), R(6), AX.X, ALU.max))
                link(vec.tensor_scalar(R(11), R(6), S(15, k), None, ALU.not_equal))
                link(vec.scalar_tensor_tensor(R(12), R(11), 1024.0, R(1), ALU.mult, ALU.add))
                link(vec.tensor_reduce(S(13, k), R(12), AX.X, ALU.min))
                link(vec.tensor_scalar(R(14), R(1), S(13, k), None, ALU.is_equal))
                link(vec.scalar_tensor_tensor(R(6), R(14), -1024.0, R(6), ALU.mult, ALU.add))
            vec.tensor_copy(sel_i[:], rt[:, 13, 0:TOP_K]).then_inc(r_sel, 1)
            softmax(6, 15, r_arg3, r_exp3)
            vec.tensor_copy(wsel[:], rt[:, 6, 0:TOP_K]).then_inc(r_w, 1)
            dve.wait_ge(r_wb, 1)
            link(vec.tensor_copy(wsel_b[:], p_small[:, 16:16 + TOP_K]))
            dve.wait_ge(r_load, 16 * 4 * TOP_K)
            for k in range(TOP_K):
                w = eW2[:, k, :, :].rearrange("p t n -> p (t n)")
                link(vec.tensor_scalar(w, w, wsel_b[:, k:k + 1], None, ALU.mult))
            link(vec.tensor_scalar(eb2s[:], eb2[:, 0, :], wsel[:, 0:1], None, ALU.mult))
            vec.scalar_tensor_tensor(eb2s[:], eb2[:, 1, :], wsel[:, 1:2], eb2s[:], ALU.mult, ALU.add).then_inc(r_ready, 1)
            obank = [p_acc[0], p_xt, p_h, p_acc[1]]

            def ffn_chunk(g, half, q):
                dve.wait_ge(f_ok[q], half * 48 + 48)
                if not (isinstance(g, int) and g < 2):
                    dve.wait_ge(f_st[q], half * 16)
                y = xg[q]
                for j in range(GRP):
                    dve.wait_ge(f_out, g * GRP + (j + 1))
                    link(vec.tensor_tensor(y[:, j, :], obank[j][0:NBLK, 0:D], xng[q][:, j, :], ALU.add))
                    dve.sem_inc(f_read, 1)
                    link(vec.bn_stats(stats[:, j, :], y[:, j, :]))
                    dve.sem_inc(wait_here, 1)
                    link(vec.bn_aggr(mv[:, j, :], stats[:, j, :]))
                rsqrt(ch, mv[:, :, 1], GRP, rs, rs_i)
                for j in range(GRP):
                    link(vec.tensor_scalar(y[:, j, :], y[:, j, :], mv[:, j, 0:1], rs[:, 0, j:j + 1], ALU.subtract, ALU.mult))
                wide = [NBLK, GRP, D]
                link(vec.tensor_tensor(y[:], y[:], gamma_b[:].unsqueeze(1).to_broadcast(wide), ALU.mult))
                link(vec.tensor_tensor(y[:], y[:], beta_b[:].unsqueeze(1).to_broadcast(wide), ALU.add))
                vec.tensor_tensor(y[:], y[:], fx1[q][:], ALU.add).then_inc(f_done, 1)
            ch.steps(NG, 2, 3, ffn_chunk)


_INS = ["x", "src", "dst", "L0_gnn_W1", "L0_gnn_att_src1", "L0_gnn_att_dst1", "L0_gnn_b1", "L0_gnn_W2", "L0_gnn_att_src2",
        "L0_gnn_att_dst2", "L0_gnn_b2", "L0_ffn_Wr", "L0_ffn_br", "L0_ffn_W1", "L0_ffn_b1", "L0_ffn_W2", "L0_ffn_b2",
        "L0_ffn_gamma", "L0_ffn_beta"]


def kernel(**inputs):
    import numpy as np
    import concourse.bacc as bacc
    from concourse.bass_utils import run_bass_kernel_spmd

    nc = bacc.Bacc("TRN2", target_bir_lowering=False, num_devices=1)
    arrays, args = {}, []
    for name in _INS:
        a = np.ascontiguousarray(inputs[name])
        arrays[f"in_{name}"] = a
        args.append(nc.dram_tensor(f"in_{name}", a.shape, mybir.dt.from_np(a.dtype), kind="ExternalInput").ap())
    args.append(nc.dram_tensor("out_x", arrays["in_x"].shape, F32, kind="ExternalOutput").ap())
    build(nc, *args)
    r = run_bass_kernel_spmd(nc, [arrays], core_ids=[0])
    return r.results[0]["out_x"]
```

```python
import math
from contextlib import ExitStack

import concourse.bass as bass
from concourse import mybir

ALU = mybir.AluOpType
ACT = mybir.ActivationFunctionType
AX = mybir.AxisListType
F32 = mybir.dt.float32
BF16 = mybir.dt.bfloat16
I32 = mybir.dt.int32
F32R = mybir.dt.float32r

P = 128
NBLK = 125
T = 18
CAP = P * T
HEADS = 4
STG = 8
GRP = 4
BIG = 1.0e30
SLOPE = 0.2
LN_EPS = 1e-5
RSQRT_MAGIC = float(0x5F3759DF)
TOP_K = 2


class Chain:

    def __init__(self, eng, sem):
        self.eng, self.sem = eng, sem
        self.base, self.n = 0, 0

    def do(self, ins):
        self.n += 1
        ins.then_inc(self.sem, 1)
        return self.n

    def after(self, count):
        self.eng.wait_ge(self.sem, self.base + count)

    def link(self, ins):
        self.after(self.do(ins))

    def steps(self, total, first, last, body, unroll=2):
        rounds = (total - first - last) // unroll
        assert rounds * unroll == total - first - last

        def at(b, i, u):
            parts = (i * (unroll // 2) + (first + u) // 2, (first + u) % 2)
            if unroll == 6:
                parts += (i * 2 + (first + u) // 3, (first + u) % 3)
            body(b, *parts)
        for b in range(first):
            before = self.n
            at(b, 0, b - first)
            per = self.n - before
        start = self.n
        if rounds:
            with self.eng.Fori(0, rounds) as i:
                for u in range(unroll):
                    self.base, self.n = i * (unroll * per) + (start + u * per), 0
                    at(i * unroll + (first + u), i, u)
                    assert self.n == per, (self.n, per)
        self.base, self.n = 0, start + per * unroll * rounds
        for b in range(total - last, total):
            at(b, 0, b - first)


def build(nc, x, src, dst, W1, as1, ad1, b1, W2, as2, ad2, b2, Wr, br, fW1, fb1, fW2, fb2, gamma, beta, out):
    N, D = x.shape
    E, = src.shape
    C = D // HEADS
    KT = D // P
    NX, F = Wr.shape[1], fW1.shape[2]
    FT = F // P
    NB = N // NBLK
    NG = NB // GRP
    HW = D + HEADS
    HWX = D + 2 * HEADS
    GW = D + 2 * HEADS + 1
    ER = 125
    EC = E // ER
    SAMP = 68 if EC % 68 == 0 else EC
    NS = EC // SAMP
    CHUNK = GRP * NBLK
    NGROUPS_ST = (T + STG - 1) // STG
    capacity = float(math.ceil(N * 1.25 / NX))
    TG = max(t for t in range(1, T + 1) if EC % t == 0)
    NW = EC // TG
    TURN = 4
    NTURN = (TG + TURN - 1) // TURN
    assert KT == 2 and NB * NBLK == N and NG * GRP == NB and EC * ER == E and E >= CAP

    def dram(name, shape, dt=F32):
        return nc.dram_tensor(name, shape, dt).ap()

    dpad = dram("dpad", (E + 2,))
    samples_d = dram("samples_d", (ER * NS,))
    tables = [dram("table1", (N, HW)), dram("table2", (N, HW))]
    x1_d = dram("x1_d", (N, D))
    xn_d = dram("xn_d", (N, D))
    xT_d = dram("xT_d", (KT, P, N))

    with ExitStack() as ctx:
        def sb(name, shape, dt=F32):
            return ctx.enter_context(nc.sbuf_tensor(name, shape, dt))

        def sem(name):
            return ctx.enter_context(nc.semaphore(name))

        bank = {n: ctx.enter_context(nc.psum_tensor(n, [P, 512], F32)) for n in
                ("p_acc0", "p_acc1", "p_st0", "p_st1", "p_expand", "p_rows", "p_xt", "p_h")}
        p_expand, p_rows, p_xt, p_h = (bank[n] for n in ("p_expand", "p_rows", "p_xt", "p_h"))
        p_acc = [bank["p_acc0"], bank["p_acc1"]]
        p_st = [bank["p_st0"], bank["p_st1"]]
        p_stb = [b[:, :].bitcast(BF16) for b in p_st]
        p_small = bank["p_acc1"]
        p_back = p_rows[:, 0:2 * HEADS]

        ident = sb("ident", [P, P])
        ident_b = sb("ident_b", [P, P], BF16)
        ones = sb("ones", [1, P])
        node_iota = sb("node_iota", [P, NBLK])
        block_base = sb("block_base", [P, NB])
        bias = [sb("bias1", [NBLK, D]), sb("bias2", [NBLK, D])]
        gamma_b, beta_b = sb("gamma_b", [NBLK, D]), sb("beta_b", [NBLK, D])

        wext = [sb("wext1", [P, KT, HWX]), sb("wext2", [P, KT, HWX])]
        att = sb("att", [P, 4, KT])
        attm = sb("attm", [P, 2, KT, 2 * HEADS])

        hid_hi, hid_lo = (sb(n, [P, TOP_K * FT, CHUNK], F32R) for n in ("hid_hi", "hid_lo"))
        G = [sb(f"G{r}", [P, T, GW]) for r in range(3)]

        def over_g(r, lo, parts, n):
            return G[r][:].rearrange("p t n -> p (t n)")[0:parts, lo:lo + n]
        dst_i = over_g(2, 0, ER, EC).bitcast(I32)
        dst_f = over_g(2, EC, ER, EC)
        wT = over_g(2, 2 * EC, P, KT * D).rearrange("p (t n) -> p t n", t=KT)
        samp = sb("samp", [ER, NS])
        sentinel = sb("sentinel", [1, 2])
        samp_b = G[0][:].rearrange("p t n -> p (t n)")[0:NB, 0:ER * NS]
        samp_lt = G[1][:].rearrange("p t n -> p (t n)")[0:NB, 0:ER * NS]
        first_node = sb("first_node", [NB, 1])
        st_f = sb("st_f", [NB, 8])
        st_i = sb("st_i", [NB, 1], I32)
        swin = sb("swin", [NB, SAMP], I32)
        swin_lt = sb("swin_lt", [NB, SAMP])
        starts_i = sb("starts_i", [1, NB], I32)
        starts_row = sb("starts_row", [1, NB + 1])
        fits = sb("fits", [1, 4])
        fits_i = sb("fits_i", [1, 1], I32)
        next_f = over_g(2, 0, ER, EC)
        falls = G[0][:].rearrange("p t n -> p (t n)")[0:ER, 0:EC]
        n_falls = sb("n_falls", [ER, 1])

        xg = [sb(f"xg{q}", [NBLK, GRP, D]) for q in range(2)]
        xng_all = sb("xng", [NBLK, 2, GRP, D])
        xng = [xng_all[:, q] for q in range(2)]
        stats = sb("stats", [NBLK, GRP, 6])
        mv = sb("mv", [NBLK, GRP, 2])
        rs = sb("rs", [NBLK, 6, GRP])
        rs_i = sb("rs_i", [NBLK, 2, GRP], I32)
        hT = [sb(f"hT{q}", [P, KT, NBLK]) for q in range(2)]
        xT = hT
        hout = [sb(f"hout{q}", [NBLK, GRP, HWX]) for q in range(2)]
        node = [sb("node1", [NBLK, NB, 2 * HEADS]), sb("node2", [NBLK, NB, 2 * HEADS])]

        over_xng = xng_all[:].rearrange("p q g d -> p (q g d)")
        n_rest, n_parts = NB * 2 * HEADS, NB * 3 * HEADS
        node_rest = over_xng[:, 0:n_rest].rearrange("p (b n) -> p b n", b=NB)
        node_parts = over_xng[:, n_rest:n_rest + n_parts].bitcast(BF16).rearrange("p (b k n) -> p b k n", b=NB, k=3)

        src_w = [sb(f"src_w{q}", [P, T], I32) for q in range(2)]
        dst_w = [sb(f"dst_w{q}", [P, T + 2]) for q in range(2)]
        hself = [sb(f"hself{q}", [NBLK, HW]) for q in range(2)]
        xres = [sb(f"xres{q}", [NBLK, D]) for q in range(2)]
        onehot_r = [sb(f"onehot{q}", [P, T, NBLK], F32R) for q in range(2)]
        onehot = [a[:].bitcast(F32) for a in onehot_r]
        onehot_b = [sb(f"onehot_b{q}", [P, T, NBLK], BF16) for q in range(2)]
        onehotT = sb("onehotT", [NBLK, T, P], BF16)
        node_q = [sb(f"node_q{q}", [NBLK, 2 * HEADS]) for q in range(2)]
        parts_q = [sb(f"parts_q{q}", [NBLK, 3, 2 * HEADS], BF16) for q in range(2)]
        node_iota_b = sb("node_iota_b", [P, NBLK], BF16)
        dloc = sb("dloc", [P, T])
        link_w = sb("link_w", [P, T + 1])
        pen = sb("pen", [P, T + 1])
        run_end = [sb(f"run_end{q}", [P, T]) for q in range(2)]
        penF = [sb(f"penF{q}", [P, HEADS, T + 1]) for q in range(2)]
        penB = [sb(f"penB{q}", [P, HEADS, T + 1]) for q in range(2)]
        whole = [sb(f"whole{q}", [P, 2, HEADS]) for q in range(2)]
        vF = sb("vF", [P, HEADS, T + 1])
        vB = sb("vB", [P, HEADS, T + 1])
        rF = sb("rF", [P, HEADS, T + 1])
        rB = sb("rB", [P, HEADS, T + 1])
        row_pen = sb("row_pen", [HEADS, 2, P])
        carF = sb("carF", [HEADS, P + 1])
        carB = sb("carB", [HEADS, P + 1])
        runmax = sb("runmax", [P, T, HEADS])
        alpha = sb("alpha", [P, T, HEADS])
        logit = sb("logit", [P, T, HEADS])
        self_s = sb("self_s", [NBLK, 8, HEADS])
        hs = sb("hs", [NBLK, D])
        num = sb("num", [NBLK, D])
        h1 = sb("h1", [NBLK, D])
        x1 = [sb(f"x1{q}", [NBLK, D]) for q in range(2)]
        xn2 = [sb(f"xn2{q}", [NBLK, D]) for q in range(2)]
        colsum = sb("colsum", [P, KT, NB])

        g_rows = G[0][0:ER, 0:TG, :]
        g_src, g_dst, g_dloc = src_w[0][0:ER, 0:TG], dst_w[0][0:ER, 0:TG], dloc[0:ER, 0:TG]
        g_onehot = onehot[0][0:ER, 0:TG, :]
        g_onehot_r = onehot_r[0][0:ER, 0:TG, :]
        g_onehotT_r = onehot_r[1][:].rearrange("p t n -> p (t n)")[0:NBLK, 0:TG * ER].rearrange("p (t n) -> p t n", n=ER)
        g_onehotT = g_onehotT_r.bitcast(F32)
        g_other = G[2][:].rearrange("p t n -> p (t n)")[0:ER, 0:TG * NBLK].rearrange("p (t n) -> p t n", n=NBLK)
        g_best = G[1][:].rearrange("p t n -> p (t n)")[0:ER, 0:HEADS * NBLK].rearrange("p (h n) -> p h n", n=NBLK)
        g_alpha, g_logit_t = alpha[0:ER, 0:TG, :], logit[0:ER, 0:TG, :]
        g_sum, g_node = num, node_q[0]
        g_state = sb("g_state", [NBLK, 6, HEADS])

        mean = sb("mean", [P, KT])
        wr_sb = sb("wr_sb", [P, KT, NX])
        rt = sb("rt", [1, 16, NX])
        sel_i = sb("sel_i", [1, TOP_K], I32)
        wsel = sb("wsel", [1, TOP_K])
        wsel_b = sb("wsel_b", [P, TOP_K])
        def over(r, lo, parts, shape):
            size = 1
            for n in shape:
                size *= n
            flat = G[r][:].rearrange("p t n -> p (t n)")[0:parts, lo:lo + size]
            names = " ".join("abc"[:len(shape)])
            return flat.rearrange(f"p ({names}) -> p {names}", **dict(zip("abc", shape)))
        eW1 = over(1, 0, P, [TOP_K, KT, F])
        eb1 = sb("eb1", [P, TOP_K, FT])
        eW2 = over(1, TOP_K * KT * F, P, [TOP_K, FT, D])
        eb2 = over(1, TOP_K * (KT * F + FT * D), NBLK, [TOP_K, D])
        eb2s = sb("eb2s", [NBLK, D])
        fxT = [over(0, q * KT * CHUNK, P, [KT, CHUNK]) for q in range(2)]
        fx1 = [over(0, 2 * KT * CHUNK + q * GRP * D, NBLK, [GRP, D]) for q in range(2)]
        NH = TOP_K * FT
        gelu_out = over(2, 0, P, [4, CHUNK])
        x_hi, x_lo = (sb(n, [P, KT, CHUNK], F32R)[:] for n in ("x_hi", "x_lo"))

        def over_onehot(q, shape):
            flat = onehot_r[q][:].rearrange("p t n -> p (t n)")[:, 0:shape[0] * shape[1] * shape[2]]
            return flat.rearrange("p (a b c) -> p a b c", a=shape[0], b=shape[1])
        w1_hi, w1_lo = over_onehot(0, [TOP_K, KT, F]), sb("w1_lo", [P, TOP_K, KT, F], F32R)[:]
        w2_hi, w2_lo = over_onehot(1, [TOP_K, FT, D]), sb("w2_lo", [P, TOP_K, FT, D], F32R)[:]

        wait_here = sem("wait_here")
        dve_s, act_s = sem("dve_chain"), sem("act_chain")
        dve_agg_s, dve_general_s, dve_ffn_s, s_next, s_falls = (sem(n) for n in (
            "dve_agg_chain", "dve_general_chain", "dve_ffn_chain", "s_next", "s_falls"))
        s_const, s_in, s_wT, s_wTc, s_att, s_watt, s_wext = (sem(n) for n in (
            "s_const", "s_in", "s_wT", "s_wTc", "s_att", "s_watt", "s_wext"))
        s_dst, s_dstf, s_pad, s_sampd, s_sampb, s_idx, s_swin, s_st, s_stT, s_starts = (sem(n) for n in (
            "s_dst", "s_dstf", "s_pad", "s_sampd", "s_sampb", "s_idx", "s_swin", "s_st", "s_stT", "s_starts"))
        x_ok = [sem(f"x_ok{q}") for q in range(2)]
        x_norm, xt_done, xt_copied, h_done, h_copied = (sem(n) for n in ("x_norm", "xt_done", "xt_copied", "h_done", "h_copied"))
        tab_st = [sem(f"tab_st{q}") for q in range(2)]
        L = []
        for l in range(2):
            d = {n: sem(f"{n}_l{l}") for n in (
                "onehot_done", "wide_ok", "hs_ok", "sum_ok", "onehot_ok", "st_done", "st_copied", "expand_done", "ends_ok", "rows_done",
                "carry_ok", "back_done", "logit_ok", "exp_ok", "prod_ok", "main_done", "acc_read", "sarg_ok", "sexp_ok",
                "feat_ok", "ft_done", "ft_copied", "hh_done", "hh_copied", "epi_done")}
            for n in ("src_ok", "dst_ok", "self_ok", "xres_ok", "stored", "stored2"):
                d[n] = [sem(f"{n}_l{l}_{q}") for q in range(2)]
            d["gathered"] = [sem(f"gathered_l{l}_{r}") for r in range(3)]
            L.append(d)
        (g_own0, g_own1, g_edges, g_gathered, g_onehot_ok, g_turned, g_turned_sb, g_best_ok, g_best_turned, g_arg, g_scale,
         g_spread, g_logit, g_exp, g_prod, g_acc, g_window, g_feat, g_ft, g_ft_sb, g_hh, g_out, g_stored, g_table) = (
            [L[0][n][0] for n in ("self_ok", "dst_ok", "src_ok", "gathered")]
            + [L[0][n] for n in ("onehot_done", "st_done", "st_copied", "ends_ok", "rows_done", "sarg_ok", "sexp_ok", "expand_done",
                                 "logit_ok", "exp_ok", "prod_ok", "main_done", "acc_read", "feat_ok", "ft_done", "ft_copied",
                                 "hh_done", "hh_copied")]
            + [L[0]["stored"][0], L[0]["stored"][1]])
        r_mean, r_logit, r_exp, r_sel, r_w, r_wb, r_load, r_ready, r_exp2, r_exp3, r_arg, r_arg2, r_arg3 = (sem(n) for n in (
            "r_mean", "r_logit", "r_exp", "r_sel", "r_w", "r_wb", "r_load", "r_ready", "r_exp2", "r_exp3", "r_arg", "r_arg2", "r_arg3"))
        f_ok = [sem(f"f_ok{q}") for q in range(2)]
        f_st = [sem(f"f_st{q}") for q in range(2)]
        f_hid, f_gelu, f_out, f_read, f_done, f_hi, f_lo, f_split = (sem(n) for n in (
            "f_hid", "f_gelu", "f_out", "f_read", "f_done", "f_hi", "f_lo", "f_split"))

        xrows = x.rearrange("(b p) d -> p b d", p=NBLK)
        outrows = out.rearrange("(b p) d -> p b d", p=NBLK)
        x1rows = x1_d.rearrange("(b p) d -> p b d", p=NBLK)
        xnrows = xn_d.rearrange("(b p) d -> p b d", p=NBLK)
        tabrows = [t.rearrange("(b p) d -> p b d", p=NBLK) for t in tables]
        SETUP_LOADS = 16 * (2 + 4 + 4 + 2)

        def rsqrt(ch, eps_var, n, r, ri):
            v, y, t = r[:, 1, 0:n], r[:, 0, 0:n], r[:, 2, 0:n]
            vec = nc.vector
            ch.link(vec.tensor_scalar(v, eps_var, LN_EPS, None, ALU.add))
            ch.link(vec.tensor_scalar(ri[:, 0, 0:n], v.bitcast(I32), 1, None, ALU.logical_shift_right))
            ch.link(vec.tensor_scalar(y.bitcast(I32), ri[:, 0, 0:n], -1.0, RSQRT_MAGIC, ALU.mult, ALU.add))
            for _ in range(3):
                ch.link(vec.tensor_tensor(t, y, y, ALU.mult))
                ch.link(vec.tensor_tensor(t, t, v, ALU.mult))
                ch.link(vec.tensor_scalar(t, t, -0.5, 1.5, ALU.mult, ALU.add))
                ch.link(vec.tensor_tensor(y, y, t, ALU.mult))

        block = ctx.enter_context(nc.Block())

        @block.sync
        def _(sp):
            ch = Chain(sp, None)
            with nc.allow_non_contiguous_dma(reason="attention vectors and samples, one element a row"):
                sp.dma_start(dst_i, dst.rearrange("(p k) -> p k", p=ER)).then_inc(s_dst, 16)
                sp.dma_start(wext[0][:, :, 0:D], W1.rearrange("(t p) n -> p t n", p=P)).then_inc(s_in, 16)
                sp.dma_start(wext[1][:, :, 0:D], W2.rearrange("(t p) n -> p t n", p=P)).then_inc(s_in, 16)
                for i, a in enumerate((as1, ad1, as2, ad2)):
                    sp.dma_start(att[:, i, :], a.rearrange("o (t h) c -> (o h c) t", t=KT)).then_inc(s_in, 16)
                for dst_t, v in ((bias[0], b1), (bias[1], b2), (gamma_b, gamma), (beta_b, beta)):
                    sp.dma_start(dst_t[:], v.partition_broadcast(NBLK)).then_inc(s_in, 16)
                sp.dma_start(wr_sb[:], Wr.rearrange("(t p) n -> p t n", p=P)).then_inc(s_in, 16)
                sp.dma_start(rt[:, 0, :], br.rearrange("(a n) -> a n", a=1)).then_inc(s_in, 16)
                for g in range(2):
                    sp.dma_start(xg[g][:], xrows[:, g * GRP:(g + 1) * GRP, :]).then_inc(x_ok[g], 16)
                sp.wait_ge(s_dstf, 1)
                sp.dma_start(dpad[bass.ds(1, E)].rearrange("(p k) -> p k", p=ER), dst_f).then_inc(s_pad, 16)
                sp.dma_start(dpad[0:1].rearrange("(a n) -> a n", a=1), sentinel[:, 0:1]).then_inc(s_pad, 16)
                sp.dma_start(dpad[bass.ds(E + 1, 1)].rearrange("(a n) -> a n", a=1), sentinel[:, 1:2]).then_inc(s_pad, 16)
                sp.dma_start(samples_d.rearrange("(p k) -> p k", p=ER), samp[:]).then_inc(s_sampd, 16)
                sp.wait_ge(s_sampd, 16)
                sp.dma_start(samp_b, samples_d.partition_broadcast(NB)).then_inc(s_sampb, 16)
                sp.wait_ge(s_pad, 48)
                sp.dma_start(next_f, dpad[bass.ds(2, E)].rearrange("(p k) -> p k", p=ER)).then_inc(s_next, 16)

            def table_group(g, half, q):
                if not isinstance(g, int) or g < NG - 2:
                    sp.wait_ge(x_norm, g + 1)
                    sp.dma_start(xg[q][:], xrows[:, bass.ds(g * GRP + 2 * GRP, GRP), :]).then_inc(x_ok[q], 16)
                sp.wait_ge(h_copied, g * GRP + GRP)
                sp.dma_start(tabrows[0][:, bass.ds(g * GRP, GRP), :], hout[q][:, :, 0:HW]).then_inc(tab_st[q], 16)
            ch.steps(NG, 2, 3, table_group)
            sp.wait_ge(tab_st[0], 16 * ((NG + 1) // 2))
            sp.wait_ge(tab_st[1], 16 * (NG // 2))
            sp.wait_ge(s_starts, 1)
            fit = sp.value_load(fits_i[0:1, 0:1], min_val=0, max_val=1)

            with sp.If(fit > 0):
                for l in range(2):
                    s = L[l]

                    def load_edges(b, q, s=s):
                        at = sp.value_load(starts_i[0:1, bass.ds(b, 1)], min_val=0, max_val=E - CAP)
                        sp.dma_start(src_w[q][:], src[bass.ds(at, CAP)].rearrange("(p k) -> p k", p=P)).then_inc(s["src_ok"][q], 16)
                        window = dpad[bass.ds(at, CAP)]
                        sp.dma_start(dst_w[q][:], bass.AP(window.tensor, window.offset, [[T, P], [1, T + 2]])).then_inc(s["dst_ok"][q], 16)

                    def load_nodes(b, q, s=s, l=l):
                        sp.dma_start(hself[q][:], tabrows[l][:, bass.ds(b, 1), :].rearrange("p b d -> p (b d)")).then_inc(s["self_ok"][q], 16)
                        if l == 1:
                            sp.dma_start(xres[q][:], xrows[:, bass.ds(b, 1), :].rearrange("p b d -> p (b d)")).then_inc(s["xres_ok"][q], 16)

                    for q in range(2):
                        sp.sem_inc(s["stored"][q], 16)
                        if l == 1:
                            sp.sem_inc(s["stored2"][q], 16)
                    for b in range(2):
                        load_edges(b, b)
                    for b in range(2):
                        load_nodes(b, b)

                    def store_block(b, q, s=s, l=l):
                        if l == 0:
                            sp.wait_ge(s["hh_copied"], b + 1)
                            sp.dma_start(tabrows[1][:, bass.ds(b, 1), :].rearrange("p b d -> p (b d)"),
                                         hout[q][:, 0, 0:HW]).then_inc(s["stored"][q], 16)
                        else:
                            sp.wait_ge(s["feat_ok"], b + 1)
                            sp.dma_start(x1rows[:, bass.ds(b, 1), :].rearrange("p b d -> p (b d)"), x1[q][:]).then_inc(s["stored"][q], 16)
                            sp.dma_start(xnrows[:, bass.ds(b, 1), :].rearrange("p b d -> p (b d)"), xn2[q][:]).then_inc(s["stored"][q], 16)
                            sp.wait_ge(s["ft_copied"], b + 1)
                            sp.dma_start(xT_d.rearrange("t p n -> p t n")[:, :, bass.ds(b * NBLK, NBLK)], hT[q][:]).then_inc(s["stored2"][q], 16)

                    def agg_block(b, half, q, third, r, s=s, l=l):
                        if not (isinstance(b, int) and b >= NB - 2):
                            sp.wait_ge(s["gathered"][r], (third + 1) * (16 * T))
                            sp.wait_ge(s["onehot_ok"], b + 1)
                            load_edges(b + 2, q)
                        if not (isinstance(b, int) and b == 0):
                            if not (isinstance(b, int) and b == NB - 1):
                                sp.wait_ge(s["epi_done"], b)
                                load_nodes(b + 1, 1 - q)
                        if not (isinstance(b, int) and b < 2):
                            store_block(b - 2, q)
                    ch.steps(NB, 2, 2, agg_block, unroll=6)
                    for b in (NB - 2, NB - 1):
                        store_block(b, b % 2)
                    for q in range(2):
                        sp.wait_ge(s["stored"][q], 16 * (l + 1) * (NB // 2) + 16)
                        if l == 1:
                            sp.wait_ge(s["stored2"][q], 16 * (NB // 2) + 16)
            with sp.Else():
                rows_w = src.rearrange("(p k) -> p k", p=ER)
                rows_d = dpad[bass.ds(1, E)].rearrange("(p k) -> p k", p=ER)
                for l in range(2):
                    with sp.Fori(0, NB) as b:
                        own = g_own0 if l == 0 else g_own1
                        sp.dma_start(hself[0][:], tabrows[l][:, bass.ds(b, 1), :].rearrange("p b d -> p (b d)")).then_inc(own, 16)
                        if l == 1:
                            sp.dma_start(xres[0][:], xrows[:, bass.ds(b, 1), :].rearrange("p b d -> p (b d)")).then_inc(own, 16)
                        with sp.Fori(0, NW) as w:
                            sp.wait_ge(g_window, b * NW + w + (l * NB * NW + 1))
                            with nc.allow_non_contiguous_dma(reason="a part of each row of the edge list"):
                                sp.dma_start(g_src, rows_w[:, bass.ds(w * TG, TG)]).then_inc(g_edges, 16)
                                sp.dma_start(g_dst, rows_d[:, bass.ds(w * TG, TG)]).then_inc(g_edges, 16)
                        sp.wait_ge(g_out, b + (l * NB + 1))
                        if l == 0:
                            sp.dma_start(tabrows[1][:, bass.ds(b, 1), :].rearrange("p b d -> p (b d)"), hout[0][:, 0, 0:HW]).then_inc(g_table, 16)
                            sp.wait_ge(g_table, b * 16 + 16)
                            sp.sem_inc(wait_here, 1)
                        else:
                            sp.dma_start(x1rows[:, bass.ds(b, 1), :].rearrange("p b d -> p (b d)"), x1[0][:]).then_inc(g_stored, 16)
                            sp.dma_start(xnrows[:, bass.ds(b, 1), :].rearrange("p b d -> p (b d)"), xn2[0][:]).then_inc(g_stored, 16)
                            sp.dma_start(xT_d.rearrange("t p n -> p t n")[:, :, bass.ds(b * NBLK, NBLK)], hT[0][:]).then_inc(g_stored, 16)
                            sp.wait_ge(g_stored, b * 48 + 48)
                            sp.sem_inc(wait_here, 1)

            sp.wait_ge(r_sel, 1)
            for k in range(TOP_K):
                e = sp.value_load(sel_i[0:1, k:k + 1], min_val=0, max_val=NX - 1)
                sp.dma_start(eW1[:, k, :, :], fW1[bass.ds(e, 1), :, :].rearrange("e (t p) f -> p (e t) f", p=P)).then_inc(r_load, 16)
                sp.dma_start(eW2[:, k, :, :], fW2[bass.ds(e, 1), :, :].rearrange("e (t p) n -> p (e t) n", p=P)).then_inc(r_load, 16)
                with nc.allow_non_contiguous_dma(reason="a bias by partition"):
                    sp.dma_start(eb1[:, k, :], fb1[bass.ds(e, 1), :].rearrange("e (t p) -> p (e t)", p=P)).then_inc(r_load, 16)
                sp.dma_start(eb2[:, k, :], fb2[bass.ds(e, 1), :].rearrange("e n -> (e n)").partition_broadcast(NBLK)).then_inc(r_load, 16)

            def load_chunk(g, q):
                sp.dma_start(fxT[q][:], xT_d.rearrange("t p n -> p t n")[:, :, bass.ds(g * CHUNK, CHUNK)]).then_inc(f_ok[q], 16)
                sp.dma_start(xng[q], xnrows[:, bass.ds(g * GRP, GRP), :]).then_inc(f_ok[q], 16)
                sp.dma_start(fx1[q][:], x1rows[:, bass.ds(g * GRP, GRP), :]).then_inc(f_ok[q], 16)
            for g in range(2):
                load_chunk(g, g)

            def ffn_chunk(g, half, q):
                sp.wait_ge(f_done, g + 1)
                sp.dma_start(outrows[:, bass.ds(g * GRP, GRP), :], xg[q][:]).then_inc(f_st[q], 16)
                if not isinstance(g, int) or g < NG - 2:
                    sp.wait_ge(f_hid, g * NH + NH)
                    load_chunk(g + 2, q)
            ch.steps(NG, 2, 3, ffn_chunk)
            sp.wait_ge(f_st[0], 16 * ((NG + 1) // 2))
            sp.wait_ge(f_st[1], 16 * (NG // 2))

        @block.gpsimd
        def _(pool):
            ch = Chain(pool, None)
            nc.gpsimd.memset(ident[:], 0.0).then_inc(s_const, 1)
            nc.gpsimd.iota(node_iota[:], [[1, NBLK]], base=0, channel_multiplier=0, allow_small_or_imprecise_dtypes=True).then_inc(s_const, 1)
            nc.gpsimd.iota(block_base[:], [[NBLK, NB]], base=0, channel_multiplier=0, allow_small_or_imprecise_dtypes=True).then_inc(s_const, 1)
            nc.gpsimd.iota(first_node[:], [[0, 1]], base=0, channel_multiplier=NBLK, allow_small_or_imprecise_dtypes=True).then_inc(s_const, 1)
            nc.gpsimd.iota(rt[:, 1, :], [[1, NX]], base=0, channel_multiplier=0, allow_small_or_imprecise_dtypes=True).then_inc(s_const, 1)
            pool.wait_ge(s_const, 5)
            nc.gpsimd.affine_select(out=ident[:], in_=ident[:], compare_op=ALU.not_equal, fill=1.0, base=0,
                                    pattern=[[-1, P]], channel_multiplier=1).then_inc(s_const, 1)
            pool.wait_ge(s_idx, 1)
            pool.indirect_dma_start(out=swin[:], out_offset=None, in_=dst.rearrange("(n k) -> n k", k=SAMP),
                                    in_offset=bass.IndirectOffsetOnAxis(ap=st_i[:], axis=0),
                                    bounds_check=E // SAMP - 1, oob_is_err=False).then_inc(s_swin, 16)

            pool.wait_ge(s_starts, 1)
            fit = pool.value_load(fits_i[0:1, 0:1], min_val=0, max_val=1)
            with pool.If(fit > 0):
                for l in range(2):
                    s = L[l]
                    if l == 0:
                        pool.wait_ge(tab_st[0], 16 * ((NG + 1) // 2))
                        pool.wait_ge(tab_st[1], 16 * (NG // 2))
                    else:
                        for q in range(2):
                            pool.wait_ge(L[0]["stored"][q], 16 * (NB // 2) + 16)

                    def gather(b, half, q, third, r, s=s, l=l):
                        pool.wait_ge(s["src_ok"][q], half * 16 + 16)
                        if not isinstance(b, int) or b >= 3:
                            pool.wait_ge(s["main_done"], b - 2)
                        elif l == 1:
                            pool.wait_ge(L[0]["main_done"], NB)
                        pool.sem_inc(wait_here, 1)
                        for t in range(T):
                            pool.indirect_dma_start(out=G[r][:, t, 0:HW], out_offset=None, in_=tables[l],
                                                    in_offset=bass.IndirectOffsetOnAxis(ap=src_w[q][:, t:t + 1], axis=0),
                                                    bounds_check=N - 1, oob_is_err=False).then_inc(s["gathered"][r], 16)
                    ch.steps(NB, 3, 1, gather, unroll=6)
            with pool.Else():
                for l in range(2):
                    with pool.Fori(0, NB) as b:
                        with pool.Fori(0, NW) as w:
                            pool.wait_ge(g_edges, (b * NW + w) * 32 + (l * NB * NW * 32 + 32))
                            pool.sem_inc(wait_here, 1)
                            for t in range(TG):
                                pool.indirect_dma_start(out=G[0][0:ER, t, 0:HW], out_offset=None, in_=tables[l],
                                                        in_offset=bass.IndirectOffsetOnAxis(ap=src_w[0][0:ER, t:t + 1], axis=0),
                                                        bounds_check=N - 1, oob_is_err=False).then_inc(g_gathered, 16)

            pool.wait_ge(f_split, 1)
            nc.gpsimd.tensor_tensor(w1_lo, eW1, w1_hi, ALU.subtract).then_inc(f_split, 1)

            def low_x(g, q):
                pool.wait_ge(f_split, g * 2 + 3)
                nc.gpsimd.tensor_tensor(x_lo, fxT[q], x_hi, ALU.subtract).then_inc(f_split, 1)

            def ffn_low(g, half, q):
                for n in range(NH):
                    pool.wait_ge(f_hi, g * NH + (n + 1))
                    nc.gpsimd.tensor_tensor(hid_lo[:, n, :], gelu_out[:, n % 4, :], hid_hi[:, n, :], ALU.subtract).then_inc(f_lo, 1)
                if not (isinstance(g, int) and g == NG - 1):
                    low_x(g + 1, 1 - q)
            low_x(0, 0)
            ch.steps(NG, 2, 3, ffn_low)

        @block.tensor
        def _(pe):
            ch = Chain(pe, None)
            pe.wait_ge(s_const, 6)
            pe.wait_ge(s_in, SETUP_LOADS)
            for l in range(2):
                if l == 1:
                    pe.wait_ge(s_wTc, 1)
                for i in range(KT):
                    for j in range(KT):
                        m = pe.transpose(p_xt[:, (j * KT + i) * P:(j * KT + i + 1) * P], wext[l][:, i, j * P:(j + 1) * P], ident[:])
                m.then_inc(s_wT, 1)
                pe.wait_ge(s_wTc, l + 1)
                pe.wait_ge(s_att, 1)
                for i in range(KT):
                    for j in range(KT):
                        m = pe.matmul(p_small[:, (l * KT + i) * 16:(l * KT + i) * 16 + 2 * HEADS], wT[:, j, i * P:(i + 1) * P], attm[:, l, j, :],
                                      start=(j == 0), stop=(j == KT - 1))
                m.then_inc(s_watt, 1)
            pe.wait_ge(s_wext, 2)
            xtb, hb = [p_xt, p_rows], [p_h, p_expand]

            def turn_x(g, j, q):
                c, k = g * GRP + j, j % 2
                if j == 0:
                    pe.wait_ge(x_norm, g + 1)
                if not (isinstance(c, int) and c < 2):
                    pe.wait_ge(xt_copied, c - 1)
                for t in range(KT):
                    m = pe.transpose(xtb[k][:, t * P:t * P + NBLK], xng[q][:, j, t * P:(t + 1) * P], ident[0:NBLK, 0:NBLK])
                m.then_inc(xt_done, 1)

            def table_group(g, half, q):
                for j in range(GRP):
                    c, k = g * GRP + j, j % 2
                    if j < GRP - 1:
                        turn_x(g, j + 1, q)
                    elif not (isinstance(g, int) and g == NG - 1):
                        turn_x(g + 1, 0, 1 - q)
                    pe.wait_ge(xt_copied, c + 1)
                    if not (isinstance(c, int) and c < 2):
                        pe.wait_ge(h_copied, c - 1)
                    for t in range(KT):
                        m = pe.matmul(hb[k][0:NBLK, 0:HWX], xT[k][:, t, :], wext[0][:, t, :], start=(t == 0), stop=(t == KT - 1))
                    m.then_inc(h_done, 1)
            turn_x(0, 0, 0)
            ch.steps(NG, 2, 3, table_group)
            pe.wait_ge(s_st, 1)
            pe.transpose(p_small[0:1, 128:128 + NB], st_f[:, 4:5], ident[0:NB, 0:NB])
            pe.transpose(p_small[0:1, 256:256 + NB], st_f[:, 3:4], ident[0:NB, 0:NB])
            pe.wait_ge(s_falls, 1)
            pe.transpose(p_small[0:1, 384:384 + ER], n_falls[:], ident[0:ER, 0:ER]).then_inc(s_stT, 1)
            pe.wait_ge(s_starts, 1)
            fit = pe.value_load(fits_i[0:1, 0:1], min_val=0, max_val=1)

            with pe.If(fit > 0):
                for l in range(2):
                    s = L[l]
                    pe.wait_ge(h_copied, NB)
                    if l == 1:
                        pe.wait_ge(L[0]["hh_copied"], NB)
                        pe.wait_ge(L[0]["epi_done"], NB)

                    def turn_onehots(b, q, groups, s=s):
                        for gi in groups:
                            n = b * NGROUPS_ST + gi
                            pe.wait_ge(s["onehot_done"], n + 1)
                            if not (isinstance(n, int) and n < 2):
                                pe.wait_ge(s["st_copied"], n - 1)
                            lo, hi = gi * STG, min(T, gi * STG + STG)
                            bankt = p_stb[(gi + q * (NGROUPS_ST % 2)) % 2]
                            for t in range(lo, hi):
                                m = pe.transpose(bankt[0:NBLK, (t - lo) * P:(t - lo + 1) * P], onehot_b[q][:, t, :], ident_b[:])
                            m.then_inc(s["st_done"], 1)

                    def expand(b, q, s=s):
                        if not (isinstance(b, int) and b == 0):
                            pe.wait_ge(s["logit_ok"], b)
                        for gi in range(NGROUPS_ST):
                            pe.wait_ge(s["st_copied"], b * NGROUPS_ST + gi + 1)
                            for t in range(gi * STG, min(T, gi * STG + STG)):
                                for k in range(3):
                                    m = pe.matmul(p_expand[:, t * 8:t * 8 + 8], onehotT[:, t, :], parts_q[q][:, k, :], start=(k == 0), stop=(k == 2))
                        m.then_inc(s["expand_done"], 1)

                    def turn(b, q, s=s, l=l):
                        pe.wait_ge(s["feat_ok"], b + 1)
                        f = h1 if l == 0 else xn2[q]
                        if not (isinstance(b, int) and b == 0):
                            pe.wait_ge(s["ft_copied"], b)
                        for t in range(KT):
                            m = pe.transpose(p_xt[:, t * P:t * P + NBLK], f[:, t * P:(t + 1) * P], ident[0:NBLK, 0:NBLK])
                        m.then_inc(s["ft_done"], 1)

                    def project(b, q, s=s):
                        pe.wait_ge(s["ft_copied"], b + 1)
                        if not (isinstance(b, int) and b == 0):
                            pe.wait_ge(s["hh_copied"], b)
                        for t in range(KT):
                            m = pe.matmul(p_h[0:NBLK, 0:HWX], hT[q][:, t, :], wext[1][:, t, :], start=(t == 0), stop=(t == KT - 1))
                        m.then_inc(s["hh_done"], 1)

                    def run_rows(b, q, s=s):
                        pe.wait_ge(s["ends_ok"], b + 1)
                        for i, a in enumerate((rF[:, :, T], whole[q][:, 0, :], rB[:, :, 0], whole[q][:, 1, :])):
                            m = pe.transpose(p_rows[0:HEADS, i * P:(i + 1) * P], a, ident[:])
                        m.then_inc(s["rows_done"], 1)

                    def carries(b, s=s):
                        pe.wait_ge(s["carry_ok"], b + 1)
                        pe.sem_inc(wait_here, 1)
                        pe.transpose(p_back[:, 0:HEADS], carF[:, 0:P], ident[0:HEADS, 0:HEADS])
                        pe.transpose(p_back[:, HEADS:2 * HEADS], carB[:, 1:P + 1], ident[0:HEADS, 0:HEADS]).then_inc(s["back_done"], 1)

                    rows_at, carries_at = ((12, 16), (14, 18))[l]

                    def agg_block(b, half, q, third, r, s=s, l=l):
                        more = not (isinstance(b, int) and b == NB - 1)
                        if not (isinstance(b, int) and b < 2):
                            project(b - 2, q) if l == 0 else turn(b - 2, q)
                        if more:
                            turn_onehots(b + 1, 1 - q, range(NGROUPS_ST))
                            expand(b + 1, 1 - q)
                        if not (isinstance(b, int) and b < 2):
                            pe.wait_ge(s["acc_read"], b - 1)
                        pe.wait_ge(s["wide_ok"], b + 1)
                        for t in range(T):
                            if t == 8 and l == 0 and not (isinstance(b, int) and b == 0):
                                turn(b - 1, 1 - q)
                            if t == rows_at and more:
                                run_rows(b + 1, 1 - q)
                            if t == carries_at and more:
                                carries(b + 1)
                            if t % 2 == 0:
                                pe.wait_ge(s["prod_ok"], b * 9 + (t // 2 + 1))
                            m = pe.matmul(p_acc[q][0:NBLK, 0:GW], onehot[q][:, t, :], G[r][:, t, :], start=(t == 0), stop=(t == T - 1))
                        m.then_inc(s["main_done"], 1)
                        if more and carries_at == T:
                            if rows_at == T:
                                run_rows(b + 1, 1 - q)
                            carries(b + 1)
                    turn_onehots(0, 0, range(NGROUPS_ST))
                    expand(0, 0)
                    run_rows(0, 0)
                    carries(0)
                    ch.steps(NB, 3, 1, agg_block, unroll=6)
                    if l == 0:
                        project(NB - 2, NB % 2)
                        turn(NB - 1, (NB - 1) % 2)
                        project(NB - 1, (NB - 1) % 2)
                    else:
                        turn(NB - 2, NB % 2)
                        turn(NB - 1, (NB - 1) % 2)
            with pe.Else():
                for l in range(2):
                    with pe.Fori(0, NB) as b:
                        with pe.Fori(0, NW) as w:
                            n = b * NW + w
                            pe.wait_ge(g_onehot_ok, n + (l * NB * NW + 1))
                            for i in range(NTURN):
                                if i >= 2:
                                    pe.wait_ge(g_turned_sb, n * NTURN + (l * NB * NW * NTURN + i - 1))
                                for t in range(i * TURN, min(TG, (i + 1) * TURN)):
                                    m = pe.transpose(p_st[i % 2][0:NBLK, (t % TURN) * P:(t % TURN) * P + ER], g_onehot[:, t, :], ident[0:ER, 0:ER])
                                m.then_inc(g_turned, 1)
                            pe.wait_ge(g_best_ok, n + (l * NB * NW + 1))
                            for h in range(HEADS):
                                m = pe.transpose(p_rows[0:NBLK, h * P:h * P + ER], g_best[:, h, :], ident[0:ER, 0:ER])
                            m.then_inc(g_best_turned, 1)
                            pe.wait_ge(g_arg, n + (l * NB * NW + 1))
                            pe.wait_ge(g_turned_sb, n * NTURN + (l * NB * NW + 1) * NTURN)
                            for t in range(TG):
                                m = pe.matmul(p_expand[0:ER, t * 8:t * 8 + 8], g_onehotT[:, t, :], g_node[:], start=True, stop=True)
                            m.then_inc(g_spread, 1)
                            pe.wait_ge(g_prod, n + (l * NB * NW + 1))
                            for t in range(TG):
                                m = pe.matmul(p_acc[0][0:NBLK, 0:HW], g_onehot[:, t, :], g_rows[:, t, 0:HW], start=(t == 0), stop=(t == TG - 1))
                            m.then_inc(g_acc, 1)
                        pe.wait_ge(g_feat, b + (l * NB + 1))
                        f = h1 if l == 0 else xn2[0]
                        for t in range(KT):
                            m = pe.transpose(p_xt[:, t * P:t * P + NBLK], f[:, t * P:(t + 1) * P], ident[0:NBLK, 0:NBLK])
                        m.then_inc(g_ft, 1)
                        if l == 0:
                            pe.wait_ge(g_ft_sb, b + 1)
                            for t in range(KT):
                                m = pe.matmul(p_h[0:NBLK, 0:HWX], hT[0][:, t, :], wext[1][:, t, :], start=(t == 0), stop=(t == KT - 1))
                            m.then_inc(g_hh, 1)

            pe.wait_ge(r_mean, 1)
            for t in range(KT):
                m = pe.matmul(p_small[0:1, 0:NX], mean[:, t:t + 1], wr_sb[:, t, :], start=(t == 0), stop=(t == KT - 1))
            m.then_inc(r_logit, 1)
            pe.wait_ge(r_w, 1)
            pe.matmul(p_small[:, 16:16 + TOP_K], ones[:, :], wsel[:, :], start=True, stop=True).then_inc(r_wb, 1)

            pe.wait_ge(r_ready, 1)
            hbank = [p_st[0], p_st[1], p_expand, p_rows]
            obank = [p_acc[0], p_xt, p_h, p_acc[1]]

            def ffn_chunk(g, half, q):
                pe.wait_ge(f_split, g * 2 + 4)
                for n in range(NH):
                    c = g * NH + n
                    if not (isinstance(c, int) and c < 4):
                        pe.wait_ge(f_gelu, c - 3)
                    k, f = n // FT, slice((n % FT) * P, (n % FT + 1) * P)
                    for t in range(KT):
                        for i, (w, v) in enumerate(((w1_hi, x_hi), (w1_hi, x_lo), (w1_lo, x_hi))):
                            m = pe.matmul(hbank[n % 4][:, 0:CHUNK], w[:, k, t, f], v[:, t, :], start=(t == 0 and i == 0), stop=(t == KT - 1 and i == 2))
                    m.then_inc(f_hid, 1)
                for j in range(GRP):
                    if not (isinstance(g, int) and g == 0):
                        pe.wait_ge(f_read, g * GRP + (j + 1 - GRP))
                    cols = slice(j * NBLK, (j + 1) * NBLK)
                    for n in range(NH):
                        if j == 0:
                            pe.wait_ge(f_hi, g * NH + (n + 1))
                        for w in (w2_hi, w2_lo):
                            pe.matmul(obank[j][0:NBLK, 0:D], hid_hi[:, n, cols], w[:, n // FT, n % FT, :], start=(n == 0 and w is w2_hi), stop=False)
                    for n in range(NH):
                        if j == 0:
                            pe.wait_ge(f_lo, g * NH + (n + 1))
                        m = pe.matmul(obank[j][0:NBLK, 0:D], hid_lo[:, n, cols], w2_hi[:, n // FT, n % FT, :], start=False, stop=(n == NH - 1))
                    m.then_inc(f_out, 1)
            ch.steps(NG, 2, 3, ffn_chunk)

        @block.scalar
        def _(act):
            ch = Chain(act, act_s)
            for l in range(2):
                act.wait_ge(s_wT, l + 1)
                if l == 1:
                    act.wait_ge(s_watt, 1)
                nc.scalar.copy(wT.rearrange("p t n -> p (t n)"), p_xt[:, 0:KT * D]).then_inc(s_wTc, 1)
                act.wait_ge(s_watt, l + 1)
                for i in range(KT):
                    m = nc.scalar.copy(wext[l][:, i, D:HWX], p_small[:, (l * KT + i) * 16:(l * KT + i) * 16 + 2 * HEADS])
                    if i == KT - 1:
                        m.then_inc(s_wext, 1)
            act.wait_ge(s_wext, 2)
            xtb, hb = [p_xt, p_rows], [p_h, p_expand]

            def copy_x(c, k):
                act.wait_ge(xt_done, c + 1)
                if not (isinstance(c, int) and c < 2):
                    act.wait_ge(h_done, c - 1)
                nc.scalar.copy(xT[k][:], xtb[k][:, 0:KT * P].rearrange("p (t n) -> p t n", t=KT)[:, :, 0:NBLK]).then_inc(xt_copied, 1)

            def table_group(g, half, q):
                for j in range(GRP):
                    c, k = g * GRP + j, j % 2
                    if not (isinstance(c, int) and c == NB - 1):
                        copy_x(c + 1, 1 - k)
                    act.wait_ge(h_done, c + 1)
                    if j == 0 and not (isinstance(g, int) and g < 2):
                        act.wait_ge(tab_st[q], half * 16)
                    nc.scalar.copy(node[0][:, bass.ds(c, 1), :].rearrange("p b n -> p (b n)"), hb[k][0:NBLK, D:HWX])
                    nc.scalar.copy(hout[q][:, j, :], hb[k][0:NBLK, 0:HWX]).then_inc(h_copied, 1)
            copy_x(0, 0)
            ch.steps(NG, 2, 3, table_group)

            act.wait_ge(s_starts, 1)
            fit = act.value_load(fits_i[0:1, 0:1], min_val=0, max_val=1)
            with act.If(fit > 0):
                for l in range(2):
                    s = L[l]

                    def copy_onehots(b, q, groups, s=s):
                        for gi in groups:
                            act.wait_ge(s["st_done"], b * NGROUPS_ST + gi + 1)
                            if gi == 0 and not (isinstance(b, int) and b == 0):
                                act.wait_ge(s["expand_done"], b)
                            lo, hi = gi * STG, min(T, gi * STG + STG)
                            nc.scalar.copy(onehotT[:, lo:hi, :], p_stb[(gi + q * (NGROUPS_ST % 2)) % 2][0:NBLK, 0:(hi - lo) * P].rearrange("p (t n) -> p t n", n=P)).then_inc(s["st_copied"], 1)

                    def widen(b, q, s=s, l=l):
                        act.wait_ge(s["onehot_done"], (b + 1) * NGROUPS_ST)
                        if not (isinstance(b, int) and b < 2):
                            act.wait_ge(s["main_done"], b - 1)
                        elif l == 1:
                            act.wait_ge(L[0]["main_done"], NB)
                        nc.scalar.copy(onehot_r[q][:], onehot_b[q][:]).then_inc(s["wide_ok"], 1)

                    def relu(b, s=s):
                        act.wait_ge(s["sum_ok"], b + 1)
                        if not (isinstance(b, int) and b == 0):
                            act.wait_ge(s["ft_done"], b)
                        nc.scalar.activation(h1[:], num[:], ACT.Relu).then_inc(s["feat_ok"], 1)

                    def features(b, half, q, s=s, l=l):
                        act.wait_ge(s["ft_done"], b + 1)
                        if l == 1:
                            act.wait_ge(s["stored2"][q], half * 16 + 16)
                        elif not (isinstance(b, int) and b < 2):
                            act.wait_ge(s["hh_done"], b - 1)
                        if l == 0:
                            nc.scalar.copy(hT[q][:], p_xt[:, 0:KT * P].rearrange("p (t n) -> p t n", t=KT)[:, :, 0:NBLK]).then_inc(s["ft_copied"], 1)
                        else:
                            for t in range(KT):
                                m = nc.scalar.activation(hT[q][:, t, :], p_xt[:, t * P:t * P + NBLK], ACT.Copy,
                                                         accum_out=colsum[:, t, bass.ds(b, 1)])
                            m.then_inc(s["ft_copied"], 1)

                    def projected(b, half, q, s=s):
                        act.wait_ge(s["hh_done"], b + 1)
                        act.wait_ge(s["stored"][q], half * 16 + 16)
                        if isinstance(b, int) and b == 0:
                            act.wait_ge(tab_st[0], 16 * ((NG + 1) // 2))
                            act.wait_ge(tab_st[1], 16 * (NG // 2))
                        nc.scalar.copy(node[1][:, bass.ds(b, 1), :].rearrange("p b n -> p (b n)"), p_h[0:NBLK, D:HWX])
                        nc.scalar.copy(hout[q][:, 0, :], p_h[0:NBLK, 0:HWX]).then_inc(s["hh_copied"], 1)

                    def own_exp(b, half, q, s=s):
                        act.wait_ge(s["sarg_ok"], b + 1)
                        ch.link(nc.scalar.activation(self_s[:, 3, :], self_s[:, 2, :], ACT.Exp))
                        act.sem_inc(s["sexp_ok"], 1)
                        act.wait_ge(s["self_ok"][q], half * 16 + 16)
                        for h in range(HEADS):
                            m = nc.scalar.activation(hs[:, h * C:(h + 1) * C], hself[q][:, h * C:(h + 1) * C], ACT.Copy, scale=self_s[:, 3, h:h + 1])
                        m.then_inc(s["hs_ok"], 1)

                    def agg_block(b, half, q, third, r, s=s, l=l):
                        first, last = isinstance(b, int) and b == 0, isinstance(b, int) and b == NB - 1
                        before = (half - 1 + q, 1 - q)
                        if not (isinstance(b, int) and b < 2):
                            (projected if l == 0 else features)(b - 2, half - 1, q)
                        if not last:
                            copy_onehots(b + 1, 1 - q, (0,))
                        if not first:
                            own_exp(b - 1, *before)
                        act.wait_ge(s["logit_ok"], b + 1)
                        nc.scalar.activation(G[r][:, :, D:HW], logit[:], ACT.Exp).then_inc(s["exp_ok"], 1)
                        if not last:
                            copy_onehots(b + 1, 1 - q, range(1, NGROUPS_ST))
                        if l == 0 and not first:
                            relu(b - 1)
                        if not last:
                            widen(b + 1, 1 - q)
                        if l == 0 and not first:
                            features(b - 1, *before)
                    copy_onehots(0, 0, range(NGROUPS_ST))
                    widen(0, 0)
                    ch.steps(NB, 3, 1, agg_block, unroll=6)
                    ends = [(b, b // 2, b % 2) for b in (NB - 2, NB - 1)]
                    own_exp(*ends[1])
                    if l == 0:
                        projected(*ends[0])
                        relu(NB - 1)
                        features(*ends[1])
                        projected(*ends[1])
                    else:
                        features(*ends[0])
                        features(*ends[1])
            with act.Else():
                for l in range(2):
                    with act.Fori(0, NB) as b:
                        with act.Fori(0, NW) as w:
                            n = b * NW + w
                            for i in range(NTURN):
                                act.wait_ge(g_turned, n * NTURN + (l * NB * NW * NTURN + i + 1))
                                t0, t1 = i * TURN, min(TG, (i + 1) * TURN)
                                nc.scalar.copy(g_onehotT_r[:, t0:t1, :], p_st[i % 2][0:NBLK, 0:(t1 - t0) * P].rearrange("p (t n) -> p t n", n=P)[:, :, 0:ER]).then_inc(g_turned_sb, 1)
                            act.wait_ge(g_arg, n + (l * NB * NW + 1))
                            nc.scalar.activation(g_state[:, 4, :], g_state[:, 3, :], ACT.Exp).then_inc(g_scale, 1)
                            act.wait_ge(g_logit, n + (l * NB * NW + 1))
                            nc.scalar.activation(g_rows[:, :, D:HW], g_logit_t, ACT.Exp).then_inc(g_exp, 1)
                        act.wait_ge(g_ft, b + (l * NB + 1))
                        if l == 0:
                            nc.scalar.copy(hT[0][:], p_xt[:, 0:KT * P].rearrange("p (t n) -> p t n", t=KT)[:, :, 0:NBLK]).then_inc(g_ft_sb, 1)
                            act.wait_ge(g_hh, b + 1)
                            nc.scalar.copy(node[1][:, bass.ds(b, 1), :].rearrange("p b n -> p (b n)"), p_h[0:NBLK, D:HWX])
                            nc.scalar.copy(hout[0][:, 0, :], p_h[0:NBLK, 0:HWX]).then_inc(g_out, 1)
                        else:
                            for t in range(KT):
                                m = nc.scalar.activation(hT[0][:, t, :], p_xt[:, t * P:t * P + NBLK], ACT.Copy, accum_out=colsum[:, t, bass.ds(b, 1)])
                            m.then_inc(g_out, 1)

            for arg, done in ((r_arg, r_exp), (r_arg2, r_exp2), (r_arg3, r_exp3)):
                act.wait_ge(arg, 1)
                nc.scalar.activation(rt[:, 4, :], rt[:, 3, :], ACT.Exp).then_inc(done, 1)
            act.wait_ge(r_load, 16 * 4 * TOP_K)
            nc.scalar.copy(w1_hi, eW1).then_inc(f_split, 1)
            hbank = [p_st[0], p_st[1], p_expand, p_rows]

            def high(g, n):
                act.wait_ge(f_gelu, g * NH + (n + 1))
                nc.scalar.copy(hid_hi[:, n, :], gelu_out[:, n % 4, :]).then_inc(f_hi, 1)

            def ffn_chunk(g, half, q):
                for n in range(NH):
                    c = g * NH + n
                    act.wait_ge(f_hid, c + 1)
                    if not (isinstance(c, int) and c < 4):
                        act.wait_ge(f_lo, c - 3)
                    nc.scalar.activation(gelu_out[:, n % 4, :], hbank[n % 4][:, 0:CHUNK], ACT.Gelu,
                                         bias=eb1[:, n // FT, n % FT:n % FT + 1]).then_inc(f_gelu, 1)
                    if n == 0 and not (isinstance(g, int) and g == 0):
                        act.wait_ge(f_out, g * GRP)
                    if n > 0:
                        high(g, n - 1)
                high(g, NH - 1)
                if not (isinstance(g, int) and g == NG - 1):
                    act.wait_ge(f_hid, g * NH + NH)
                    high_x(half + q, 1 - q)

            def high_x(half, q):
                act.wait_ge(f_ok[q], half * 48 + 48)
                nc.scalar.copy(x_hi, fxT[q]).then_inc(f_split, 1)
            act.wait_ge(f_split, 2)
            high_x(0, 0)
            ch.steps(NG, 2, 3, ffn_chunk)

        @block.vector
        def _(dve):
            vec = nc.vector
            ch = Chain(dve, dve_s)
            link = ch.link
            link(vec.memset(sentinel[:, 0:1], -1.0))
            link(vec.memset(sentinel[:, 1:2], -2.0))
            dve.wait_ge(s_dst, 16)
            link(vec.tensor_copy(dst_f, dst_i))
            vec.tensor_copy(samp[:], dst_f.rearrange("p (n k) -> p n k", k=SAMP)[:, :, 0]).then_inc(s_dstf, 1)
            link(vec.memset(ones[:], 1.0))
            link(vec.memset(attm[:].rearrange("p l t h -> p (l t h)"), 0.0))
            dve.wait_ge(s_in, SETUP_LOADS)
            for i in range(4):
                for h in range(HEADS):
                    p0, t = (h % 2) * C, h // 2
                    m = vec.tensor_copy(attm[p0:p0 + C, i // 2, t, (i % 2) * HEADS + h:(i % 2) * HEADS + h + 1], att[p0:p0 + C, i, t:t + 1])
            m.then_inc(s_att, 1)
            dve.wait_ge(s_const, 6)
            link(vec.tensor_copy(ident_b[:], ident[:]))
            dve.wait_ge(s_sampb, 16)
            link(vec.tensor_scalar(samp_lt, samp_b, first_node[:, 0:1], None, ALU.is_lt))
            link(vec.tensor_reduce(st_f[:, 0:1], samp_lt, AX.X, ALU.add))
            link(vec.tensor_scalar(st_f[:, 1:2], st_f[:, 0:1], -1.0, 0.0, ALU.add, ALU.max))
            vec.tensor_copy(st_i[:], st_f[:, 1:2]).then_inc(s_idx, 1)
            dve.wait_ge(s_swin, 16)
            link(vec.tensor_scalar(swin_lt[:], swin[:], first_node[:, 0:1], None, ALU.is_lt))
            link(vec.tensor_reduce(st_f[:, 2:3], swin_lt[:], AX.X, ALU.add))
            link(vec.tensor_scalar(st_f[:, 3:4], st_f[:, 1:2], float(SAMP), st_f[:, 2:3], ALU.mult, ALU.add))
            vec.tensor_scalar(st_f[:, 4:5], st_f[:, 3:4], float(E - CAP), None, ALU.min).then_inc(s_st, 1)
            dve.wait_ge(s_next, 16)
            link(vec.tensor_tensor(falls, dst_f, next_f, ALU.is_gt))
            vec.tensor_reduce(n_falls[:], falls, AX.X, ALU.add).then_inc(s_falls, 1)

            def table_group(g, half, q):
                dve.wait_ge(x_ok[q], half * 16 + 16)
                for j in range(GRP):
                    m = vec.bn_stats(stats[:, j, :], xg[q][:, j, :])
                link(m)
                dve.sem_inc(wait_here, 1)
                for j in range(GRP):
                    m = vec.bn_aggr(mv[:, j, :], stats[:, j, :])
                link(m)
                rsqrt(ch, mv[:, :, 1], GRP, rs, rs_i)
                if not (isinstance(g, int) and g < 2):
                    dve.wait_ge(xt_done, g * GRP - GRP)
                for j in range(GRP):
                    m = vec.tensor_scalar(xng[q][:, j, :], xg[q][:, j, :], mv[:, j, 0:1], rs[:, 0, j:j + 1], ALU.subtract, ALU.mult)
                m.then_inc(x_norm, 1)
            ch.steps(NG, 2, 3, table_group)
            dve.wait_ge(s_stT, 1)
            link(vec.tensor_copy(starts_i[:], p_small[0:1, 128:128 + NB]))
            vec.memset(starts_row[:, NB:NB + 1], float(E))
            vec.tensor_reduce(fits[:, 0:1], p_small[0:1, 384:384 + ER], AX.X, ALU.add)
            link(vec.tensor_copy(starts_row[:, 0:NB], p_small[0:1, 256:256 + NB]))
            link(vec.tensor_tensor(starts_row[:, 0:NB], starts_row[:, 1:NB + 1], starts_row[:, 0:NB], ALU.subtract))
            link(vec.tensor_reduce(fits[:, 1:2], starts_row[:, 0:NB], AX.X, ALU.max))
            link(vec.tensor_scalar(fits[:, 2:3], fits[:, 0:1], 1.0, None, ALU.is_equal))
            link(vec.tensor_scalar(fits[:, 3:4], fits[:, 1:2], float(CAP), None, ALU.is_le))
            vec.tensor_tensor(fits_i[:], fits[:, 2:3], fits[:, 3:4], ALU.mult).then_inc(s_starts, 1)

            for t_, col in ((vF, 0), (vB, T)):
                link(vec.memset(t_[:, :, col], -BIG))
            for q in range(2):
                link(vec.memset(penF[q][:, :, 0], -BIG))
                link(vec.memset(penB[q][:, :, T], -BIG))
            link(vec.memset(carF[:, 0:1], -BIG))
            link(vec.memset(carB[:, P:P + 1], -BIG))
            link(vec.tensor_copy(node_iota_b[:], node_iota[:]))
            dve.wait_ge(s_starts, 1)
            fit = dve.value_load(fits_i[0:1, 0:1], min_val=0, max_val=1)

            def by_head(h):
                return slice(h * C, (h + 1) * C)

            def norm_step(i, q):
                v, y, t = rs[:, 1, 0:1], rs[:, 0, 0:1], rs[:, 2, 0:1]
                if i == 0:
                    link(vec.bn_stats(stats[:, 0, :], x1[q][:]))
                    dve.sem_inc(wait_here, 1)
                    return ch.do(vec.bn_aggr(mv[:, 0, :], stats[:, 0, :]))
                if i == 1:
                    return ch.do(vec.tensor_scalar(v, mv[:, 0, 1:2], LN_EPS, None, ALU.add))
                if i == 2:
                    link(vec.tensor_scalar(rs_i[:, 0, 0:1], v.bitcast(I32), 1, None, ALU.logical_shift_right))
                    return ch.do(vec.tensor_scalar(y.bitcast(I32), rs_i[:, 0, 0:1], -1.0, RSQRT_MAGIC, ALU.mult, ALU.add))
                if i in (3, 5, 7):
                    return ch.do(vec.tensor_scalar(t, y, y, v, ALU.mult, ALU.mult))
                link(vec.tensor_scalar(t, t, -0.5, 1.5, ALU.mult, ALU.add))
                return ch.do(vec.tensor_scalar(y, y, t, None, ALU.mult))

            with dve.If(fit > 0):
                ch = Chain(dve, dve_agg_s)
                link = ch.link
                for l in range(2):
                    s = L[l]
                    if l == 0:
                        dve.wait_ge(h_copied, NB)
                    else:
                        dve.wait_ge(L[0]["hh_copied"], NB)
                        dve.wait_ge(L[0]["expand_done"], NB)

                    link(vec.tensor_copy(node_parts[:, :, 0, :], node[l][:]))
                    link(vec.tensor_tensor(node_rest, node[l][:], node_parts[:, :, 0, :], ALU.subtract))
                    link(vec.tensor_copy(node_parts[:, :, 1, :], node_rest))
                    link(vec.tensor_tensor(node_rest, node_rest, node_parts[:, :, 1, :], ALU.subtract))
                    link(vec.tensor_copy(node_parts[:, :, 2, :], node_rest))

                    def local(b, half, q, s=s):
                        dve.wait_ge(s["dst_ok"][q], half * 16 + 16)
                        return ch.do(vec.tensor_scalar(dloc[:], dst_w[q][:, 1:T + 1], block_base[:, bass.ds(b, 1)], None, ALU.subtract))

                    def onehots(q, t0, t1, s=s):
                        for t in range(t0, t1):
                            m = vec.tensor_scalar(onehot_b[q][:, t, :], node_iota_b[:, :], dloc[:, t:t + 1], None, ALU.is_equal)
                        if t1 % STG == 0 or t1 == T:
                            m.then_inc(s["onehot_done"], 1)

                    def pen_step(i, q):
                        d = dst_w[q]
                        if i == 0:
                            vec.tensor_tensor(link_w[:], d[:, 0:T + 1], d[:, 1:T + 2], ALU.is_equal)
                            vec.tensor_tensor(whole[q][:, 0, :], d[:, 0:1].to_broadcast([P, HEADS]), d[:, T:T + 1].to_broadcast([P, HEADS]), ALU.is_equal)
                            return ch.do(vec.tensor_tensor(whole[q][:, 1, :], d[:, 1:2].to_broadcast([P, HEADS]), d[:, T + 1:T + 2].to_broadcast([P, HEADS]), ALU.is_equal))
                        if i == 1:
                            vec.tensor_scalar(pen[:], link_w[:], -1.0, BIG, ALU.add, ALU.mult)
                            vec.tensor_scalar(run_end[q][:], link_w[:, 1:T + 1], -1.0, 1.0, ALU.mult, ALU.add)
                            return ch.do(vec.tensor_scalar(whole[q][:], whole[q][:], -1.0, BIG, ALU.add, ALU.mult))
                        vec.tensor_copy(penF[q][:, :, 1:T + 1], pen[:, 0:T].unsqueeze(1).to_broadcast([P, HEADS, T]))
                        return ch.do(vec.tensor_copy(penB[q][:, :, 0:T], pen[:, 1:T + 1].unsqueeze(1).to_broadcast([P, HEADS, T])))

                    def nodes(b, q, l=l):
                        vec.tensor_copy(node_q[q][:], node[l][:, bass.ds(b, 1), :].rearrange("p b n -> p (b n)"))
                        vec.tensor_copy(parts_q[q][:], node_parts[:, bass.ds(b, 1), :, :].rearrange("p b k n -> p (b k) n"))

                    def own_step(i, b, q, s=s):
                        own, top, arg = (self_s[:, k, :] for k in (0, 1, 2))
                        acc = p_acc[q][0:NBLK, :]
                        if i == 0:
                            dve.wait_ge(s["main_done"], b + 1)
                            vec.tensor_scalar(self_s[:, 5, 0:1], acc[:, GW - 1:GW], -1.0, BIG, ALU.add, ALU.mult)
                            return ch.do(vec.tensor_tensor(own, node_q[q][:, 0:HEADS], node_q[q][:, HEADS:2 * HEADS], ALU.add))
                        if i == 1:
                            vec.tensor_scalar(top, acc[:, HW:HW + HEADS], self_s[:, 5, 0:1], None, ALU.add)
                            return ch.do(vec.scalar_tensor_tensor(own, own, SLOPE, own, ALU.mult, ALU.max))
                        if i == 2:
                            return ch.do(vec.tensor_tensor(top, top, own, ALU.max))
                        vec.tensor_tensor(arg, own, top, ALU.subtract).then_inc(s["sarg_ok"], 1)

                    def quotient(b, half, q, s=s, l=l):
                        acc = p_acc[q][0:NBLK, :]
                        es, den = self_s[:, 3, :], self_s[:, 4, :]
                        dve.wait_ge(s["sexp_ok"], b + 1)
                        c = ch.do(vec.tensor_tensor(den, acc[:, D:HW], es, ALU.add))
                        if l == 0 and not (isinstance(b, int) and b == 0):
                            dve.wait_ge(s["feat_ok"], b)
                        ch.after(c)
                        c = ch.do(vec.tensor_scalar(den, den, 1e-16, None, ALU.max))
                        dve.wait_ge(s["hs_ok"], b + 1)
                        c1 = ch.do(vec.tensor_tensor(num[:], hs[:], acc[:, 0:D], ALU.add))
                        ch.after(c)
                        c = ch.do(vec.reciprocal(den, den))
                        if l == 1:
                            dve.wait_ge(s["xres_ok"][q], half * 16 + 16)
                            c2 = ch.do(vec.tensor_tensor(xres[q][:], xres[q][:], bias[1][:], ALU.add))
                            if not (isinstance(b, int) and b < 2):
                                dve.wait_ge(s["stored"][q], half * 32 + 16)
                                dve.wait_ge(s["ft_done"], b - 1)
                            ch.after(c2)
                        ch.after(c1)
                        dve.sem_inc(s["acc_read"], 1)
                        ch.after(c)
                        more, res = (bias[0], num) if l == 0 else (xres[q], x1[q])
                        for h in range(HEADS):
                            hc = slice(h * C, (h + 1) * C)
                            m = vec.scalar_tensor_tensor(res[:, hc], num[:, hc], self_s[:, 4, h:h + 1], more[:, hc], ALU.mult, ALU.add)
                        if l == 0:
                            m.then_inc(s["sum_ok"], 1)
                        else:
                            link(m)
                        dve.sem_inc(s["epi_done"], 1)

                    def norm_apply(b, q, s=s):
                        vec.tensor_scalar(xn2[q][:], x1[q][:], mv[:, 0, 0:1], rs[:, 0, 0:1], ALU.subtract, ALU.mult).then_inc(s["feat_ok"], 1)

                    def agg_block(b, half, q, third, r, s=s, l=l):
                        g = G[r]
                        p = 1 - q
                        later = not (isinstance(b, int) and b == 0)
                        more = not (isinstance(b, int) and b == NB - 1)

                        def flat(a):
                            return a[:].rearrange("p h t -> p (h t)")

                        def scans():
                            vec.tensor_tensor_scan(flat(rF), flat(penF[q]), flat(vF), -BIG, ALU.add, ALU.max)
                            return ch.do(vec.tensor_tensor_scan(flat(rB)[:, ::-1], flat(penB[q])[:, ::-1], flat(vB)[:, ::-1], -BIG, ALU.add, ALU.max))
                        dve.wait_ge(s["gathered"][r], (third + 1) * (16 * T))
                        a_src = g[:, :, D:HW].rearrange("p t h -> p h t")
                        vec.tensor_copy(vF[:, :, 1:T + 1], a_src)
                        c = ch.do(vec.tensor_copy(vB[:, :, 0:T], a_src))
                        if more:
                            c_next = local(b + 1, half + q, p)
                            c_pen = pen_step(0, p)
                        ch.after(c)
                        c = scans()
                        if more:
                            if later:
                                dve.wait_ge(s["wide_ok"], b)
                                dve.wait_ge(s["st_done"], b * NGROUPS_ST)
                            ch.after(c_next)
                            onehots(p, 0, 1)
                        ch.after(c)
                        dve.sem_inc(s["ends_ok"], 1)
                        if more:
                            ch.after(c_pen)
                            c_pen = pen_step(1, p)
                            onehots(p, 1, 4)
                        dve.wait_ge(s["rows_done"], b + 1)
                        rows = p_rows[0:HEADS, :].rearrange("h (i p) -> h i p", p=P)
                        c = ch.do(vec.tensor_copy(row_pen[:], rows[:, 1::2, :]))
                        if more:
                            onehots(p, 4, 5)
                        ch.after(c)
                        vec.tensor_tensor_scan(carF[:, 1:P + 1], row_pen[:, 0, :], rows[:, 0, :], -BIG, ALU.add, ALU.max)
                        c = ch.do(vec.tensor_tensor_scan(carB[:, 0:P][:, ::-1], row_pen[:, 1, :][:, ::-1], rows[:, 2, :][:, ::-1], -BIG, ALU.add, ALU.max))
                        if more:
                            onehots(p, 5, 6)
                        ch.after(c)
                        dve.sem_inc(s["carry_ok"], 1)
                        dve.wait_ge(s["expand_done"], b + 1)
                        spread = p_expand[:, 0:T * 8].rearrange("p (t n) -> p t n", n=8)
                        a_self, a_dst = spread[:, :, 0:HEADS], spread[:, :, HEADS:2 * HEADS]
                        ca = ch.do(vec.tensor_tensor(alpha[:], g[:, :, D:HW], a_dst, ALU.add))
                        if later:
                            co = own_step(0, b - 1, p)
                        if more:
                            ch.after(c_pen)
                            pen_step(2, p)
                        ch.after(ca)
                        ca = ch.do(vec.scalar_tensor_tensor(alpha[:], alpha[:], SLOPE, alpha[:], ALU.mult, ALU.max))
                        if later:
                            ch.after(co)
                            co = own_step(1, b - 1, p)
                        dve.wait_ge(s["back_done"], b + 1)
                        vec.tensor_copy(vF[:, :, 0], p_back[:, 0:HEADS])
                        c = ch.do(vec.tensor_copy(vB[:, :, T], p_back[:, HEADS:2 * HEADS]))
                        if later:
                            ch.after(co)
                            co = own_step(2, b - 1, p)
                        if more:
                            onehots(p, 6, 7)
                        ch.after(c)
                        c = scans()
                        if later:
                            ch.after(co)
                            own_step(3, b - 1, p)
                        if more:
                            nodes(b + 1, p)
                            onehots(p, 7, 8)
                        ch.after(c)
                        vec.memset(vF[:, :, 0], -BIG)
                        vec.memset(vB[:, :, T], -BIG)
                        c = ch.do(vec.tensor_tensor(runmax[:], rF[:, :, 1:T + 1].rearrange("p h t -> p t h"), rB[:, :, 0:T].rearrange("p h t -> p t h"), ALU.max))
                        if more:
                            onehots(p, 8, 10)
                        ch.after(c)
                        c = ch.do(vec.tensor_tensor(runmax[:], runmax[:], a_self, ALU.max))
                        if more:
                            onehots(p, 10, 12)
                        ch.after(c)
                        c = ch.do(vec.tensor_tensor(runmax[:], runmax[:], a_dst, ALU.add))
                        if more:
                            onehots(p, 12, 14)
                        ch.after(c)
                        c = ch.do(vec.scalar_tensor_tensor(runmax[:], runmax[:], SLOPE, runmax[:], ALU.mult, ALU.max))
                        if more:
                            onehots(p, 14, 16)
                        ch.after(ca)
                        ch.after(c)
                        c = ch.do(vec.tensor_tensor(alpha[:], alpha[:], runmax[:], ALU.subtract))
                        if more:
                            onehots(p, 16, 18)
                        ch.after(c)
                        vec.tensor_scalar(logit[:], alpha[:], 0.0, None, ALU.min).then_inc(s["logit_ok"], 1)
                        vec.tensor_tensor(g[:, :, HW:HW + HEADS], runmax[:], run_end[q][:].unsqueeze(2).to_broadcast([P, T, HEADS]), ALU.mult)
                        vec.tensor_copy(g[:, :, HW + HEADS], run_end[q][:])
                        if later:
                            quotient(b - 1, half - 1 + q, p)
                        dve.wait_ge(s["exp_ok"], b + 1)
                        count = 0
                        for i in range(9):
                            t0, t1 = i * 2, i * 2 + 2
                            hv = g[:, t0:t1, 0:D].rearrange("p t (h c) -> p t h c", h=HEADS)
                            vec.tensor_tensor(hv, hv, g[:, t0:t1, D:HW].unsqueeze(3).to_broadcast([P, 2, HEADS, C]), ALU.mult).then_inc(s["prod_ok"], 1)
                            if l == 1 and later:
                                if count:
                                    ch.after(count)
                                count = norm_step(i, p)
                        if l == 1 and later:
                            ch.after(count)
                            norm_apply(b - 1, p)
                        if more:
                            dve.sem_inc(s["onehot_ok"], 1)

                    c = local(0, 0, 0)
                    ch.after(c)
                    if l == 1:
                        dve.wait_ge(L[0]["wide_ok"], NB)
                    nodes(0, 0)
                    for t0 in range(0, T, STG):
                        onehots(0, t0, min(T, t0 + STG))
                    for i in range(3):
                        ch.after(pen_step(i, 0))
                    dve.sem_inc(s["onehot_ok"], 1)
                    ch.steps(NB, 3, 1, agg_block, unroll=6)
                    last_q = (NB - 1) % 2
                    for i in range(4):
                        c = own_step(i, NB - 1, last_q)
                        if i < 3:
                            ch.after(c)
                    quotient(NB - 1, (NB - 1) // 2, last_q)
                    if l == 1:
                        for i in range(9):
                            ch.after(norm_step(i, (NB - 1) % 2))
                        norm_apply(NB - 1, (NB - 1) % 2)
                dve.wait_ge(L[1]["ft_copied"], NB)
            with dve.Else():
                ch = Chain(dve, dve_general_s)
                link = ch.link
                top, new, a_dst_n, arg, shrink, den = (g_state[:, i, :] for i in range(6))
                BEFORE, WINDOW, AFTER = 8, TG + 15, (4, 18)
                dve.sem_inc(g_window, 1)
                for l in range(2):
                    block_links = BEFORE + NW * WINDOW + AFTER[l]
                    start = l * NB * (BEFORE + NW * WINDOW + AFTER[0])
                    with dve.Fori(0, NB) as b:
                        ch.base, ch.n = b * block_links + start, 0
                        dve.wait_ge(g_own0 if l == 0 else g_own1, b * (16 * (l + 1)) + 16 * (l + 1))
                        nb = node[l][:, bass.ds(b, 1), :].rearrange("p b n -> p (b n)")
                        c_top = ch.do(vec.tensor_copy(top, nb[:, 0:HEADS]))
                        c = ch.do(vec.tensor_copy(g_node[:, 0:HEADS], nb[:, HEADS:2 * HEADS]))
                        link(vec.tensor_copy(a_dst_n, nb[:, HEADS:2 * HEADS]))
                        link(vec.memset(den, 1.0))
                        link(vec.tensor_copy(g_sum[:], hself[0][:, 0:D]))
                        link(vec.tensor_tensor(new, top, a_dst_n, ALU.add))
                        link(vec.scalar_tensor_tensor(new, new, SLOPE, new, ALU.mult, ALU.max))
                        link(vec.tensor_copy(g_node[:, HEADS:2 * HEADS], new))
                        assert ch.n == BEFORE, ch.n
                        dve.sem_inc(wait_here, 1)
                        with dve.Fori(0, NW) as w:
                            n = b * NW + w
                            ch.base, ch.n = b * block_links + w * WINDOW + (start + BEFORE), 0
                            dve.wait_ge(g_edges, n * 32 + (l * NB * NW * 32 + 32))
                            link(vec.tensor_scalar(g_dloc, g_dst, block_base[0:ER, bass.ds(b, 1)], None, ALU.subtract))
                            for t in range(TG):
                                m = vec.tensor_scalar(g_onehot_r[:, t, :], node_iota[0:ER, :], g_dloc[:, t:t + 1], None, ALU.is_equal)
                            link(m)
                            dve.sem_inc(g_onehot_ok, 1)
                            link(vec.tensor_scalar(g_other, g_onehot, -1.0, BIG, ALU.add, ALU.mult))
                            dve.wait_ge(g_gathered, n * (16 * TG) + (l * NB * NW + 1) * (16 * TG))
                            for t in range(TG):
                                for h in range(HEADS):
                                    a = g_rows[:, t, D + h:D + h + 1]
                                    if t == 0:
                                        m = vec.tensor_scalar(g_best[:, h, :], g_other[:, t, :], a, None, ALU.add)
                                    else:
                                        m = vec.scalar_tensor_tensor(g_best[:, h, :], g_other[:, t, :], a, g_best[:, h, :], ALU.add, ALU.max)
                                link(m)
                            dve.sem_inc(g_best_ok, 1)
                            dve.wait_ge(g_best_turned, n + (l * NB * NW + 1))
                            turned = p_rows[0:NBLK, :].rearrange("p (h n) -> p h n", n=P)[:, :, 0:ER]
                            link(vec.tensor_reduce(new, turned, AX.X, ALU.max))
                            link(vec.tensor_tensor(top, top, new, ALU.max))
                            link(vec.tensor_tensor(new, top, a_dst_n, ALU.add))
                            link(vec.scalar_tensor_tensor(new, new, SLOPE, new, ALU.mult, ALU.max))
                            link(vec.tensor_tensor(arg, g_node[:, HEADS:2 * HEADS], new, ALU.subtract))
                            link(vec.tensor_copy(g_node[:, HEADS:2 * HEADS], new))
                            dve.sem_inc(g_arg, 1)
                            dve.wait_ge(g_spread, n + (l * NB * NW + 1))
                            spread = p_expand[0:ER, 0:TG * 8].rearrange("p (t n) -> p t n", n=8)
                            link(vec.tensor_tensor(g_alpha, g_rows[:, :, D:HW], spread[:, :, 0:HEADS], ALU.add))
                            link(vec.scalar_tensor_tensor(g_alpha, g_alpha, SLOPE, g_alpha, ALU.mult, ALU.max))
                            link(vec.tensor_tensor(g_alpha, g_alpha, spread[:, :, HEADS:2 * HEADS], ALU.subtract))
                            vec.tensor_scalar(g_logit_t, g_alpha, 0.0, None, ALU.min).then_inc(g_logit, 1)
                            dve.wait_ge(g_exp, n + (l * NB * NW + 1))
                            hv = g_rows[:, :, 0:D].rearrange("p t (h c) -> p t h c", h=HEADS)
                            for t in range(TG):
                                m = vec.tensor_tensor(hv[:, t], hv[:, t], g_rows[:, t, D:HW].unsqueeze(2).to_broadcast([ER, HEADS, C]), ALU.mult)
                            m.then_inc(g_prod, 1)
                            dve.wait_ge(g_scale, n + (l * NB * NW + 1))
                            dve.wait_ge(g_acc, n + (l * NB * NW + 1))
                            acc = p_acc[0][0:NBLK, :]
                            link(vec.tensor_tensor(den, den, shrink, ALU.mult))
                            link(vec.tensor_tensor(den, den, acc[:, D:HW], ALU.add))
                            for h in range(HEADS):
                                m = vec.scalar_tensor_tensor(g_sum[:, by_head(h)], g_sum[:, by_head(h)], shrink[:, h:h + 1], acc[:, by_head(h)], ALU.mult, ALU.add)
                            link(m)
                            assert ch.n == WINDOW, (ch.n, WINDOW)
                            dve.sem_inc(g_window, 1)
                        ch.base, ch.n = b * block_links + (start + BEFORE + NW * WINDOW), 0
                        link(vec.tensor_scalar(den, den, 1e-16, None, ALU.max))
                        link(vec.reciprocal(den, den))
                        if l == 0:
                            for h in range(HEADS):
                                m = vec.scalar_tensor_tensor(g_sum[:, by_head(h)], g_sum[:, by_head(h)], den[:, h:h + 1], bias[0][:, by_head(h)], ALU.mult, ALU.add)
                            link(m)
                            link(vec.tensor_scalar(h1[:], g_sum[:], 0.0, None, ALU.max))
                            dve.sem_inc(g_feat, 1)
                        else:
                            link(vec.tensor_tensor(xres[0][:], xres[0][:], bias[1][:], ALU.add))
                            for h in range(HEADS):
                                m = vec.scalar_tensor_tensor(x1[0][:, by_head(h)], g_sum[:, by_head(h)], den[:, h:h + 1], xres[0][:, by_head(h)], ALU.mult, ALU.add)
                            link(m)
                            for i in range(9):
                                ch.after(norm_step(i, 0))
                            vec.tensor_scalar(xn2[0][:], x1[0][:], mv[:, 0, 0:1], rs[:, 0, 0:1], ALU.subtract, ALU.mult).then_inc(g_feat, 1)
                        assert ch.n == AFTER[l], (l, ch.n)
                dve.wait_ge(g_out, 2 * NB)


            ch = Chain(dve, dve_ffn_s)
            link = ch.link
            link(vec.tensor_reduce(mean[:], colsum[:], AX.X, ALU.add))
            vec.tensor_scalar(mean[:], mean[:], 1.0 / N, None, ALU.mult).then_inc(r_mean, 1)
            dve.wait_ge(r_logit, 1)
            R = lambda i: rt[:, i, :]
            S = lambda i, k: rt[:, i, k:k + 1]
            link(vec.tensor_tensor(R(2), p_small[0:1, 0:NX], R(0), ALU.add))

            def softmax(dst_i_, src_i_, arg, done):
                link(vec.tensor_reduce(S(5, 0), R(src_i_), AX.X, ALU.max))
                vec.tensor_scalar(R(3), R(src_i_), S(5, 0), None, ALU.subtract).then_inc(arg, 1)
                dve.wait_ge(done, 1)
                link(vec.tensor_reduce(S(5, 1), R(4), AX.X, ALU.add))
                link(vec.reciprocal(S(5, 2), S(5, 1)))
                link(vec.tensor_scalar(R(dst_i_), R(4), S(5, 2), None, ALU.mult))
            softmax(6, 2, r_arg, r_exp)
            link(vec.tensor_scalar(R(7), R(6), float(N), None, ALU.mult))
            link(vec.tensor_scalar(R(8), R(7), capacity, None, ALU.is_gt))
            link(vec.tensor_scalar(R(9), R(7), capacity, None, ALU.max))
            link(vec.reciprocal(R(9), R(9)))
            link(vec.tensor_scalar(R(9), R(9), capacity, -1.0, ALU.mult, ALU.add))
            link(vec.tensor_tensor(R(9), R(9), R(8), ALU.mult))
            link(vec.tensor_scalar(R(9), R(9), 1.0, None, ALU.add))
            link(vec.tensor_tensor(R(10), R(6), R(9), ALU.mult))
            softmax(6, 10, r_arg2, r_exp2)
            link(vec.memset(R(15), -BIG))
            for k in range(TOP_K):
                link(vec.tensor_reduce(S(15, k), R(6), AX.X, ALU.max))
                link(vec.tensor_scalar(R(11), R(6), S(15, k), None, ALU.not_equal))
                link(vec.scalar_tensor_tensor(R(12), R(11), 1024.0, R(1), ALU.mult, ALU.add))
                link(vec.tensor_reduce(S(13, k), R(12), AX.X, ALU.min))
                link(vec.tensor_scalar(R(14), R(1), S(13, k), None, ALU.is_equal))
                link(vec.scalar_tensor_tensor(R(6), R(14), -1024.0, R(6), ALU.mult, ALU.add))
            vec.tensor_copy(sel_i[:], rt[:, 13, 0:TOP_K]).then_inc(r_sel, 1)
            softmax(6, 15, r_arg3, r_exp3)
            vec.tensor_copy(wsel[:], rt[:, 6, 0:TOP_K]).then_inc(r_w, 1)
            dve.wait_ge(r_wb, 1)
            link(vec.tensor_copy(wsel_b[:], p_small[:, 16:16 + TOP_K]))
            dve.wait_ge(r_load, 16 * 4 * TOP_K)
            for k in range(TOP_K):
                w = eW2[:, k, :, :].rearrange("p t n -> p (t n)")
                link(vec.tensor_scalar(w, w, wsel_b[:, k:k + 1], None, ALU.mult))
            link(vec.tensor_copy(w2_hi, eW2))
            vec.tensor_tensor(w2_lo, eW2, w2_hi, ALU.subtract).then_inc(r_ready, 1)
            link(vec.tensor_scalar(eb2s[:], eb2[:, 0, :], wsel_b[0:NBLK, 0:1], None, ALU.mult))
            link(vec.scalar_tensor_tensor(eb2s[:], eb2[:, 1, :], wsel_b[0:NBLK, 1:2], eb2s[:], ALU.mult, ALU.add))
            obank = [p_acc[0], p_xt, p_h, p_acc[1]]

            def ffn_chunk(g, half, q):
                dve.wait_ge(f_ok[q], half * 48 + 48)
                if not (isinstance(g, int) and g < 2):
                    dve.wait_ge(f_st[q], half * 16)
                y = xg[q]
                wide = [NBLK, GRP, D]
                link(vec.tensor_tensor(y[:], xng[q], eb2s[:].unsqueeze(1).to_broadcast(wide), ALU.add))
                for j in range(GRP):
                    dve.wait_ge(f_out, g * GRP + (j + 1))
                    link(vec.tensor_tensor(y[:, j, :], obank[j][0:NBLK, 0:D], y[:, j, :], ALU.add))
                    dve.sem_inc(f_read, 1)
                    link(vec.bn_stats(stats[:, j, :], y[:, j, :]))
                    dve.sem_inc(wait_here, 1)
                    link(vec.bn_aggr(mv[:, j, :], stats[:, j, :]))
                rsqrt(ch, mv[:, :, 1], GRP, rs, rs_i)
                for j in range(GRP):
                    m = vec.tensor_scalar(y[:, j, :], y[:, j, :], mv[:, j, 0:1], rs[:, 0, j:j + 1], ALU.subtract, ALU.mult)
                link(m)
                link(vec.tensor_tensor(y[:], y[:], gamma_b[:].unsqueeze(1).to_broadcast(wide), ALU.mult))
                link(vec.tensor_tensor(y[:], y[:], beta_b[:].unsqueeze(1).to_broadcast(wide), ALU.add))
                vec.tensor_tensor(y[:], y[:], fx1[q][:], ALU.add).then_inc(f_done, 1)
            ch.steps(NG, 2, 3, ffn_chunk)


_INS = ["x", "src", "dst", "L0_gnn_W1", "L0_gnn_att_src1", "L0_gnn_att_dst1", "L0_gnn_b1", "L0_gnn_W2", "L0_gnn_att_src2",
        "L0_gnn_att_dst2", "L0_gnn_b2", "L0_ffn_Wr", "L0_ffn_br", "L0_ffn_W1", "L0_ffn_b1", "L0_ffn_W2", "L0_ffn_b2",
        "L0_ffn_gamma", "L0_ffn_beta"]


def kernel(**inputs):
    import numpy as np
    import concourse.bacc as bacc
    from concourse.bass_utils import run_bass_kernel_spmd

    nc = bacc.Bacc("TRN2", target_bir_lowering=False, num_devices=1)
    arrays, args = {}, []
    for name in _INS:
        a = np.ascontiguousarray(inputs[name])
        arrays[f"in_{name}"] = a
        args.append(nc.dram_tensor(f"in_{name}", a.shape, mybir.dt.from_np(a.dtype), kind="ExternalInput").ap())
    args.append(nc.dram_tensor("out_x", arrays["in_x"].shape, F32, kind="ExternalOutput").ap())
    build(nc, *args)
    r = run_bass_kernel_spmd(nc, [arrays], core_ids=[0])
    return r.results[0]["out_x"]
```
